# Optimizing a Trainium2 kernel written in Bass

```python
import numpy as np
import jax
import jax.numpy as jnp

def _softmax(x, axis=-1):
    return jax.nn.softmax(x, axis=axis)

def _gelu(x):
    return jax.nn.gelu(x, approximate=True)

def _silu(x):
    return jax.nn.silu(x)

def _sigmoid(x):
    return jax.nn.sigmoid(x)

def _layernorm(x, axis=-1, eps=1e-05):
    m = jnp.mean(x, axis=axis, keepdims=True)
    v = jnp.var(x, axis=axis, keepdims=True)
    return (x - m) / jnp.sqrt(v + eps)

def _scatter_add(tgt, idx, src, axis=0):
    return tgt.at[idx].add(src)

def _segment_sum(src, seg, n):
    return jax.ops.segment_sum(src, seg, n)
kernel_name = 'mk_perceiver_d2_seqx_r4_9baca3'

def setup_inputs(seed: int=0):
    np.random.seed(seed)
    _w = jnp.asarray

    def _rec_inputs():
        import jax
        import jax.numpy as jnp
        _rk = jax.random.key(seed)
        x = -0.0002928 + 1 * jax.random.normal(jax.random.fold_in(_rk, 1), (1, 128, 256), jnp.float32)
        _lenS = 128 - jax.random.randint(jax.random.fold_in(_rk, 7), (1,), 0, max(1, 128 // 4) + 1, jnp.int32)
        _lenS2 = 12544 - jax.random.randint(jax.random.fold_in(_rk, 8), (1,), 0, max(1, 12544 // 4) + 1, jnp.int32)
        _ctx_1024P = jax.random.normal(jax.random.fold_in(_rk, 11), (1, 16, 256), jnp.float32)
        _ctx_1024c = jax.random.dirichlet(jax.random.fold_in(_rk, 511), 0.3 * jnp.ones((16,), jnp.float32), (1, 12544))
        _ctx_1024t = jnp.einsum('bsk,bkd->bsd', _ctx_1024c, _ctx_1024P)
        _ctx_1024t = _ctx_1024t * jax.lax.rsqrt(jnp.mean(jnp.square(_ctx_1024t)) + 1e-12) * 0.953939
        ctx_1024 = -1.39393e-06 + 0.999914 * (_ctx_1024t + 0.3 * jax.random.normal(jax.random.fold_in(_rk, 611), (1, 12544, 256), jnp.float32))
        _validS = jnp.arange(128)[None, :] < _lenS[:, None]
        _validS2 = jnp.arange(12544)[None, :] < _lenS2[:, None]
        _causal = jnp.tril(jnp.ones((128, 128), dtype=bool))
        mask_BxSxS2_bf1 = jnp.ones((1, 128, 12544), dtype=bool)
        return (x, ctx_1024, mask_BxSxS2_bf1)
    x, ctx_1024, mask_BxSxS2_bf1 = _rec_inputs()

    def _L0_xattn_setup():
        import jax, jax.numpy as jnp
        import numpy as np
        DIM = 256
        HEAD_DIM = 64
        NUM_HEADS = DIM // HEAD_DIM
        SCALE = HEAD_DIM ** (-0.5)
        key = jax.random.key(seed)
        k_x, k_ctx, k_wq, k_wkv, k_wo = jax.random.split(key, 5)
        B, N, M = (2, 512, 512)
        x = jax.random.normal(k_x, (B, N, DIM), dtype=jnp.float32)
        context = jax.random.normal(k_ctx, (B, M, DIM), dtype=jnp.float32)
        mask = jnp.ones((B, N, M), dtype=bool)
        s = DIM ** (-0.5)
        Wq = jax.random.normal(k_wq, (DIM, DIM), dtype=jnp.float32) * s
        Wkv = jax.random.normal(k_wkv, (DIM, 2 * DIM), dtype=jnp.float32) * s
        Wo = jax.random.normal(k_wo, (DIM, DIM), dtype=jnp.float32) * s
        return {'x': x, 'context': context, 'mask': mask, 'Wq': Wq, 'Wkv': Wkv, 'Wo': Wo}
    _L0_xattn_all = _L0_xattn_setup()
    _L0_xattn_in = {k: v for k, v in _L0_xattn_all.items() if k in ('Wq', 'Wkv', 'Wo')}
    del _L0_xattn_all

    def _L0_attn_setup():
        import jax, jax.numpy as jnp
        import numpy as np
        import math
        B, L, HID = (2, 1024, 256)
        NH, DK, DV = (12, 64, 128)
        KD, VD, CS = (NH * DK, NH * DV, 4)
        SCALE = DK ** (-0.5)

        def _causal_depthwise_conv(x, w):
            c, k = w.shape
            xt = jnp.transpose(x, (0, 2, 1))
            out = jax.lax.conv_general_dilated(xt, w[:, None, :], window_strides=(1,), padding=[(k - 1, 0)], feature_group_count=c, dimension_numbers=('NCH', 'OIH', 'NCH'))
            return jnp.transpose(out, (0, 2, 1))

        def _l2norm(x, eps=1e-06):
            return x * jax.lax.rsqrt(jnp.sum(x * x, axis=-1, keepdims=True) + eps)

        def _gated_delta_net(hidden_states, Wq, Wk, Wv, Wg, Wo, conv_q, conv_k, conv_v, Wgk, Wb, b_b, A_log, dt_bias, g_norm_weight):
            b, l, _ = hidden_states.shape
            q = jax.nn.silu(_causal_depthwise_conv(hidden_states @ Wq, conv_q))
            k = jax.nn.silu(_causal_depthwise_conv(hidden_states @ Wk, conv_k))
            v = jax.nn.silu(_causal_depthwise_conv(hidden_states @ Wv, conv_v))
            gk = -jnp.exp(A_log) * jax.nn.softplus(hidden_states @ Wgk + dt_bias)
            beta = jax.nn.sigmoid(hidden_states @ Wb + b_b)
            q = jnp.transpose(q.reshape(b, l, NH, DK), (0, 2, 1, 3))
            k = jnp.transpose(k.reshape(b, l, NH, DK), (0, 2, 1, 3))
            v = jnp.transpose(v.reshape(b, l, NH, DV), (0, 2, 1, 3))
            q = _l2norm(q) * SCALE
            k = _l2norm(k)
            qs = jnp.moveaxis(q, 2, 0)
            ks_ = jnp.moveaxis(k, 2, 0)
            vs = jnp.moveaxis(v, 2, 0)
            bs = jnp.moveaxis(beta, 1, 0)
            gs = jnp.moveaxis(gk, 1, 0)

            def step(S, inp):
                qt, kt, vt, bt, gt = inp
                S = S * jnp.exp(gt)[..., None, None]
                kv = jnp.einsum('bhk,bhkv->bhv', kt, S)
                delta = (vt - kv) * bt[..., None]
                S = S + jnp.einsum('bhk,bhv->bhkv', kt, delta)
                ot = jnp.einsum('bhk,bhkv->bhv', qt, S)
                return (S, ot)
            S0 = jnp.zeros((b, NH, DK, DV), hidden_states.dtype)
            _, os_ = jax.lax.scan(step, S0, (qs, ks_, vs, bs, gs))
            o = jnp.moveaxis(os_, 0, 1)
            g = (hidden_states @ Wg).reshape(b, l, NH, DV)
            var = jnp.mean(o * o, axis=-1, keepdims=True)
            o = o * jax.lax.rsqrt(var + 1e-05) * g_norm_weight
            o = o * g * jax.nn.sigmoid(g)
            return o.reshape(b, l, VD) @ Wo
        key = jax.random.key(seed)
        ks = jax.random.split(key, 16)
        rn = lambda i, shape, s: jax.random.normal(ks[i], shape, jnp.float32) * s
        hidden_states = rn(0, (B, L, HID), 1.0)
        Wq = rn(1, (HID, KD), HID ** (-0.5))
        Wk = rn(2, (HID, KD), HID ** (-0.5))
        Wv = rn(3, (HID, VD), HID ** (-0.5))
        Wg = rn(4, (HID, VD), HID ** (-0.5))
        Wo = rn(5, (VD, HID), VD ** (-0.5))
        conv_q = rn(6, (KD, CS), 0.5)
        conv_k = rn(7, (KD, CS), 0.5)
        conv_v = rn(8, (VD, CS), 0.5)
        Wgk = rn(9, (HID, NH), HID ** (-0.5))
        Wb = rn(10, (HID, NH), HID ** (-0.5))
        b_b = rn(11, (NH,), 0.1)
        A = jax.random.uniform(ks[12], (NH,), jnp.float32, 0.5, 16.0)
        A_log = jnp.log(A)
        dt = jnp.exp(jax.random.uniform(ks[13], (NH,), jnp.float32) * (math.log(0.1) - math.log(0.001)) + math.log(0.001))
        dt = jnp.clip(dt, 0.0001, None)
        dt_bias = dt + jnp.log(-jnp.expm1(-dt))
        g_norm_weight = jnp.ones((DV,), jnp.float32)
        return dict(hidden_states=hidden_states, Wq=Wq, Wk=Wk, Wv=Wv, Wg=Wg, Wo=Wo, conv_q=conv_q, conv_k=conv_k, conv_v=conv_v, Wgk=Wgk, Wb=Wb, b_b=b_b, A_log=A_log, dt_bias=dt_bias, g_norm_weight=g_norm_weight)
    _L0_attn_all = _L0_attn_setup()
    _L0_attn_in = {k: v for k, v in _L0_attn_all.items() if k in ('Wq', 'Wk', 'Wv', 'Wg', 'Wo', 'conv_q', 'conv_k', 'conv_v', 'Wgk', 'Wb', 'b_b', 'A_log', 'dt_bias', 'g_norm_weight')}
    del _L0_attn_all

    def _L0_ffn_setup():
        import jax, jax.numpy as jnp
        import numpy as np
        B, S, D, E = (2, 512, 256, 8)
        key = jax.random.key(seed)
        ks = jax.random.split(key, 5)
        x = jax.random.normal(ks[0], (B, S, D), dtype=jnp.float32)
        router_w = jax.random.normal(ks[1], (E, D), dtype=jnp.float32) * 0.02
        router_b = jnp.zeros((E,), dtype=jnp.float32)
        expert_w = jax.random.normal(ks[2], (E, D, D), dtype=jnp.float32) * 0.02
        expert_b = jnp.zeros((E, D), dtype=jnp.float32)
        return {'x': x, 'router_w': router_w, 'router_b': router_b, 'expert_w': expert_w, 'expert_b': expert_b}
    _L0_ffn_all = _L0_ffn_setup()
    _L0_ffn_in = {k: v for k, v in _L0_ffn_all.items() if k in ('router_w', 'router_b', 'expert_w', 'expert_b')}
    del _L0_ffn_all

    def _L1_xattn_setup():
        import jax, jax.numpy as jnp
        import numpy as np
        N_HEADS = 16
        EMBED_DIM = 256
        HEAD_DIM = EMBED_DIM // N_HEADS
        B, T_TGT, T_SRC = (2, 512, 512)
        key = jax.random.key(seed)
        ks = jax.random.split(key, 8)
        s = 1.0 / np.sqrt(EMBED_DIM)
        return {'x_1': jax.random.normal(ks[0], (B, T_TGT, EMBED_DIM), dtype=jnp.float32), 'x_2': jax.random.normal(ks[1], (B, T_SRC, EMBED_DIM), dtype=jnp.float32), 'Wq': jax.random.uniform(ks[2], (EMBED_DIM, EMBED_DIM), jnp.float32, -s, s), 'bq': jax.random.uniform(ks[3], (EMBED_DIM,), jnp.float32, -s, s), 'Wk': jax.random.uniform(ks[4], (EMBED_DIM, EMBED_DIM), jnp.float32, -s, s), 'bk': jax.random.uniform(ks[5], (EMBED_DIM,), jnp.float32, -s, s), 'Wv': jax.random.uniform(ks[6], (EMBED_DIM, EMBED_DIM), jnp.float32, -s, s), 'bv': jax.random.uniform(ks[7], (EMBED_DIM,), jnp.float32, -s, s)}
    _L1_xattn_all = _L1_xattn_setup()
    _L1_xattn_in = {k: v for k, v in _L1_xattn_all.items() if k in ('Wq', 'bq', 'Wk', 'bk', 'Wv', 'bv')}
    del _L1_xattn_all

    def _L1_attn_setup():
        import jax, jax.numpy as jnp
        import numpy as np
        _SCAN_CHUNK = 32

        def _causal_decay_scan(x, decay, init):
            B, H, T, D = x.shape
            C = min(_SCAN_CHUNK, T)
            assert T % C == 0
            nC = T // C
            log_decay = jnp.log(jnp.clip(decay.astype(jnp.float32), 1e-08, None))
            c_idx = jnp.arange(C, dtype=jnp.float32)
            log_p = log_decay[..., None] * c_idx.reshape(1, 1, C, 1)
            p = jnp.exp(log_p)
            inv_p = jnp.exp(-log_p)
            init_p = jnp.exp(log_decay[..., None] * (c_idx + 1.0).reshape(1, 1, C, 1))
            xc = x.reshape(B, H, nC, C, D).transpose(2, 0, 1, 3, 4).astype(jnp.float32)

            def step(state, chunk):
                cs = jnp.cumsum(chunk * inv_p, axis=2)
                out = cs * p + state[:, :, None, :] * init_p
                return (out[:, :, -1, :], out)
            _, outs = jax.lax.scan(step, init.astype(jnp.float32), xc)
            return outs.transpose(1, 2, 0, 3, 4).reshape(B, H, T, D).astype(x.dtype)

        def _phi(x):
            return jax.nn.elu(x) + 1.0
        key = jax.random.key(seed)
        ks = jax.random.split(key, 5)
        B, T, hidden, H = (4, 1024, 256, 16)
        s = 1.0 / np.sqrt(hidden)
        x = jax.random.normal(ks[0], (B, T, hidden), dtype=jnp.float32)
        Wqkv = jax.random.normal(ks[1], (3 * hidden, hidden), dtype=jnp.float32) * s
        Wout = jax.random.normal(ks[2], (hidden, hidden), dtype=jnp.float32) * s
        Wgate = jax.random.normal(ks[3], (hidden, hidden), dtype=jnp.float32) * s
        bgate = jnp.zeros((hidden,), dtype=jnp.float32)
        logit = float(np.log(0.95 / 0.05))
        decay_param = jnp.full((H,), logit, dtype=jnp.float32)
        return {'x': x, 'Wqkv': Wqkv, 'Wout': Wout, 'Wgate': Wgate, 'bgate': bgate, 'decay_param': decay_param}
    _L1_attn_all = _L1_attn_setup()
    _L1_attn_in = {k: v for k, v in _L1_attn_all.items() if k in ('Wqkv', 'Wout', 'Wgate', 'bgate', 'decay_param')}
    del _L1_attn_all

    def _L1_ffn_setup():
        import jax, jax.numpy as jnp
        import numpy as np
        IN_DIM = 256
        OUT_DIM = 256
        NUM_EXPERTS = 8
        TOP_K = 2
        key = jax.random.key(seed)
        ks = jax.random.split(key, 5)
        s = 1.0 / np.sqrt(IN_DIM)
        x = jax.random.normal(ks[0], (4, 512, IN_DIM), dtype=jnp.float32)
        Wg = jax.random.uniform(ks[1], (IN_DIM, NUM_EXPERTS), jnp.float32, -s, s)
        bg = jnp.zeros((NUM_EXPERTS,), jnp.float32)
        We = jax.random.uniform(ks[2], (NUM_EXPERTS, OUT_DIM, IN_DIM), jnp.float32, -s, s)
        be = jax.random.uniform(ks[3], (NUM_EXPERTS, OUT_DIM), jnp.float32, -s, s)
        return {'x': x, 'Wg': Wg, 'bg': bg, 'We': We, 'be': be}
    _L1_ffn_all = _L1_ffn_setup()
    _L1_ffn_in = {k: v for k, v in _L1_ffn_all.items() if k in ('Wg', 'bg', 'We', 'be')}
    del _L1_ffn_all
    return {'x': x, 'ctx_1024': ctx_1024, 'mask_BxSxS2_bf1': mask_BxSxS2_bf1, 'L0_xattn_Wq': _L0_xattn_in['Wq'], 'L0_xattn_Wkv': _L0_xattn_in['Wkv'], 'L0_xattn_Wo': _L0_xattn_in['Wo'], 'L0_attn_Wq': _L0_attn_in['Wq'], 'L0_attn_Wk': _L0_attn_in['Wk'], 'L0_attn_Wv': _L0_attn_in['Wv'], 'L0_attn_Wg': _L0_attn_in['Wg'], 'L0_attn_Wo': _L0_attn_in['Wo'], 'L0_attn_conv_q': _L0_attn_in['conv_q'], 'L0_attn_conv_k': _L0_attn_in['conv_k'], 'L0_attn_conv_v': _L0_attn_in['conv_v'], 'L0_attn_Wgk': _L0_attn_in['Wgk'], 'L0_attn_Wb': _L0_attn_in['Wb'], 'L0_attn_b_b': _L0_attn_in['b_b'], 'L0_attn_A_log': _L0_attn_in['A_log'], 'L0_attn_dt_bias': _L0_attn_in['dt_bias'], 'L0_attn_g_norm_weight': _L0_attn_in['g_norm_weight'], 'L0_ffn_router_w': _L0_ffn_in['router_w'], 'L0_ffn_router_b': _L0_ffn_in['router_b'], 'L0_ffn_expert_w': _L0_ffn_in['expert_w'], 'L0_ffn_expert_b': _L0_ffn_in['expert_b'], 'L1_xattn_Wq': _L1_xattn_in['Wq'], 'L1_xattn_bq': _L1_xattn_in['bq'], 'L1_xattn_Wk': _L1_xattn_in['Wk'], 'L1_xattn_bk': _L1_xattn_in['bk'], 'L1_xattn_Wv': _L1_xattn_in['Wv'], 'L1_xattn_bv': _L1_xattn_in['bv'], 'L1_attn_Wqkv': _L1_attn_in['Wqkv'], 'L1_attn_Wout': _L1_attn_in['Wout'], 'L1_attn_Wgate': _L1_attn_in['Wgate'], 'L1_attn_bgate': _L1_attn_in['bgate'], 'L1_attn_decay_param': _L1_attn_in['decay_param'], 'L1_ffn_Wg': _L1_ffn_in['Wg'], 'L1_ffn_bg': _L1_ffn_in['bg'], 'L1_ffn_We': _L1_ffn_in['We'], 'L1_ffn_be': _L1_ffn_in['be']}

def reference(x, ctx_1024, mask_BxSxS2_bf1, L0_xattn_Wq, L0_xattn_Wkv, L0_xattn_Wo, L0_attn_Wq, L0_attn_Wk, L0_attn_Wv, L0_attn_Wg, L0_attn_Wo, L0_attn_conv_q, L0_attn_conv_k, L0_attn_conv_v, L0_attn_Wgk, L0_attn_Wb, L0_attn_b_b, L0_attn_A_log, L0_attn_dt_bias, L0_attn_g_norm_weight, L0_ffn_router_w, L0_ffn_router_b, L0_ffn_expert_w, L0_ffn_expert_b, L1_xattn_Wq, L1_xattn_bq, L1_xattn_Wk, L1_xattn_bk, L1_xattn_Wv, L1_xattn_bv, L1_attn_Wqkv, L1_attn_Wout, L1_attn_Wgate, L1_attn_bgate, L1_attn_decay_param, L1_ffn_Wg, L1_ffn_bg, L1_ffn_We, L1_ffn_be):
    import jax
    import jax.numpy as jnp

    def _L0_xattn_ref(x, context, mask, Wq, Wkv, Wo):
        import jax, jax.numpy as jnp
        import numpy as np
        DIM = 256
        HEAD_DIM = 64
        NUM_HEADS = DIM // HEAD_DIM
        SCALE = HEAD_DIM ** (-0.5)
        B, N, C = x.shape
        M = context.shape[1]
        H, D = (NUM_HEADS, HEAD_DIM)
        q = (x @ Wq).reshape(B, N, H, D).transpose(0, 2, 1, 3)
        kv = (context @ Wkv).reshape(B, M, 2, H, D).transpose(2, 0, 3, 1, 4)
        k, v = (kv[0], kv[1])
        attn = jnp.einsum('bhnd,bhmd->bhnm', q, k) * SCALE
        attn = jnp.where(mask[:, None, :, :], attn, -jnp.inf)
        attn = jax.nn.softmax(attn, axis=-1)
        out = jnp.einsum('bhnm,bhmd->bhnd', attn, v)
        out = out.transpose(0, 2, 1, 3).reshape(B, N, C)
        return out @ Wo

    def _L0_attn_ref(hidden_states, Wq, Wk, Wv, Wg, Wo, conv_q, conv_k, conv_v, Wgk, Wb, b_b, A_log, dt_bias, g_norm_weight):
        import jax, jax.numpy as jnp
        import numpy as np
        import math
        B, L, HID = (2, 1024, 256)
        NH, DK, DV = (12, 64, 128)
        KD, VD, CS = (NH * DK, NH * DV, 4)
        SCALE = DK ** (-0.5)

        def _causal_depthwise_conv(x, w):
            c, k = w.shape
            xt = jnp.transpose(x, (0, 2, 1))
            out = jax.lax.conv_general_dilated(xt, w[:, None, :], window_strides=(1,), padding=[(k - 1, 0)], feature_group_count=c, dimension_numbers=('NCH', 'OIH', 'NCH'))
            return jnp.transpose(out, (0, 2, 1))

        def _l2norm(x, eps=1e-06):
            return x * jax.lax.rsqrt(jnp.sum(x * x, axis=-1, keepdims=True) + eps)

        def _gated_delta_net(hidden_states, Wq, Wk, Wv, Wg, Wo, conv_q, conv_k, conv_v, Wgk, Wb, b_b, A_log, dt_bias, g_norm_weight):
            b, l, _ = hidden_states.shape
            q = jax.nn.silu(_causal_depthwise_conv(hidden_states @ Wq, conv_q))
            k = jax.nn.silu(_causal_depthwise_conv(hidden_states @ Wk, conv_k))
            v = jax.nn.silu(_causal_depthwise_conv(hidden_states @ Wv, conv_v))
            gk = -jnp.exp(A_log) * jax.nn.softplus(hidden_states @ Wgk + dt_bias)
            beta = jax.nn.sigmoid(hidden_states @ Wb + b_b)
            q = jnp.transpose(q.reshape(b, l, NH, DK), (0, 2, 1, 3))
            k = jnp.transpose(k.reshape(b, l, NH, DK), (0, 2, 1, 3))
            v = jnp.transpose(v.reshape(b, l, NH, DV), (0, 2, 1, 3))
            q = _l2norm(q) * SCALE
            k = _l2norm(k)
            qs = jnp.moveaxis(q, 2, 0)
            ks_ = jnp.moveaxis(k, 2, 0)
            vs = jnp.moveaxis(v, 2, 0)
            bs = jnp.moveaxis(beta, 1, 0)
            gs = jnp.moveaxis(gk, 1, 0)

            def step(S, inp):
                qt, kt, vt, bt, gt = inp
                S = S * jnp.exp(gt)[..., None, None]
                kv = jnp.einsum('bhk,bhkv->bhv', kt, S)
                delta = (vt - kv) * bt[..., None]
                S = S + jnp.einsum('bhk,bhv->bhkv', kt, delta)
                ot = jnp.einsum('bhk,bhkv->bhv', qt, S)
                return (S, ot)
            S0 = jnp.zeros((b, NH, DK, DV), hidden_states.dtype)
            _, os_ = jax.lax.scan(step, S0, (qs, ks_, vs, bs, gs))
            o = jnp.moveaxis(os_, 0, 1)
            g = (hidden_states @ Wg).reshape(b, l, NH, DV)
            var = jnp.mean(o * o, axis=-1, keepdims=True)
            o = o * jax.lax.rsqrt(var + 1e-05) * g_norm_weight
            o = o * g * jax.nn.sigmoid(g)
            return o.reshape(b, l, VD) @ Wo
        return _gated_delta_net(hidden_states, Wq, Wk, Wv, Wg, Wo, conv_q, conv_k, conv_v, Wgk, Wb, b_b, A_log, dt_bias, g_norm_weight)

    def _L0_ffn_ref(x, router_w, router_b, expert_w, expert_b):
        import jax, jax.numpy as jnp
        import numpy as np
        B, S, D, E = (2, 512, 256, 8)
        logits = jnp.einsum('bsd,ed->bse', x, router_w) + router_b
        probs = jax.nn.softmax(logits, axis=-1)
        weights = jnp.max(probs, axis=-1)
        top1 = jnp.argmax(probs, axis=-1)
        y_all = jnp.einsum('bsd,eod->bseo', x, expert_w) + expert_b
        y = jnp.take_along_axis(y_all, top1[:, :, None, None], axis=2)[:, :, 0, :]
        out = y * weights[:, :, None]
        return out

    def _L1_xattn_ref(x_1, x_2, Wq, bq, Wk, bk, Wv, bv):
        import jax, jax.numpy as jnp
        import numpy as np
        N_HEADS = 16
        EMBED_DIM = 256
        HEAD_DIM = EMBED_DIM // N_HEADS
        B, T_TGT, T_SRC = (2, 512, 512)
        Bt, Tt, C = x_1.shape
        q = (x_1 @ Wq.T + bq).reshape(Bt, Tt, N_HEADS, HEAD_DIM).transpose(0, 2, 1, 3)
        k = (x_2 @ Wk.T + bk).reshape(Bt, -1, N_HEADS, HEAD_DIM).transpose(0, 2, 1, 3)
        v = (x_2 @ Wv.T + bv).reshape(Bt, -1, N_HEADS, HEAD_DIM).transpose(0, 2, 1, 3)
        scores = jnp.einsum('bhqd,bhkd->bhqk', q, k) * HEAD_DIM ** (-0.5)
        attn = jax.nn.softmax(scores, axis=-1)
        out = jnp.einsum('bhqk,bhkd->bhqd', attn, v)
        return out.transpose(0, 2, 1, 3).reshape(Bt, Tt, C)

    def _L1_attn_ref(x, Wqkv, Wout, Wgate, bgate, decay_param):
        import jax, jax.numpy as jnp
        import numpy as np
        _SCAN_CHUNK = 32

        def _causal_decay_scan(x, decay, init):
            B, H, T, D = x.shape
            C = min(_SCAN_CHUNK, T)
            assert T % C == 0
            nC = T // C
            log_decay = jnp.log(jnp.clip(decay.astype(jnp.float32), 1e-08, None))
            c_idx = jnp.arange(C, dtype=jnp.float32)
            log_p = log_decay[..., None] * c_idx.reshape(1, 1, C, 1)
            p = jnp.exp(log_p)
            inv_p = jnp.exp(-log_p)
            init_p = jnp.exp(log_decay[..., None] * (c_idx + 1.0).reshape(1, 1, C, 1))
            xc = x.reshape(B, H, nC, C, D).transpose(2, 0, 1, 3, 4).astype(jnp.float32)

            def step(state, chunk):
                cs = jnp.cumsum(chunk * inv_p, axis=2)
                out = cs * p + state[:, :, None, :] * init_p
                return (out[:, :, -1, :], out)
            _, outs = jax.lax.scan(step, init.astype(jnp.float32), xc)
            return outs.transpose(1, 2, 0, 3, 4).reshape(B, H, T, D).astype(x.dtype)

        def _phi(x):
            return jax.nn.elu(x) + 1.0
        B, T, hidden = x.shape
        H = decay_param.shape[0]
        D = hidden // H
        qkv = x @ Wqkv.T
        q, k, v = jnp.split(qkv, 3, axis=-1)
        q = q.reshape(B, T, H, D).transpose(0, 2, 1, 3)
        k = k.reshape(B, T, H, D).transpose(0, 2, 1, 3)
        v = v.reshape(B, T, H, D).transpose(0, 2, 1, 3)
        q = _phi(q)
        k = _phi(k)
        decay = jax.nn.sigmoid(decay_param).reshape(1, H, 1)
        kv_init = jnp.zeros((B, H, D), dtype=x.dtype)
        ksum_init = jnp.zeros((B, H, D), dtype=x.dtype)
        running_kv = _causal_decay_scan(k * v, decay, kv_init)
        running_ksum = _causal_decay_scan(k, decay, ksum_init)
        den = jnp.clip(jnp.sum(q * running_ksum, axis=-1, keepdims=True), 1e-06, None)
        out = q * running_kv / den
        v_direct = v.transpose(0, 2, 1, 3).reshape(B, T, hidden)
        out = out.transpose(0, 2, 1, 3).reshape(B, T, hidden)
        g = jax.nn.sigmoid(out @ Wgate.T + bgate)
        out = g * out + (1.0 - g) * v_direct
        return out @ Wout.T

    def _L1_ffn_ref(x, Wg, bg, We, be):
        import jax, jax.numpy as jnp
        import numpy as np
        IN_DIM = 256
        OUT_DIM = 256
        NUM_EXPERTS = 8
        TOP_K = 2
        gate = jax.nn.softmax(x @ Wg + bg, axis=-1)
        topk_vals, topk_idx = jax.lax.top_k(gate, TOP_K)
        onehot = jax.nn.one_hot(topk_idx, NUM_EXPERTS, dtype=gate.dtype)
        gate_sparse = jnp.einsum('bsk,bske->bse', topk_vals, onehot)
        gate_sparse = gate_sparse / jnp.sum(gate_sparse, axis=-1, keepdims=True)
        y = jnp.einsum('bsi,eoi->bseo', x, We) + be[None, None, :, :].transpose(0, 1, 2, 3)
        out = jnp.einsum('bseo,bse->bso', y, gate_sparse)
        return out
    x = x + _L0_xattn_ref(_layernorm(x, axis=-1), ctx_1024, mask_BxSxS2_bf1, L0_xattn_Wq, L0_xattn_Wkv, L0_xattn_Wo)
    x = x + _L0_attn_ref(_layernorm(x, axis=-1), L0_attn_Wq, L0_attn_Wk, L0_attn_Wv, L0_attn_Wg, L0_attn_Wo, L0_attn_conv_q, L0_attn_conv_k, L0_attn_conv_v, L0_attn_Wgk, L0_attn_Wb, L0_attn_b_b, L0_attn_A_log, L0_attn_dt_bias, L0_attn_g_norm_weight)
    x = x + _L0_ffn_ref(_layernorm(x, axis=-1), L0_ffn_router_w, L0_ffn_router_b, L0_ffn_expert_w, L0_ffn_expert_b)
    x = x + _L1_xattn_ref(_layernorm(x, axis=-1), ctx_1024, L1_xattn_Wq, L1_xattn_bq, L1_xattn_Wk, L1_xattn_bk, L1_xattn_Wv, L1_xattn_bv)
    x = x + _L1_attn_ref(_layernorm(x, axis=-1), L1_attn_Wqkv, L1_attn_Wout, L1_attn_Wgate, L1_attn_bgate, L1_attn_decay_param)
    x = x + _L1_ffn_ref(_layernorm(x, axis=-1), L1_ffn_Wg, L1_ffn_bg, L1_ffn_We, L1_ffn_be)
    return x

_drawn_inputs = setup_inputs


def setup_inputs(seed=0):
    import zlib

    import numpy as np

    out = dict(_drawn_inputs(seed))
    spreads = {'L0_attn_g_norm_weight': (1.0, 0.2),
     'L0_ffn_router_b': (0.0, 0.1),
     'L0_ffn_expert_b': (0.0, 0.1),
     'L1_attn_bgate': (0.0, 0.1),
     'L1_attn_decay_param': (2.944438934326172, 0.6),
     'L1_ffn_bg': (0.0, 0.1)}
    factors = {'L0_attn_b_b': 2.826,
     'L1_xattn_bq': 8.0,
     'L1_xattn_bk': 8.0,
     'L1_attn_Wgate': 3.277,
     'L1_ffn_be': 3.246}
    for name, (base, spread) in spreads.items():
        noise = np.random.default_rng([zlib.crc32(name.encode()), seed]).standard_normal(out[name].shape)
        drawn = base * np.exp(spread * noise) if base else spread * noise
        out[name] = jnp.asarray(drawn.astype(out[name].dtype))
    for name, factor in factors.items():
        out[name] = (out[name] * factor).astype(out[name].dtype)
    return out
```

```python
from contextlib import ExitStack

import concourse.bass as bass
from concourse import mybir

F32 = mybir.dt.float32
BF16 = mybir.dt.bfloat16
U8 = mybir.dt.uint8
ALU = mybir.AluOpType
ACT = mybir.ActivationFunctionType
AX = mybir.AxisListType

P = 128
D = 256
DC = D // P
M = 12544
CT = 7
CH = CT * P
HCH = CH // 2
NCH = M // CH
LN_EPS = 1e-5
MASKED = float(2.0 ** 100)
LOWEST = -float(2.0 ** 101)

H0, D0 = 4, 64
S0 = D0 ** -0.5
H1, D1 = 16, 16
S1 = D1 ** -0.5
K_TERM = (0, 1, 0, 1, 2, 0)
Q_TERM = (0, 0, 1, 1, 0, 2)
NJ = len(K_TERM)
KROWS = NJ * D1
KONES = KROWS + 3

NH, DK, DV = 12, 64, 128
KB = NH * DK // P
VB = NH * DV // P
CB = 2 * KB + VB
TAPS = 4
GH = 4
NG = NH // GH
LEVELS = (1, 2, 4, 8, 16, 32, 64)

E = 8
HL, DL = 16, 16


def build(nc, a, out):
    sems = {}
    counts = {}
    ctx = ExitStack()

    def S(name):
        if name not in sems:
            sems[name] = nc.alloc_semaphore(name)
        return sems[name]

    def renew(keep):
        old = [sems.pop(name) for name in list(sems) if name not in keep]
        counts.clear()
        nc.clear_and_free_semaphores(old)
        with nc.Block() as block:
            @block.gpsimd
            def _(pool):
                pool.nop()

    def some(value):
        return not (isinstance(value, int) and value <= 0)

    def nth(name):
        counts[name] = counts.get(name, 0) + 1
        return counts[name]

    def bc(ap, axis, shape):
        return ap.unsqueeze(axis).to_broadcast(shape)

    def wcols(w, c=DC):
        return w.rearrange("(c p) n -> p c n", c=c)

    def sb(st, name, shape, dt=F32):
        return st.enter_context(nc.sbuf_tensor(name, shape, dt))

    def maximum(dve, x, c, s, mx, top, run, dm, neg, n3, reads):
        dve.wait_ge(S("smread" + x), reads * (c + 1))
        dve.tensor_reduce(top[:], mx[:], AX.X, ALU.max).then_inc(S("maxstep" + x), 1)
        dve.wait_ge(S("maxstep" + x), 6 * c + 1)
        dve.tensor_tensor(run[:, s], run[:, 1 - s], top[:], ALU.max).then_inc(S("maxstep" + x), 1)
        dve.wait_ge(S("maxstep" + x), 6 * c + 2)
        if some(c - 1):
            dve.wait_ge(S("f" + x), c - 1)
        dve.tensor_scalar(neg[:], run[:, s], -1.0, None, ALU.mult).then_inc(S("maxstep" + x), 1)
        if some(c):
            dve.wait_ge(S("mt" + x), c)
        dve.tensor_scalar(n3[:, 0], run[:, s], -1.0, None, ALU.mult).then_inc(S("maxstep" + x), 1)
        dve.tensor_tensor(dm[:, s], run[:, 1 - s], run[:, s], ALU.subtract).then_inc(S("dm" + x), 1)
        dve.wait_ge(S("maxstep" + x), 6 * c + 4)
        dve.tensor_tensor(neg[:], neg[:], n3[:, 0], ALU.subtract).then_inc(S("maxstep" + x), 1)
        dve.wait_ge(S("maxstep" + x), 6 * c + 5)
        dve.tensor_copy(n3[:, 1], neg[:]).then_inc(S("maxstep" + x), 1)
        dve.wait_ge(S("maxstep" + x), 6 * c + 6)
        dve.tensor_tensor(n3[:, 2], neg[:], n3[:, 1], ALU.subtract).then_inc(S("n3" + x), 1)

    with ctx:
        bank = [ctx.enter_context(nc.psum_tensor(f"bank{i}", [P, 512], F32)) for i in range(8)]
        bankb = [b[:].bitcast(BF16) for b in bank]

        keep = ctx.enter_context(ExitStack())
        xres = sb(keep, "xres", [P, D])
        ident = sb(keep, "ident", [P, P])
        identb = sb(keep, "identb", [P, P], BF16)
        onesb = sb(keep, "onesb", [P, P], BF16)
        tri = sb(keep, "tri", [P, P])
        below = sb(keep, "below", [P, P])
        mhalf = sb(keep, "mhalf", [P, NH])
        eps6 = sb(keep, "eps6", [P, 1])
        stats = sb(keep, "stats", [P, 6])
        mv = sb(keep, "mv", [P, 2])
        rstd = sb(keep, "rstd", [P, 1])
        xn = sb(keep, "xn", [P, D])
        hT = sb(keep, "hT", [P, DC, P])

        def ln_dve(dve, tag):
            dve.bn_stats(stats[:], xres[:]).then_inc(S(tag + "_stats"), 1)
            dve.wait_ge(S(tag + "_stats"), nth(tag + "_stats"))
            dve.bn_aggr(mv[:], stats[:]).then_inc(S(tag + "_var"), 1)
            dve.wait_ge(S(tag + "_var"), nth(tag + "_var"))
            dve.wait_ge(S(tag + "_rstd"), 2)
            dve.tensor_scalar(xn[:], xres[:], mv[:, 0:1], rstd[:, 0:1], ALU.subtract, ALU.mult).then_inc(S(tag + "_xn"), 1)
            dve.wait_ge(S(tag + "_xn"), nth(tag + "_xn"))

        def ln_pool(pool, tag):
            pool.wait_ge(S(tag + "_var"), 1)
            pool.tensor_scalar(rstd[:], mv[:, 1:2], LN_EPS, None, ALU.add).then_inc(S(tag + "_rstd"), 1)
            pool.wait_ge(S(tag + "_rstd"), nth(tag + "_rstd"))
            pool.tensor_tensor(rstd[:], rstd[:], mhalf[:, 0:1], ALU.pow).then_inc(S(tag + "_rstd"), 1)
            pool.wait_ge(S(tag + "_rstd"), nth(tag + "_rstd"))

        def ln_pe(pe, tag, b):
            pe.wait_ge(S(tag + "_xn"), 1)
            for k in range(DC):
                ins = pe.transpose(bank[b][:, k * P:(k + 1) * P], xn[:, k * P:(k + 1) * P], ident[:])
            ins.then_inc(S(tag + "_xnT"), 1)

        def ln_act(act, tag, b):
            act.wait_ge(S(tag + "_xnT"), 1)
            act.copy(hT[:].rearrange("p k t -> p (k t)"), bank[b][:, 0:D]).then_inc(S(tag + "_hT"), 1)

        er = ExitStack()
        ew0 = sb(er, "ew0", [P, E * DC, D])

        gw = ExitStack()
        Wc = sb(gw, "Wc", [P, DC, CB * P])
        Wg = sb(gw, "Wg", [P, DC, NH * DV])
        Wo = sb(gw, "Wo", [P, NH, D])
        Wgb = sb(gw, "Wgb", [P, DC, 2 * NH])
        convw = sb(gw, "convw", [P, CB, TAPS])
        gbias = sb(gw, "gbias", [P, 2 * NH])
        nA = sb(gw, "nA", [P, NH])
        gnw = sb(gw, "gnw", [P, DV])

        def load_delta_weights(eng):
            def get(dst, src):
                eng.dma_start(dst, src).then_inc(S("gw_in"), 16)
            get(Wc[:, :, 0:KB * P], wcols(a["L0_attn_Wq"]))
            get(Wc[:, :, KB * P:2 * KB * P], wcols(a["L0_attn_Wk"]))
            get(Wc[:, :, 2 * KB * P:], wcols(a["L0_attn_Wv"]))
            get(Wg[:], wcols(a["L0_attn_Wg"]))
            get(Wo[:], wcols(a["L0_attn_Wo"], NH))
            get(Wgb[:, :, 0:NH], wcols(a["L0_attn_Wgk"]))
            get(Wgb[:, :, NH:], wcols(a["L0_attn_Wb"]))
            get(convw[:, 0:KB], wcols(a["L0_attn_conv_q"], KB))
            get(convw[:, KB:2 * KB], wcols(a["L0_attn_conv_k"], KB))
            get(convw[:, 2 * KB:], wcols(a["L0_attn_conv_v"], VB))
            get(gbias[:, 0:NH], a["L0_attn_dt_bias"].partition_broadcast(P))
            get(gbias[:, NH:], a["L0_attn_b_b"].partition_broadcast(P))
            get(nA[:], a["L0_attn_A_log"].partition_broadcast(P))
            get(gnw[:], a["L0_attn_g_norm_weight"].partition_broadcast(P))
            eng.dma_start(ew0[:], a["L0_ffn_expert_w"].rearrange("e (c p) d -> p (e c) d", p=P)).then_inc(S("ew0_in"), 16)
        GW_LOADS = 14

        xa = ExitStack()
        Wo0 = sb(xa, "Wo0", [P, DC, D])
        run0 = sb(xa, "run0", [P, 2, H0])
        acc0 = sb(xa, "acc0", [P, H0, D0 + 1])
        o0 = sb(xa, "o0", [P, D])
        oT0 = sb(xa, "oT0", [P, DC, P])
        rd0 = sb(xa, "rd0", [P, H0])
        fl0 = sb(xa, "fl0", [P, H0])
        l0 = ExitStack()
        Wq0 = sb(l0, "Wq0", [P, DC, D])
        Wkv0 = sb(l0, "Wkv0", [P, DC, 2 * D])
        q0 = sb(l0, "q0", [P, DC, 2, P])
        eye4 = sb(l0, "eye4", [P, H0, P], BF16)
        ctx0 = sb(l0, "ctx0", [P, 2, CT, D])
        ctxT0 = sb(l0, "ctxT0", [P, DC, CH])
        kT0 = sb(l0, "kT0", [P, 2, DC, CH])
        v0 = sb(l0, "v0", [P, 2, CT, H0, D0 + 1])
        mask0 = sb(l0, "mask0", [P, 2, CH], U8)
        pen0 = sb(l0, "pen0", [P, 2, CH], BF16)
        gate0 = sb(l0, "gate0", [P, 2])
        junk0 = sb(l0, "junk0", [P, 2, HCH])
        mx0 = sb(l0, "mx0", [P, H0, 2])
        m40 = sb(l0, "m40", [P, H0])
        dm0 = sb(l0, "dm0", [P, 2, H0])
        f0 = sb(l0, "f0", [P, 2, H0])
        neg0 = sb(l0, "neg0", [P, H0])
        n30 = sb(l0, "n30", [P, 3, H0], BF16)
        n3T0 = sb(l0, "n3T0", [3 * H0, 2, P], BF16)
        mrow0 = sb(l0, "mrow0", [P, 2, H0, P], BF16)
        p0 = sb(l0, "p0", [P, 2, H0 * P])
        ots0 = sb(l0, "ots0", [D0 + 1, H0 * P])

        ctx_rows = a["ctx_1024"].rearrange("b m d -> (b m) d")
        mask_rows = a["mask_BxSxS2_bf1"].rearrange("b q m -> (b q) m")

        def chunk_of(c):
            return ctx_rows[bass.ds(c * CH, CH), :].rearrange("(t p) d -> p t d", p=P)

        with nc.Block() as block:
            @block.sync
            def _(sp):
                sp.dma_start(xres[:], a["x"].rearrange("b q d -> (b q) d")).then_inc(S("x_in"), 16)
                sp.dma_start(Wq0[:], wcols(a["L0_xattn_Wq"])).then_inc(S("wq0_in"), 16)
                sp.dma_start(Wkv0[:], wcols(a["L0_xattn_Wkv"])).then_inc(S("wkv0_in"), 16)
                sp.dma_start(Wo0[:], wcols(a["L0_xattn_Wo"])).then_inc(S("wo0_in"), 16)

            @block.gpsimd
            def _(pool):
                pool.memset(eps6[:], 1e-6).then_inc(S("eps6"), 1)
                pool.memset(mhalf[:], -0.5).then_inc(S("mhalf"), 1)
                pool.wait_ge(S("mhalf"), 1)
                pool.memset(ident[:], 0.0).then_inc(S("ident"), 1)
                pool.wait_ge(S("ident"), nth("ident"))
                pool.affine_select(out=ident[:], in_=ident[:], compare_op=ALU.not_equal, fill=1.0, base=0,
                                              pattern=[[-1, P]], channel_multiplier=1).then_inc(S("ident"), 1)
                pool.wait_ge(S("ident"), nth("ident"))
                ln_pool(pool, "ln0")
                pool.tensor_copy(identb[:], ident[:]).then_inc(S("identb"), 1)
                pool.wait_ge(S("identb"), nth("identb"))
                pool.memset(onesb[:], 1.0).then_inc(S("onesb"), 1)
                pool.wait_ge(S("onesb"), nth("onesb"))
                pool.tensor_copy(eye4[:], bc(identb[:], 1, [P, H0, P])).then_inc(S("eye4"), 1)
                pool.wait_ge(S("eye4"), nth("eye4"))
                pool.memset(tri[:], 1.0).then_inc(S("tri"), 1)
                pool.wait_ge(S("tri"), nth("tri"))
                pool.affine_select(out=tri[:], in_=tri[:], compare_op=ALU.is_ge, fill=0.0, base=0,
                                              pattern=[[1, P]], channel_multiplier=-1).then_inc(S("tri"), 1)
                pool.wait_ge(S("tri"), nth("tri"))
                pool.memset(below[:], 1.0).then_inc(S("below"), 1)
                pool.wait_ge(S("below"), nth("below"))
                pool.affine_select(out=below[:], in_=below[:], compare_op=ALU.is_gt, fill=0.0, base=0,
                                              pattern=[[-1, P]], channel_multiplier=1).then_inc(S("below"), 1)
                pool.wait_ge(S("below"), nth("below"))
                pool.memset(v0[:], 1.0).then_inc(S("v0_ones"), 1)
                pool.memset(mrow0[:], 0.0).then_inc(S("mrow0_zero"), 1)
                pool.memset(acc0[:], 0.0).then_inc(S("acc0_zero"), 1)
                pool.memset(run0[:], LOWEST).then_inc(S("run0_lowest"), 1)

            @block.vector
            def _(dve):
                dve.memset(q0[:], 0.0).then_inc(S("q0_zero"), 1)
                dve.wait_ge(S("x_in"), 16)
                ln_dve(dve, "ln0")
                dve.wait_ge(S("q0_zero"), 1)
                dve.wait_ge(S("q0_psum"), 1)
                for b in range(DC):
                    for e in range(2):
                        r = slice(e * D0, (e + 1) * D0)
                        dve.tensor_scalar(q0[r, b, e, :], bank[1][r, b * P:(b + 1) * P], S0, None,
                                          ALU.mult).then_inc(S("q0"), 1)

            @block.tensor
            def _(pe):
                pe.wait_ge(S("ident"), 2)
                ln_pe(pe, "ln0", 0)
                pe.wait_ge(S("ln0_hT"), 1)
                pe.wait_ge(S("wq0_in"), 16)
                for b in range(DC):
                    for k in range(DC):
                        ins = pe.matmul(bank[1][:, b * P:(b + 1) * P], Wq0[:, k, b * P:(b + 1) * P], hT[:, k, :],
                                        start=(k == 0), stop=(k == DC - 1))
                ins.then_inc(S("q0_psum"), 1)

            @block.scalar
            def _(act):
                ln_act(act, "ln0", 0)

        XP, KV, SM, ST, OT, OB = 0, (1, 2), (3, 0), (4, 5), 6, 7
        TG = ((0, 0, 4), (1, 0, 4), (0, 4, 3), (1, 4, 3))
        VG = ((0, 2), (2, 2), (4, 2), (6, 1))
        PLAN0 = ((("T0",), ("T1",)), (("T2",), ("T3", "K0")), (("K1",), ("S0", "K2")), (("S1", "K3"), ("S2", "S3")),
                 (("S4", "V0"), ("S5",)), (("S6", "S7"), ("V1", "M0")), (("V2",), ("V3",)))
        ALL0 = tuple(op for before, after in PLAN0 for op in before + after)

        def steps(eng, step, last):
            step(0, 0, 0)
            with eng.Fori(0, (NCH - 2) // 2) as i:
                step(i * 2 + 1, 1, i)
                step(i * 2 + 2, 0, i + 1)
            last(NCH - 1, 1, (NCH - 2) // 2)

        with nc.Block() as block:
            @block.sync
            def _(sp):
                def load(c, s):
                    if some(4 * (c - 1)):
                        sp.wait_ge(S("xp0"), 4 * (c - 1))
                    sp.dma_start(ctx0[:, s], chunk_of(c)).then_inc(S(f"ctx0_{s}"), 16)
                    if some(c - 1):
                        sp.wait_ge(S("pen0"), c - 1)
                    sp.dma_start(mask0[:, s], mask_rows[:, bass.ds(c * CH, CH)]).then_inc(S(f"mask0_{s}"), 16)

                def rows(c, s):
                    sp.wait_ge(S("n3T0"), c + 1)
                    for k in range(3):
                        sp.dma_start(mrow0[k:k + 1, s], n3T0[k * H0:(k + 1) * H0, s, :]).then_inc(S(f"mrow0_{s}"), 16)

                load(0, 0)
                load(1, 1)
                rows(0, 0)

                def step(c, s, n):
                    load(c + 2, s)
                    rows(c + 1, 1 - s)
                step(0, 0, 0)
                with sp.Fori(0, (NCH - 4) // 2) as i:
                    step(i * 2 + 1, 1, i)
                    step(i * 2 + 2, 0, i + 1)
                step(NCH - 3, 1, None)
                rows(NCH - 1, 1)

            @block.tensor
            def _(pe):
                def side(op, c, s, n):
                    k = int(op[1:])
                    if op[0] == "T":
                        if k == 0:
                            pe.wait_ge(S(f"ctx0_{s}"), 16 * n + 16)
                            if some(c):
                                pe.wait_ge(S("n3T0"), c)
                        if some(4 * c + k):
                            pe.wait_ge(S("ctxT0"), 4 * c + k)
                        h, t0, nt = TG[k]
                        for t in range(nt):
                            ins = pe.transpose(bank[XP][:, t * P:(t + 1) * P], ctx0[:, s, t0 + t, h * P:(h + 1) * P],
                                               ident[:])
                        ins.then_inc(S("xp0"), 1)
                    elif op[0] == "K":
                        half, b = k // 2, k % 2
                        pe.wait_ge(S("ctxT0"), 4 * c + 2 * half + 2)
                        if some(8 * c + k - 1):
                            pe.wait_ge(S("kvread0"), 8 * c + k - 1)
                        for i in range(DC):
                            ins = pe.matmul(bank[KV[k % 2]][:, 0:HCH], Wkv0[:, i, b * P:(b + 1) * P],
                                            ctxT0[:, i, half * HCH:(half + 1) * HCH], start=(i == 0), stop=(i == DC - 1))
                        ins.then_inc(S("kv0"), 1)
                    elif op[0] == "S":
                        half, h = k // H0, k % H0
                        pe.wait_ge(S("kvread0"), 8 * c + 2 * half + h // 2 + 1)
                        if k == 1:
                            pe.wait_ge(S("ctxT0"), 4 * c + 4)
                        if some(8 * c + k - 1) and k != 1:
                            pe.wait_ge(S("smread0"), 8 * c + k - 1)
                        pe.matmul(bank[SM[k % 2]][:, 0:HCH], q0[:, h // 2, h % 2, :],
                                  kT0[:, s, h // 2, half * HCH:(half + 1) * HCH],
                                  start=True, stop=True).then_inc(S("sm0"), 1)
                    elif op[0] == "V":
                        t0, nt = VG[k]
                        if some(8 * c + 4 + k - 1):
                            pe.wait_ge(S("kvread0"), 8 * c + 4 + k - 1)
                        for t in range(nt):
                            for i in range(DC):
                                ins = pe.matmul(bank[KV[k % 2]][:, t * D:(t + 1) * D],
                                                ctxT0[:, i, (t0 + t) * P:(t0 + t + 1) * P], Wkv0[:, i, D:2 * D],
                                                start=(i == 0), stop=(i == DC - 1))
                        ins.then_inc(S("kv0"), 1)
                    else:
                        pe.wait_ge(S("n30"), c + 1)
                        pe.transpose(bankb[XP][0:3 * H0, 0:P], n30[:].rearrange("p k h -> p (k h)"),
                                     identb[:]).then_inc(S("mt0"), 1)

                def scores(c, s, n, t):
                    tile = slice(t * P, (t + 1) * P)
                    u = (s + t) % 2
                    if t == 0:
                        pe.wait_ge(S(f"mrow0_{s}"), 48 * n + 48)
                        pe.wait_ge(S("pen0"), c + 1)
                    if some(CT * c + t - 1):
                        pe.wait_ge(S("exp0"), CT * c + t - 1)
                    for b in range(DC):
                        pe.matmul(bank[ST[u]][:, b * 2 * P:(b + 1) * 2 * P], kT0[:, s, b, tile],
                                  q0[:, b].rearrange("p e q -> p (e q)"), start=(b == 0), stop=False,
                                  skip_group_check=True)
                    pe.matmul(bank[ST[u]][:], pen0[:, s, tile], eye4[:].rearrange("p h q -> p (h q)"),
                              start=False, stop=False, skip_group_check=True)
                    pe.matmul(bank[ST[u]][:], onesb[:], mrow0[:, s].rearrange("p h q -> p (h q)"),
                              start=False, stop=True, skip_group_check=True).then_inc(S("st0"), 1)

                def values(c, s, t):
                    pe.wait_ge(S("exp0"), CT * c + t + 1)
                    if t == 0:
                        if some(c):
                            pe.wait_ge(S("ots0"), c)
                        pe.wait_ge(S("kvread0"), 8 * c + 8)
                    for h in range(H0):
                        ins = pe.matmul(bank[OT][0:D0 + 1, h * P:(h + 1) * P], v0[:, s, t, h, :],
                                        p0[:, (s + t) % 2, h * P:(h + 1) * P],
                                        start=(t == 0 and h == 0), stop=(t == CT - 1), skip_group_check=True)
                    ins.then_inc(S("pv0"), 1)

                def turn(c):
                    pe.wait_ge(S("ots0"), c + 1)
                    if some(2 * c):
                        pe.wait_ge(S("acc0"), 2 * c)
                    for h in range(H0):
                        ins = pe.transpose(bank[OB][:, h * (D0 + 1):(h + 1) * (D0 + 1)], ots0[:, h * P:(h + 1) * P],
                                           ident[0:D0 + 1, 0:D0 + 1])
                    ins.then_inc(S("ob0"), 1)

                pe.wait_ge(S("q0"), 4)
                pe.wait_ge(S("wkv0_in"), 16)
                for op in ALL0:
                    side(op, 0, 0, 0)

                def step(c, s, n, ahead=True):
                    scores(c, s, n, 0)
                    if not (isinstance(c, int) and c == 0):
                        turn(c - 1)
                    for t in range(CT):
                        if t + 1 < CT:
                            scores(c, s, n, t + 1)
                        for op in PLAN0[t][0] if ahead else ():
                            side(op, c + 1, 1 - s, n + s)
                        values(c, s, t)
                        for op in PLAN0[t][1] if ahead else ():
                            side(op, c + 1, 1 - s, n + s)
                steps(pe, step, lambda c, s, n: step(c, s, n, False))
                turn(NCH - 1)

            @block.vector
            def _(dve):
                def side(op, c, s, n):
                    k = int(op[1:])
                    if op[0] == "T":
                        h, t0, nt = TG[k]
                        dve.wait_ge(S("xp0"), 4 * c + k + 1)
                        if some(8 * c):
                            dve.wait_ge(S("kv0"), 8 * c)
                        dve.tensor_copy(ctxT0[:, h, t0 * P:(t0 + nt) * P],
                                        bank[XP][:, 0:nt * P]).then_inc(S("ctxT0"), 1)
                    elif op[0] == "S":
                        half, h = k // H0, k % H0
                        dve.wait_ge(S("sm0"), 8 * c + k + 1)
                        if k == 0:
                            dve.wait_ge(S("pen0"), c + 1)
                        dve.memset(gate0[:, k % 2:k % 2 + 1], 0.0)
                        dve.tensor_tensor_reduce(out=junk0[:, k % 2], in0=bank[SM[k % 2]][:, 0:HCH],
                                                 in1=pen0[:, s, half * HCH:(half + 1) * HCH], scale=1.0,
                                                 scalar=LOWEST, op0=ALU.add, op1=ALU.max,
                                                 accum_out=mx0[:, h, half:half + 1]).then_inc(S("smread0"), 1)
                    elif op[0] == "M":
                        maximum(dve, "0", c, s, mx0, m40, run0, dm0, neg0, n30[:], 8)

                def rescale(c, s):
                    dve.wait_ge(S("f0"), c + 1)
                    dve.tensor_tensor(acc0[:], acc0[:], bc(f0[:, s, :], 2, [P, H0, D0 + 1]), ALU.mult).then_inc(S("acc0"), 1)
                    dve.wait_ge(S("acc0"), 2 * c + 1)
                    dve.wait_ge(S("ob0"), c + 1)
                    dve.tensor_tensor(acc0[:], acc0[:], bank[OB][:, 0:H0 * (D0 + 1)].rearrange("p (h d) -> p h d", h=H0),
                                      ALU.add).then_inc(S("acc0"), 1)
                    dve.wait_ge(S("acc0"), 2 * c + 2)

                def penalty(c, s, n):
                    dve.wait_ge(S(f"mask0_{s}"), 16 * n + 16)
                    if some(CT * (c - 1)):
                        dve.wait_ge(S("st0"), CT * (c - 1))
                    dve.tensor_scalar(pen0[:, s], mask0[:, s], MASKED, -MASKED, ALU.mult,
                                      ALU.add).then_inc(S("pen0"), 1)

                penalty(0, 0, 0)
                for op in ALL0:
                    side(op, 0, 0, 0)

                def step(c, s, n):
                    for op in ALL0:
                        side(op, c + 1, 1 - s, n + s)
                        if op == "T1":
                            penalty(c + 1, 1 - s, n + s)
                        if op == "T2" and not (isinstance(c, int) and c == 0):
                            rescale(c - 1, 1 - s)
                steps(dve, step, lambda c, s, n: rescale(c - 1, 1 - s))
                rescale(NCH - 1, 1)

            @block.scalar
            def _(act):
                def side(op, c, s, n):
                    k = int(op[1:])
                    if op[0] == "K":
                        half, b = k // 2, k % 2
                        act.wait_ge(S("kv0"), 8 * c + k + 1)
                        if some(CT * (c - 1)):
                            act.wait_ge(S("st0"), CT * (c - 1))
                        act.copy(kT0[:, s, b, half * HCH:(half + 1) * HCH],
                                 bank[KV[k % 2]][:, 0:HCH]).then_inc(S("kvread0"), 1)
                    elif op[0] == "V":
                        t0, nt = VG[k]
                        act.wait_ge(S("kv0"), 8 * c + 4 + k + 1)
                        if some(CT * (c - 1)):
                            act.wait_ge(S("pv0"), CT * (c - 1))
                        act.copy(v0[:, s, t0:t0 + nt, :, 0:D0],
                                 bank[KV[k % 2]][:, 0:nt * D].rearrange("p (t h d) -> p t h d", t=nt, h=H0)
                                 ).then_inc(S("kvread0"), 1)
                    elif op[0] == "M":
                        act.wait_ge(S("mt0"), c + 1)
                        act.copy(n3T0[:, s, :], bankb[XP][0:3 * H0, 0:P]).then_inc(S("n3T0"), 1)
                        act.wait_ge(S("dm0"), c + 1)
                        act.activation(f0[:, s, :], dm0[:, s, :], ACT.Exp).then_inc(S("f0"), 1)

                def softmax(c, s, t):
                    act.wait_ge(S("st0"), CT * c + t + 1)
                    if some(CT * c + t - 1):
                        act.wait_ge(S("pv0"), CT * c + t - 1)
                    u = (s + t) % 2
                    act.activation(p0[:, u, :], bank[ST[u]][:], ACT.Exp).then_inc(S("exp0"), 1)

                def read_out(c):
                    act.wait_ge(S("pv0"), CT * (c + 1))
                    if some(c):
                        act.wait_ge(S("ob0"), c)
                    act.copy(ots0[:], bank[OT][0:D0 + 1, :]).then_inc(S("ots0"), 1)

                load_delta_weights(act)
                for op in ALL0:
                    side(op, 0, 0, 0)

                def step(c, s, n, ahead=True):
                    if not (isinstance(c, int) and c == 0):
                        read_out(c - 1)
                    softmax(c, s, 0)
                    for t in range(CT):
                        if t + 1 < CT:
                            softmax(c, s, t + 1)
                        for op in PLAN0[t][0] + PLAN0[t][1] if ahead else ():
                            side(op, c + 1, 1 - s, n + s)
                steps(act, step, lambda c, s, n: step(c, s, n, False))
                read_out(NCH - 1)
        l0.close()


        gd = ExitStack()
        level = sb(gd, "level", [P, len(LEVELS), P])
        pair = sb(gd, "pair", [P, P])
        blk64 = sb(gd, "blk64", [P, P])
        half = sb(gd, "half", [P, 2])
        xpad = sb(gd, "xpad", [P, CB, P + TAPS - 1])
        cv = sb(gd, "cv", [P, CB, P])
        gz = sb(gd, "gz", [P, 2 * NH])
        ge = sb(gd, "ge", [P, 2 * NH])
        gp = sb(gd, "gp", [P, NH])
        beta = sb(gd, "beta", [P, NH])
        gk = sb(gd, "gk", [P, NH])
        sg = sb(gd, "sg", [P, NH, DV])
        R = sb(gd, "R", [P, 2, NH, P])
        DT = sb(gd, "DT", [P, NH, P])
        Dm = sb(gd, "Dm", [P, NH, P])
        sq = sb(gd, "sq", [P, NH, P])
        rs = sb(gd, "rs", [P, NH, P])
        kz = sb(gd, "kz", [P, NH, P])
        Am = sb(gd, "Am", [P, 2, NH, P])
        bv = sb(gd, "bv", [P, NH, DV])
        w = sb(gd, "w", [P, NH, DV])
        at = sb(gd, "at", [P, NH, P])
        oh = sb(gd, "oh", [P, NH, DV])
        ss = sb(gd, "ss", [P, NH])
        oT = sb(gd, "oT", [P, NH, P])
        A, AT = (xpad[:].rearrange("p a b -> p (a b)")[:, k * NH * P:(k + 1) * NH * P].rearrange(
            "p (h t) -> p h t", h=NH) for k in range(2))
        X, U = R[:, 0], R[:, 1]
        Z, dl = sq, rs

        def hb(g):
            return slice(g * GH, (g + 1) * GH)

        def b4(i):
            return bank[i][:].rearrange("p (h t) -> p h t", h=GH)

        with nc.Block() as block:
            @block.gpsimd
            def _(pool):
                pool.memset(xpad[:, :, 0:TAPS - 1], 0.0).then_inc(S("xpad_zero"), 1)
                pool.memset(level[:], 0.0).then_inc(S("masks"), 1)
                pool.wait_ge(S("masks"), nth("masks"))
                for n, z in enumerate(LEVELS):
                    v = level[:, n].rearrange("p (b u) -> p b u", u=2 * z)[:, :, z:2 * z]
                    nb = P // (2 * z)
                    pool.memset(v, 1.0).then_inc(S("masks"), 1)
                    pool.wait_ge(S("masks"), nth("masks"))
                    pool.affine_select(out=v, in_=v, compare_op=ALU.is_ge, fill=0.0, base=0,
                                                  pattern=[[-2 * z, nb], [0, z]], channel_multiplier=1).then_inc(S("masks"), 1)
                    pool.wait_ge(S("masks"), nth("masks"))
                    pool.affine_select(out=v, in_=v, compare_op=ALU.is_ge, fill=0.0, base=z - 1,
                                                  pattern=[[2 * z, nb], [0, z]], channel_multiplier=-1).then_inc(S("masks"), 1)
                    pool.wait_ge(S("masks"), nth("masks"))
                pool.memset(pair[:], 0.0).then_inc(S("masks"), 1)
                pool.wait_ge(S("masks"), nth("masks"))
                v = pair[:].rearrange("p (b u) -> p b u", u=2)[:, :, 0:1]
                pool.affine_select(out=v, in_=v, compare_op=ALU.not_equal, fill=1.0, base=-1,
                                              pattern=[[-2, P // 2], [0, 1]], channel_multiplier=1).then_inc(S("masks"), 1)
                pool.wait_ge(S("masks"), nth("masks"))
                pool.memset(blk64[:], 0.0).then_inc(S("masks"), 1)
                pool.wait_ge(S("masks"), nth("masks"))
                pool.memset(half[:], 0.0).then_inc(S("masks"), 1)
                pool.wait_ge(S("masks"), nth("masks"))
                for e in range(2):
                    r = slice(e * DK, (e + 1) * DK)
                    pool.memset(blk64[r, r], 1.0).then_inc(S("masks"), 1)
                    pool.wait_ge(S("masks"), nth("masks"))
                    pool.memset(half[r, e:e + 1], 1.0).then_inc(S("masks"), 1)
                    pool.wait_ge(S("masks"), nth("masks"))
                ln_pool(pool, "ln1")
                pool.wait_ge(S("gk"), 1)
                pool.tensor_tensor(R[:, 0], bc(tri[:], 1, [P, NH, P]), bc(gk[:], 2, [P, NH, P]), ALU.mult).then_inc(S("R"), 1)
                pool.wait_ge(S("R"), nth("R"))
                pool.tensor_tensor(R[:, 1], bc(below[:], 1, [P, NH, P]), bc(gk[:], 2, [P, NH, P]), ALU.mult).then_inc(S("R"), 1)
                pool.wait_ge(S("R"), nth("R"))
                pool.wait_ge(S("dexp"), 6)
                pool.tensor_tensor(Dm[:], Dm[:], bc(below[:], 1, [P, NH, P]), ALU.mult).then_inc(S("Dm"), 1)
                pool.wait_ge(S("Dm"), nth("Dm"))
                pool.tensor_tensor(Dm[:], Dm[:], bc(beta[:], 2, [P, NH, P]), ALU.mult).then_inc(S("Dm"), 1)
                pool.wait_ge(S("Dm"), nth("Dm"))
                pool.tensor_tensor(DT[:], DT[:], bc(tri[:], 1, [P, NH, P]), ALU.mult).then_inc(S("DT"), 1)
                pool.wait_ge(S("DT"), nth("DT"))
                for n in range(1, len(LEVELS)):
                    pool.wait_ge(S("AT"), NG)
                    if some(NG * (n - 2)):
                        pool.wait_ge(S("Zmm"), NG * (n - 2))
                    pool.tensor_tensor(Am[:, n % 2], AT, bc(level[:, n], 1, [P, NH, P]), ALU.mult).then_inc(S("Am"), 1)
                pool.wait_ge(S("ss"), 1)
                pool.tensor_scalar(ss[:], ss[:], 1.0 / DV, LN_EPS, ALU.mult, ALU.add).then_inc(S("rms"), 1)
                pool.wait_ge(S("rms"), nth("rms"))
                pool.tensor_tensor(ss[:], ss[:], mhalf[:], ALU.pow).then_inc(S("rms"), 1)
                pool.wait_ge(S("rms"), nth("rms"))

            @block.vector
            def _(dve):
                dve.tensor_scalar(fl0[:], run0[:, 1], -MASKED / 2, None, ALU.is_gt).then_inc(S("o0step"), 1)
                dve.wait_ge(S("o0step"), nth("o0step"))
                dve.tensor_tensor(rd0[:], acc0[:, :, D0], fl0[:], ALU.mult).then_inc(S("o0step"), 1)
                dve.wait_ge(S("o0step"), nth("o0step"))
                dve.reciprocal(rd0[:], rd0[:]).then_inc(S("o0step"), 1)
                dve.wait_ge(S("o0step"), nth("o0step"))
                o3 = o0[:].rearrange("p (h d) -> p h d", h=H0)
                dve.tensor_tensor(o3, acc0[:, :, 0:D0], bc(fl0[:], 2, [P, H0, D0]), ALU.mult).then_inc(S("o0step"), 1)
                dve.wait_ge(S("o0step"), nth("o0step"))
                dve.tensor_tensor(o3, o3, bc(rd0[:], 2, [P, H0, D0]), ALU.mult).then_inc(S("o0"), 1)
                dve.wait_ge(S("o0"), nth("o0"))
                dve.wait_ge(S("x1_psum"), 1)
                dve.tensor_tensor(xres[:], xres[:], bank[6][:, 0:D], ALU.add).then_inc(S("x1"), 1)
                dve.wait_ge(S("x1"), nth("x1"))
                ln_dve(dve, "ln1")
                dve.wait_ge(S("gates_psum"), 1)
                dve.tensor_tensor(gz[:], bank[7][:, 0:2 * NH], gbias[:], ALU.add).then_inc(S("gstep"), 1)
                dve.wait_ge(S("gstep"), nth("gstep"))
                dve.tensor_scalar(gp[:], gz[:, 0:NH], -1.0, None, ALU.mult).then_inc(S("gstep"), 1)
                dve.wait_ge(S("gstep"), nth("gstep"))
                dve.tensor_tensor(ge[:, 0:NH], gz[:, 0:NH], gp[:], ALU.min).then_inc(S("gstep"), 1)
                dve.wait_ge(S("gstep"), nth("gstep"))
                dve.tensor_scalar(ge[:, NH:], gz[:, NH:], -1.0, None, ALU.mult).then_inc(S("ge_in"), 1)
                dve.wait_ge(S("ge_in"), nth("ge_in"))
                dve.tensor_scalar(gp[:], gz[:, 0:NH], 0.0, None, ALU.max).then_inc(S("gstep"), 1)
                dve.wait_ge(S("gstep"), nth("gstep"))
                dve.wait_ge(S("ge"), 1)
                dve.tensor_scalar(ge[:], ge[:], 1.0, None, ALU.add).then_inc(S("ge1"), 1)
                dve.wait_ge(S("ge1"), nth("ge1"))
                dve.reciprocal(beta[:], ge[:, NH:]).then_inc(S("beta"), 1)
                dve.wait_ge(S("beta"), nth("beta"))
                dve.wait_ge(S("softplus"), 1)
                dve.tensor_tensor(gp[:], gp[:], ge[:, 0:NH], ALU.add).then_inc(S("gstep"), 1)
                dve.wait_ge(S("gstep"), nth("gstep"))
                dve.scalar_tensor_tensor(out=gk[:], in0=gp[:], scalar=-1.0, in1=nA[:], op0=ALU.mult,
                                                   op1=ALU.mult).then_inc(S("gk"), 1)
                dve.wait_ge(S("gk"), nth("gk"))
                for g in range(CB // GH):
                    dve.wait_ge(S("tap"), g + 1)
                    for j in range(TAPS - 1):
                        for b in range(g * GH, (g + 1) * GH):
                            ins = dve.scalar_tensor_tensor(out=cv[:, b], in0=xpad[:, b, j:j + P],
                                                           scalar=convw[:, b, j:j + 1], in1=cv[:, b],
                                                           op0=ALU.mult, op1=ALU.add)
                        ins.then_inc(S("conv" if j == TAPS - 2 else "convstep"), 1)
                        dve.wait_ge(S("conv" if j == TAPS - 2 else "convstep"), nth("conv" if j == TAPS - 2 else "convstep"))
                dve.wait_ge(S("silu"), NG)
                dve.tensor_tensor(sq[:], cv[:, 0:NH], cv[:, 0:NH], ALU.mult).then_inc(S("sq"), 1)
                dve.wait_ge(S("sq"), nth("sq"))
                dve.wait_ge(S("rs"), NG)
                dve.tensor_tensor(cv[:, KB:2 * KB], cv[:, KB:2 * KB], rs[:, KB:], ALU.mult).then_inc(S("kn"), 1)
                dve.wait_ge(S("kn"), nth("kn"))
                kv_ = kz[:].rearrange("p (b e) t -> p b e t", e=2)
                for e in range(2):
                    dve.tensor_scalar(kv_[:, :, e], cv[:, KB:2 * KB], half[:, e:e + 1], None, ALU.mult).then_inc(S("kz"), 1)
                    dve.wait_ge(S("kz"), nth("kz"))
                dve.scalar_tensor_tensor(out=cv[:, 0:KB], in0=cv[:, 0:KB], scalar=DK ** -0.5,
                                                   in1=rs[:, 0:KB], op0=ALU.mult, op1=ALU.mult).then_inc(S("qn"), 1)
                dve.wait_ge(S("qn"), nth("qn"))
                dve.wait_ge(S("Dm"), 2)
                for g in range(NG):
                    dve.wait_ge(S("KK"), g + 1)
                    dve.tensor_tensor(A[:, hb(g)], b4(g), Dm[:, hb(g)], ALU.mult).then_inc(S("A"), 1)
                    dve.wait_ge(S("A"), nth("A"))
                for g in range(NG):
                    dve.wait_ge(S("A"), g + 1)
                    dve.tensor_tensor(X[:, hb(g)], A[:, hb(g)], bc(pair[:], 1, [P, GH, P]), ALU.mult).then_inc(S("XU"), 1)
                    dve.wait_ge(S("XU"), nth("XU"))
                    dve.tensor_tensor(X[:, hb(g)], bc(ident[:], 1, [P, GH, P]), X[:, hb(g)], ALU.subtract).then_inc(S("XU"), 1)
                    dve.wait_ge(S("XU"), nth("XU"))
                    dve.wait_ge(S("AT"), g + 1)
                    dve.tensor_tensor(U[:, hb(g)], AT[:, hb(g)], bc(level[:, 0], 1, [P, GH, P]), ALU.mult).then_inc(S("XU"), 1)
                    dve.wait_ge(S("XU"), nth("XU"))
                    dve.tensor_tensor(U[:, hb(g)], bc(ident[:], 1, [P, GH, P]), U[:, hb(g)], ALU.subtract).then_inc(S("XU"), 1)
                    dve.wait_ge(S("XU"), nth("XU"))
                dve.wait_ge(S("DT"), 1)
                for g in range(NG):
                    dve.wait_ge(S("KQ"), g + 1)
                    dve.tensor_tensor(at[:, hb(g)], b4(5 + g), DT[:, hb(g)], ALU.mult).then_inc(S("at"), 1)
                    dve.wait_ge(S("at"), nth("at"))
                for g in range(NG):
                    dve.wait_ge(S("vT"), g + 1)
                    dve.tensor_tensor(bv[:, hb(g)], b4(5 + g), bc(beta[:, hb(g)], 2, [P, GH, P]), ALU.mult).then_inc(S("bv"), 1)
                    dve.wait_ge(S("bv"), nth("bv"))
                for n in range(1, len(LEVELS) - 1):
                    for g in range(NG):
                        dve.wait_ge(S("XZ"), NG * (n - 1) + g + 1)
                        dve.tensor_tensor(X[:, hb(g)], X[:, hb(g)], b4(3 + g), ALU.subtract).then_inc(S("X"), 1)
                        dve.wait_ge(S("ZU"), NG * (n - 1) + g + 1)
                        dve.tensor_tensor(U[:, hb(g)], U[:, hb(g)], b4(g), ALU.subtract).then_inc(S("U"), 1)
                for g in range(NG):
                    dve.wait_ge(S("dmm"), g + 1)
                    dve.wait_ge(S("w"), g + 1)
                    dve.tensor_tensor(dl[:, hb(g)], w[:, hb(g)], b4(g), ALU.subtract).then_inc(S("dl"), 1)
                    dve.wait_ge(S("dl"), nth("dl"))
                dve.wait_ge(S("oh"), NG)
                dve.wait_ge(S("at_used"), 1)
                dve.tensor_tensor(at[:], oh[:], oh[:], ALU.mult).then_inc(S("ostep"), 1)
                dve.wait_ge(S("ostep"), nth("ostep"))
                dve.tensor_reduce(ss[:], at[:], AX.X, ALU.add).then_inc(S("ss"), 1)
                dve.wait_ge(S("ss"), nth("ss"))
                dve.tensor_tensor(oh[:], oh[:], sg[:], ALU.mult).then_inc(S("ostep"), 1)
                dve.wait_ge(S("ostep"), nth("ostep"))
                dve.tensor_tensor(oh[:], oh[:], bc(gnw[:], 1, [P, NH, DV]), ALU.mult).then_inc(S("ostep"), 1)
                dve.wait_ge(S("ostep"), nth("ostep"))
                dve.wait_ge(S("rms"), 2)
                dve.tensor_tensor(oh[:], oh[:], bc(ss[:], 2, [P, NH, DV]), ALU.mult).then_inc(S("on"), 1)
                dve.wait_ge(S("on"), nth("on"))
                dve.wait_ge(S("x2_psum"), 1)
                dve.tensor_tensor(xres[:], xres[:], bank[6][:, 0:D], ALU.add).then_inc(S("x2"), 1)
                dve.wait_ge(S("x2"), nth("x2"))

            @block.scalar
            def _(act):
                act.wait_ge(S("o0T_psum"), 1)
                act.copy(oT0[:].rearrange("p k t -> p (k t)"), bank[7][:, 0:D]).then_inc(S("o0T"), 1)
                ln_act(act, "ln1", 7)
                act.wait_ge(S("gw_in"), 16 * GW_LOADS)
                act.activation(nA[:], nA[:], ACT.Exp).then_inc(S("nA"), 1)
                act.wait_ge(S("ge_in"), 1)
                act.activation(ge[:], ge[:], ACT.Exp).then_inc(S("ge"), 1)
                act.wait_ge(S("ge1"), 1)
                act.activation(ge[:, 0:NH], ge[:, 0:NH], ACT.Ln).then_inc(S("softplus"), 1)
                act.wait_ge(S("xpad_zero"), 1)
                for g in range(CB // GH):
                    act.wait_ge(S("cproj"), g + 1)
                    act.copy(xpad[:, g * GH:(g + 1) * GH, TAPS - 1:], b4(g))
                    for j in range(GH):
                        b = g * GH + j
                        ins = act.activation(cv[:, b], bank[g][:, j * P:(j + 1) * P], ACT.Copy,
                                             scale=convw[:, b, TAPS - 1:TAPS])
                    ins.then_inc(S("tap"), 1)
                for k, b in enumerate((6, 0, 1)):
                    act.wait_ge(S("gproj"), k + 1)
                    act.activation(sg[:, hb(k)], b4(b), ACT.Silu).then_inc(S("sg"), 1)
                for g in range(CB // GH):
                    act.wait_ge(S("conv"), g + 1)
                    act.activation(cv[:, g * GH:(g + 1) * GH], cv[:, g * GH:(g + 1) * GH], ACT.Silu).then_inc(S("silu"), 1)
                for k, b in enumerate((5, 6, 0, 2, 3, 4)):
                    act.wait_ge(S("dsum"), k + 1)
                    dst = (Dm, DT)[k // NG]
                    act.activation(dst[:, hb(k % NG)], b4(b), ACT.Exp).then_inc(S("dexp"), 1)
                for g in range(NG):
                    act.wait_ge(S("n2"), g + 1)
                    act.activation(rs[:, hb(g)], b4(1 + g), ACT.Ln, bias=eps6[:, 0:1]).then_inc(S("lnn"), 1)
                    act.wait_ge(S("lnn"), g + 1)
                    act.activation(rs[:, hb(g)], rs[:, hb(g)], ACT.Exp, scale=-0.5).then_inc(S("rs"), 1)
                for g in range(NG):
                    act.wait_ge(S("AT_psum"), g + 1)
                    act.copy(AT[:, hb(g)], b4((3, 4, 3)[g])).then_inc(S("AT"), 1)
                for n in range(1, len(LEVELS) - 1):
                    for g in range(NG):
                        act.wait_ge(S("Zmm"), NG * (n - 1) + g + 1)
                        act.copy(Z[:, hb(g)], b4(g)).then_inc(S("Z"), 1)
                for g in range(NG):
                    act.wait_ge(S("wmm"), g + 1)
                    act.copy(w[:, hb(g)], b4(3 + g)).then_inc(S("w"), 1)
                for g in range(NG):
                    act.wait_ge(S("zmm"), g + 1)
                    act.copy(Z[:, hb(g)], b4(g)).then_inc(S("z"), 1)
                for g in range(NG):
                    act.wait_ge(S("omm"), g + 1)
                    act.copy(oh[:, hb(g)], b4(3 + g)).then_inc(S("oh"), 1)
                for g in range(NG):
                    act.wait_ge(S("oT_psum"), g + 1)
                    act.copy(oT[:, hb(g)], b4(g)).then_inc(S("oT"), 1)

            @block.tensor
            def _(pe):
                def heads(g, b, lhs, rhs, name, transpose=False):
                    for j in range(GH):
                        h = g * GH + j
                        o = bank[b][:, j * P:(j + 1) * P]
                        ins = pe.transpose(o, lhs(h), ident[:]) if transpose else \
                            pe.matmul(o, lhs(h), rhs(h), start=True, stop=True)
                    ins.then_inc(S(name), 1)

                pe.wait_ge(S("o0"), 1)
                for k in range(DC):
                    ins = pe.transpose(bank[7][:, k * P:(k + 1) * P], o0[:, k * P:(k + 1) * P], ident[:])
                ins.then_inc(S("o0T_psum"), 1)
                pe.wait_ge(S("o0T"), 1)
                pe.wait_ge(S("wo0_in"), 16)
                for k in range(DC):
                    ins = pe.matmul(bank[6][:, 0:D], oT0[:, k, :], Wo0[:, k, :], start=(k == 0), stop=(k == DC - 1))
                ins.then_inc(S("x1_psum"), 1)
                ln_pe(pe, "ln1", 7)
                pe.wait_ge(S("ln1_hT"), 1)
                pe.wait_ge(S("gw_in"), 16 * GW_LOADS)
                for k in range(DC):
                    ins = pe.matmul(bank[7][:, 0:2 * NH], hT[:, k, :], Wgb[:, k, :], start=(k == 0), stop=(k == DC - 1))
                ins.then_inc(S("gates_psum"), 1)
                for g in range(CB // GH):
                    for j in range(GH):
                        b = g * GH + j
                        for k in range(DC):
                            ins = pe.matmul(bank[g][:, j * P:(j + 1) * P], Wc[:, k, b * P:(b + 1) * P], hT[:, k, :],
                                            start=(k == 0), stop=(k == DC - 1))
                    ins.then_inc(S("cproj"), 1)
                for g, b in enumerate((6, 0, 1)):
                    if b != 6:
                        pe.wait_ge(S("tap"), b + 1)
                    for k in range(DC):
                        ins = pe.matmul(bank[b][:], hT[:, k, :], Wg[:, k, g * 512:(g + 1) * 512],
                                        start=(k == 0), stop=(k == DC - 1))
                    ins.then_inc(S("gproj"), 1)
                pe.wait_ge(S("R"), 2)
                pe.wait_ge(S("tap"), CB // GH)
                pe.wait_ge(S("sg"), 2)
                for g, b in enumerate((5, 6, 0)):
                    pe.matmul(bank[b][:], tri[:], R[:, 1, hb(g)].rearrange("p h t -> p (h t)"), start=True,
                              stop=True).then_inc(S("dsum"), 1)
                for g, b in enumerate((2, 3, 4)):
                    pe.matmul(bank[b][:], below[:], R[:, 0, hb(g)].rearrange("p h t -> p (h t)"), start=True,
                              stop=True).then_inc(S("dsum"), 1)
                pe.wait_ge(S("sq"), 1)
                pe.wait_ge(S("dexp"), 6)
                pe.wait_ge(S("sg"), 3)
                for g in range(NG):
                    pe.matmul(bank[1 + g][:], blk64[:], sq[:, hb(g)].rearrange("p h t -> p (h t)"), start=True,
                              stop=True).then_inc(S("n2"), 1)
                pe.wait_ge(S("kz"), 2)
                kn = lambda h: cv[:, KB + h // 2]
                for g in range(NG):
                    if some(g):
                        pe.wait_ge(S("rs"), g)
                    heads(g, g, lambda h: kz[:, h], kn, "KK")
                for g in range(NG):
                    pe.wait_ge(S("A"), g + 1)
                    if some(g - 1):
                        pe.wait_ge(S("AT"), g - 1)
                    heads(g, (3, 4, 3)[g], lambda h: A[:, h], None, "AT_psum", True)
                pe.wait_ge(S("qn"), 1)
                for g in range(NG):
                    heads(g, 5 + g, lambda h: kz[:, h], lambda h: cv[:, h // 2], "KQ")
                pe.wait_ge(S("silu"), CB // GH)
                for g in range(NG):
                    pe.wait_ge(S("at"), g + 1)
                    heads(g, 5 + g, lambda h: cv[:, 2 * KB + h], None, "vT", True)
                pe.wait_ge(S("AT"), NG)
                for n in range(1, len(LEVELS) - 1):
                    pe.wait_ge(S("Am"), n)
                    for g in range(NG):
                        pe.wait_ge(S("XU"), 4 * (g + 1))
                        if some(NG * (n - 2) + g + 1):
                            pe.wait_ge(S("X"), NG * (n - 2) + g + 1)
                        if some(NG * (n - 2) + g + 1):
                            pe.wait_ge(S("U"), NG * (n - 2) + g + 1)
                        heads(g, g, lambda h: Am[:, n % 2, h], lambda h: X[:, h], "Zmm")
                    for g in range(NG):
                        pe.wait_ge(S("Z"), NG * (n - 1) + g + 1)
                        pe.wait_ge(S("bv"), 1)
                        heads(g, 3 + g, lambda h: U[:, h], lambda h: Z[:, h], "XZ")
                        heads(g, g, lambda h: Z[:, h], lambda h: U[:, h], "ZU")
                nl = len(LEVELS) - 2
                for g in range(NG):
                    pe.wait_ge(S("U"), NG * (nl - 1) + g + 1)
                    pe.wait_ge(S("X"), NG * (nl - 1) + g + 1)
                    pe.wait_ge(S("bv"), g + 1)
                    heads(g, 3 + g, lambda h: U[:, h], lambda h: bv[:, h], "wmm")
                pe.wait_ge(S("Am"), nl + 1)
                for g in range(NG):
                    pe.wait_ge(S("w"), g + 1)
                    heads(g, g, lambda h: Am[:, (nl + 1) % 2, h], lambda h: w[:, h], "zmm")
                for g in range(NG):
                    pe.wait_ge(S("z"), g + 1)
                    heads(g, g, lambda h: U[:, h], lambda h: Z[:, h], "dmm")
                for g in range(NG):
                    pe.wait_ge(S("dl"), g + 1)
                    heads(g, 3 + g, lambda h: at[:, h], lambda h: dl[:, h], "omm")
                pe.sem_inc(S("at_used"), 1)
                pe.wait_ge(S("on"), 1)
                for g in range(NG):
                    heads(g, g, lambda h: oh[:, h], None, "oT_psum", True)
                for g in range(NG):
                    pe.wait_ge(S("oT"), g + 1)
                    for h in range(g * GH, (g + 1) * GH):
                        ins = pe.matmul(bank[6][:, 0:D], oT[:, h], Wo[:, h], start=(h == 0), stop=(h == NH - 1))
                ins.then_inc(S("x2_psum"), 1)
        gd.close()
        xa.close()
        gw.close()

        def experts(tag, ew, router, router_rows, router_bias, expert_bias, top, last):
            mo = ExitStack()
            eT = sb(mo, "eT" + tag, [P, DC, E, D])
            rwT = sb(mo, "rwT" + tag, [P, DC, E])
            rw = sb(mo, "rw" + tag, [E, D])
            rb = sb(mo, "rb" + tag, [P, E])
            eb = sb(mo, "eb" + tag, [E, D])
            order = sb(mo, "order" + tag, [P, E])
            lg = sb(mo, "lg" + tag, [P, E])
            lx = sb(mo, "lx" + tag, [P, E])
            best = sb(mo, "best" + tag, [P, 1])
            pick = sb(mo, "pick" + tag, [P, E])
            eq = sb(mo, "eq" + tag, [P, E])
            chosen = sb(mo, "chosen" + tag, [P, E])
            ex = sb(mo, "ex" + tag, [P, E])
            total = sb(mo, "total" + tag, [P, 1])
            wt = sb(mo, "wt" + tag, [P, E])
            wtT = sb(mo, "wtT" + tag, [E, P])
            n = lambda name: tag + name

            def product(pe, g):
                pe.wait_ge(S(n("eT")), 2 * g + 2)
                b = (5, 6, 7, 0)[g]
                for k in range(DC):
                    ins = pe.matmul(bank[b][:], hT[:, k, :], eT[:, k, 2 * g:2 * g + 2].rearrange("p e o -> p (e o)"),
                                    start=(k == 0), stop=(k == DC - 1))
                ins.then_inc(S(n("y")), 1)

            with nc.Block() as block:
                @block.sync
                def _(sp):
                    if router_rows:
                        sp.dma_start(rw[:], router).then_inc(S(n("rw_in")), 16)
                    else:
                        sp.dma_start(rwT[:], wcols(router)).then_inc(S(n("rw_in")), 16)
                    sp.dma_start(rb[:], router_bias.partition_broadcast(P)).then_inc(S(n("rb_in")), 16)
                    sp.dma_start(eb[:], expert_bias).then_inc(S(n("eb_in")), 16)
                    if last:
                        sp.wait_ge(S(n("x")), 1)
                        sp.dma_start(out.rearrange("b q d -> (b q) d"), xres[:]).then_inc(S("out"), 16)
                        sp.wait_ge(S("out"), 16)

                @block.gpsimd
                def _(pool):
                    for e in range(E):
                        pool.memset(order[:, e:e + 1], float(E - e)).then_inc(S(n("order")), 1)
                    ln_pool(pool, n("ln"))

                @block.tensor
                def _(pe):
                    ln_pe(pe, n("ln"), 0)
                    pe.wait_ge(S(n("rw_in")), 16)
                    if router_rows:
                        for k in range(DC):
                            ins = pe.transpose(bank[1][:, k * E:(k + 1) * E], rw[:, k * P:(k + 1) * P], ident[0:E, 0:E])
                        ins.then_inc(S(n("rwT_psum")), 1)
                        pe.wait_ge(S(n("rwT")), 1)
                    pe.wait_ge(S(n("ln_hT")), 1)
                    for k in range(DC):
                        ins = pe.matmul(bank[2][:, 0:E], hT[:, k, :], rwT[:, k, :], start=(k == 0), stop=(k == DC - 1))
                    ins.then_inc(S(n("logits_psum")), 1)
                    pe.wait_ge(S(tag + "ew_in" if last else "ew0_in"), 16)
                    for i in range(E):
                        if i >= 2:
                            if some(i - 1):
                                pe.wait_ge(S(n("eT")), i - 1)
                        for k in range(DC):
                            for c in range(DC):
                                ins = pe.transpose(bank[3 + i % 2][:, (k * DC + c) * P:(k * DC + c + 1) * P],
                                                   ew[:, i * DC + c, k * P:(k + 1) * P], ident[:])
                        ins.then_inc(S(n("eT_psum")), 1)
                        if i >= 2 and i % 2:
                            product(pe, i // 2 - 1)
                    product(pe, E // 2 - 1)
                    pe.wait_ge(S(n("wt")), 1)
                    pe.transpose(bank[1][0:E, 0:P], wt[:], ident[:]).then_inc(S(n("wtT_psum")), 1)
                    pe.wait_ge(S(n("wtT")), 1)
                    pe.wait_ge(S(n("eb_in")), 16)
                    pe.matmul(bank[2][:, 0:D], wtT[:], eb[:], start=True, stop=True).then_inc(S(n("bias_psum")), 1)

                @block.scalar
                def _(act):
                    if router_rows:
                        act.wait_ge(S(n("rwT_psum")), 1)
                        act.copy(rwT[:].rearrange("p k e -> p (k e)"), bank[1][:, 0:DC * E]).then_inc(S(n("rwT")), 1)
                    ln_act(act, n("ln"), 0)
                    for i in range(E):
                        act.wait_ge(S(n("eT_psum")), i + 1)
                        act.copy(eT[:, :, i, :], bank[3 + i % 2][:].rearrange("p (k o) -> p k o", k=DC)
                                 ).then_inc(S(n("eT")), 1)
                        if i == 2:
                            act.wait_ge(S(n("shifted")), 1)
                            act.activation(ex[:], lx[:], ACT.Exp).then_inc(S(n("ex")), 1)
                    act.wait_ge(S(n("wtT_psum")), 1)
                    act.copy(wtT[:], bank[1][0:E, 0:P]).then_inc(S(n("wtT")), 1)

                @block.vector
                def _(dve):
                    ln_dve(dve, n("ln"))
                    dve.wait_ge(S(n("rb_in")), 16)
                    dve.wait_ge(S(n("logits_psum")), 1)
                    dve.tensor_tensor(lg[:], bank[2][:, 0:E], rb[:], ALU.add).then_inc(S(n("step")), 1)
                    dve.wait_ge(S(n("step")), nth(n("step")))
                    dve.tensor_reduce(best[:], lg[:], AX.X, ALU.max).then_inc(S(n("step")), 1)
                    dve.wait_ge(S(n("step")), nth(n("step")))
                    dve.tensor_scalar(lx[:], lg[:], best[:, 0:1], None, ALU.subtract).then_inc(S(n("shifted")), 1)
                    dve.wait_ge(S(n("shifted")), nth(n("shifted")))
                    dve.wait_ge(S(n("order")), E)
                    for r in range(top):
                        if r:
                            dve.scalar_tensor_tensor(out=lg[:], in0=pick[:], scalar=LOWEST, in1=lg[:], op0=ALU.mult,
                                                         op1=ALU.add).then_inc(S(n("step")), 1)
                            dve.wait_ge(S(n("step")), nth(n("step")))
                            dve.tensor_reduce(best[:], lg[:], AX.X, ALU.max).then_inc(S(n("step")), 1)
                            dve.wait_ge(S(n("step")), nth(n("step")))
                        dve.tensor_scalar(eq[:], lg[:], best[:, 0:1], None, ALU.is_ge).then_inc(S(n("step")), 1)
                        dve.wait_ge(S(n("step")), nth(n("step")))
                        dve.tensor_tensor(eq[:], eq[:], order[:], ALU.mult).then_inc(S(n("step")), 1)
                        dve.wait_ge(S(n("step")), nth(n("step")))
                        dve.tensor_reduce(best[:], eq[:], AX.X, ALU.max).then_inc(S(n("step")), 1)
                        dve.wait_ge(S(n("step")), nth(n("step")))
                        dve.tensor_scalar(pick[:], eq[:], best[:, 0:1], None, ALU.is_ge).then_inc(S(n("step")), 1)
                        dve.wait_ge(S(n("step")), nth(n("step")))
                        if r:
                            dve.tensor_tensor(chosen[:], chosen[:], pick[:], ALU.add).then_inc(S(n("step")), 1)
                            dve.wait_ge(S(n("step")), nth(n("step")))
                        else:
                            dve.tensor_copy(chosen[:], pick[:]).then_inc(S(n("step")), 1)
                            dve.wait_ge(S(n("step")), nth(n("step")))
                    dve.wait_ge(S(n("ex")), 1)
                    dve.tensor_tensor(wt[:], ex[:], chosen[:], ALU.mult).then_inc(S(n("step")), 1)
                    dve.wait_ge(S(n("step")), nth(n("step")))
                    dve.tensor_reduce(total[:], ex[:] if top == 1 else wt[:], AX.X, ALU.add).then_inc(S(n("step")), 1)
                    dve.wait_ge(S(n("step")), nth(n("step")))
                    dve.reciprocal(total[:], total[:]).then_inc(S(n("step")), 1)
                    dve.wait_ge(S(n("step")), nth(n("step")))
                    dve.tensor_scalar(wt[:], wt[:], total[:, 0:1], None, ALU.mult).then_inc(S(n("wt")), 1)
                    dve.wait_ge(S(n("wt")), nth(n("wt")))
                    for e in range(E):
                        dve.wait_ge(S(n("y")), e // 2 + 1)
                        dve.scalar_tensor_tensor(out=xres[:], in0=bank[(5, 6, 7, 0)[e // 2]][:, (e % 2) * D:(e % 2 + 1) * D],
                                                     scalar=wt[:, e:e + 1], in1=xres[:], op0=ALU.mult, op1=ALU.add).then_inc(S(n("step")), 1)
                        dve.wait_ge(S(n("step")), nth(n("step")))
                    dve.wait_ge(S(n("bias_psum")), 1)
                    dve.tensor_tensor(xres[:], xres[:], bank[2][:, 0:D], ALU.add).then_inc(S(n("x")), 1)
                    dve.wait_ge(S(n("x")), nth(n("x")))
            mo.close()

        renew(("ew0_in",))
        experts("moe0", ew0, a["L0_ffn_router_w"], True, a["L0_ffn_router_b"], a["L0_ffn_expert_b"], 1, False)
        er.close()

        fw = ExitStack()
        ew1 = sb(fw, "ew1", [P, E * DC, D])
        lw = ExitStack()
        lraw = sb(lw, "lraw", [P, 10, D])
        xb = ExitStack()
        acc1 = sb(xb, "acc1", [P, H1, D1 + 1])
        bv1 = sb(xb, "bv1", [P, D])
        rd1 = sb(xb, "rd1", [P, H1])
        o1 = sb(xb, "o1", [P, D])
        l1 = ExitStack()
        VW = H1 * (D1 + 1) + D1 - 1
        qrows = sb(l1, "qrows", [KONES, 2, H1, P], BF16)
        krows = sb(l1, "krows", [KONES, 2, H1, CH], BF16)
        v1 = sb(l1, "v1", [P, 2, CT, VW])
        WT1 = sb(l1, "WT1", [P, 3, DC, D])
        b1 = sb(l1, "b1", [P, 2, DC])
        ctx1 = sb(l1, "ctx1", [P, 2, CT, D])
        ctxT1 = sb(l1, "ctxT1", [P, 2, DC, CH])
        kf = sb(l1, "kf", [P, 2, HCH])
        kt3 = sb(l1, "kt3", [P, 3, DC, CH], BF16)
        mx1 = sb(l1, "mx1", [P, H1, 2])
        top1 = sb(l1, "top1", [P, H1])
        run1 = sb(l1, "run1", [P, 2, H1])
        dm1 = sb(l1, "dm1", [P, 2, H1])
        f1 = sb(l1, "f1", [P, 2, H1])
        HP = 32
        neg1 = sb(l1, "neg1", [P, H1])
        n31 = sb(l1, "n31", [P, 3, HP], BF16)
        n3T1 = sb(l1, "n3T1", [3 * HP, 2, P], BF16)
        p1 = sb(l1, "p1", [P, 4, GH * P])
        ots1 = sb(l1, "ots1", [P, GH * P])
        kscr = nc.dram_tensor("kscr", (2, 3, D, CH), BF16).ap()
        qscr = nc.dram_tensor("qscr", (3, D, P), BF16).ap()

        raw = ExitStack()
        raw1 = sb(raw, "raw1", [P, 3, DC, D])
        qf = sb(raw, "qf", [P, DC, P])
        q3 = sb(raw, "q3", [P, 3, DC, P], BF16)

        with nc.Block() as block:
            @block.sync
            def _(sp):
                for k, name in enumerate(("L1_xattn_Wq", "L1_xattn_Wk", "L1_xattn_Wv")):
                    sp.dma_start(raw1[:, k], wcols(a[name])).then_inc(S("raw1_in"), 16)
                for k, name in enumerate(("L1_xattn_bq", "L1_xattn_bk")):
                    sp.dma_start(b1[:, k, :], a[name].rearrange("(c p) -> p c", c=DC),
                                 allow_slow_non_contiguous=True).then_inc(S("b1_in"), 16)
                sp.dma_start(bv1[:], a["L1_xattn_bv"].partition_broadcast(P)).then_inc(S("bv1_in"), 16)
                sp.dma_start(krows[KROWS:KONES].rearrange("p s h (r c) -> p (s h r) c", c=P),
                             onesb[KROWS:KONES].unsqueeze(1).to_broadcast([3, 2 * H1 * CT, P])
                             ).then_inc(S("krows_ones"), 16)
                sp.wait_ge(S("q3"), 3)
                sp.dma_start(qscr.rearrange("k (b p) q -> p (k b) q", b=DC),
                             q3[:].rearrange("p k b q -> p (k b) q")).then_inc(S("qscr"), 16)
                sp.wait_ge(S("qscr"), 16)
                for s in range(2):
                    for j in range(NJ):
                        sp.dma_start(qrows[j * D1:(j + 1) * D1, s],
                                     qscr[Q_TERM[j]].rearrange("(h d) q -> d h q", d=D1)).then_inc(S("qrows_in"), 16)

            @block.gpsimd
            def _(pool):
                ln_pool(pool, "ln2")
                v = v1[:].rearrange("p s t w -> p (s t) w")
                pool.memset(v[:, :, 0:H1 * (D1 + 1)].rearrange("p t (h d) -> p t h d", h=H1)[:, :, :, D1],
                            1.0).then_inc(S("v1_ones"), 1)
                pool.memset(v[:, :, H1 * (D1 + 1):], 0.0).then_inc(S("v1_ones"), 1)
                pool.memset(n31[:], 0.0).then_inc(S("n31_zero"), 1)
                pool.memset(acc1[:], 0.0).then_inc(S("acc1_zero"), 1)
                pool.memset(run1[:], LOWEST).then_inc(S("run1_lowest"), 1)

            @block.tensor
            def _(pe):
                ln_pe(pe, "ln2", 0)
                pe.wait_ge(S("raw1_in"), 48)
                for w_ in range(3):
                    for k in range(DC):
                        for c in range(DC):
                            ins = pe.transpose(bank[1 + w_][:, (k * DC + c) * P:(k * DC + c + 1) * P],
                                               raw1[:, w_, c, k * P:(k + 1) * P], ident[:])
                    ins.then_inc(S("WT1_psum"), 1)
                pe.wait_ge(S("WT1"), 1)
                pe.wait_ge(S("ln2_hT"), 1)
                for b in range(DC):
                    for k in range(DC):
                        ins = pe.matmul(bank[4][:, b * P:(b + 1) * P], WT1[:, 0, k, b * P:(b + 1) * P], hT[:, k, :],
                                        start=(k == 0), stop=(k == DC - 1))
                ins.then_inc(S("q1_psum"), 1)

            @block.scalar
            def _(act):
                ln_act(act, "ln2", 0)
                for w_ in range(3):
                    act.wait_ge(S("WT1_psum"), w_ + 1)
                    act.copy(WT1[:, w_].rearrange("p k o -> p (k o)"), bank[1 + w_][:]).then_inc(S("WT1"), 1)

            @block.vector
            def _(dve):
                ln_dve(dve, "ln2")
                dve.wait_ge(S("b1_in"), 32)
                dve.wait_ge(S("q1_psum"), 1)
                for b in range(DC):
                    dve.tensor_scalar(qf[:, b], bank[4][:, b * P:(b + 1) * P], b1[:, 0, b:b + 1], S1,
                                                ALU.add, ALU.mult).then_inc(S("qf"), 1)
                    dve.wait_ge(S("qf"), nth("qf"))
                dve.tensor_copy(q3[:, 0], qf[:]).then_inc(S("q3"), 1)
                dve.wait_ge(S("q3"), nth("q3"))
                dve.tensor_tensor(qf[:], qf[:], q3[:, 0], ALU.subtract).then_inc(S("qf"), 1)
                dve.wait_ge(S("qf"), nth("qf"))
                dve.tensor_copy(q3[:, 1], qf[:]).then_inc(S("q3"), 1)
                dve.wait_ge(S("q3"), nth("q3"))
                dve.tensor_tensor(q3[:, 2], qf[:], q3[:, 1], ALU.subtract).then_inc(S("q3"), 1)
                dve.wait_ge(S("q3"), nth("q3"))
        raw.close()

        XP1, KV1, SM1, ST1, OT1, OB1 = 0, 1, (2, 3, 0), (4, 5), 6, 7
        UNITS = CT * H1 // GH
        PLAN1 = (
            (("T0",), ("V0",)), (("T1",), ()), (("T2",), ("V1",)), (("T3",), ()), (("S0",), ("S1",)),
            (("S2", "K0", "S3"), ("S4",)), (("S5",), ("S6",)), (("S7",), ("S8",)), (("S9", "K1", "S10"), ("S11",)),
            (("S12",), ("S13",)), (("S14",), ("S15",)), (("S16", "K2", "S17"), ("S18",)), (("S19",), ("S20",)),
            (("S21",), ("S22",)), (("S23", "K3", "S24"), ("S25",)), (("S26",), ("S27",)), (("S28",), ("S29",)),
            (("S30",), ("S31",)), ((), ()), ((), ()), ((), ()), (("V2",), ()), ((), ()), (("M0",), ()), (("V3",), ()),
            ((), ()), ((), ()), ((), ()))

        def early(op):
            return op[0] in "TK"

        ALL1 = tuple(op for before, after in PLAN1 for op in before + after)

        def steps1(eng, step):
            step(0, 0, 0, True, True)
            with eng.Fori(0, (NCH - 4) // 2) as i:
                step(i * 2 + 1, 1, i, True, True)
                step(i * 2 + 2, 0, i + 1, True, True)
            step(NCH - 3, 1, (NCH - 4) // 2, True, True)
            step(NCH - 2, 0, (NCH - 2) // 2, False, True)
            step(NCH - 1, 1, (NCH - 2) // 2, False, False)

        def sides(side, ops, c, s, n, two, one):
            for op in ops:
                if early(op):
                    if two:
                        side(op, c + 2, s, n + 1)
                elif one:
                    side(op, c + 1, 1 - s, n + s)

        with nc.Block() as block:
            @block.sync
            def _(sp):
                def load(c, s):
                    if some(4 * (c - 1)):
                        sp.wait_ge(S("xp1"), 4 * (c - 1))
                    sp.dma_start(ctx1[:, s], chunk_of(c)).then_inc(S(f"ctx1_{s}"), 16)

                def store(c, s, n):
                    sp.wait_ge(S("k31"), 4 * (c + 1))
                    sp.dma_start(kscr[s].rearrange("k (b p) m -> p (k b) m", b=DC),
                                 kt3[:].rearrange("p k b m -> p (k b) m")).then_inc(S(f"kscr_{s}"), 16)

                def gather(c, s, n):
                    used = UNITS * (c - 1)
                    stored = 16 * (n + 1)
                    if not isinstance(used, int):
                        used, stored = sp.snap(used), sp.snap(stored)
                    sp.wait_ge(S(f"kscr_{s}"), stored)
                    if some(used):
                        sp.wait_ge(S("st1"), used)
                    for j in range(NJ):
                        sp.dma_start(krows[j * D1:(j + 1) * D1, s],
                                     kscr[s, K_TERM[j]].rearrange("(h d) m -> d h m", d=D1)
                                     ).then_inc(S(f"krows_{s}"), 16)

                def rows(c, s):
                    sp.wait_ge(S("n3T1"), c + 1)
                    for k in range(3):
                        sp.dma_start(qrows[KROWS + k:KROWS + k + 1, s],
                                     n3T1[k * HP:k * HP + H1, s, :]).then_inc(S(f"mrow1_{s}"), 16)

                load(0, 0)
                load(1, 1)
                sp.dma_start(ew1[:], a["L1_ffn_We"].rearrange("e (c p) d -> p (e c) d", p=P)).then_inc(S("moe1ew_in"), 16)
                for k, name in enumerate(("L1_attn_Wqkv", "L1_attn_Wout", "L1_attn_Wgate")):
                    o = (0, 6, 8, 10)
                    sp.dma_start(lraw[:, o[k]:o[k + 1]], wcols(a[name], o[k + 1] - o[k])).then_inc(S("lraw_in"), 16)
                store(0, 0, 0)
                gather(0, 0, 0)
                load(2, 0)
                store(1, 1, 0)
                gather(1, 1, 0)
                rows(0, 0)

                def step(c, s, n, two, one):
                    if one and not (isinstance(c, int) and c == 0):
                        gather(c + 1, 1 - s, n + s)
                    if two and not (isinstance(c, int) and c == NCH - 3):
                        load(c + 3, 1 - s)
                    if two:
                        store(c + 2, s, n + 1)
                    if one:
                        rows(c + 1, 1 - s)
                steps1(sp, step)

            @block.gpsimd
            def _(pool):
                def parts(c):
                    for k in range(4):
                        half, b = k // 2, k % 2
                        cols = slice(half * HCH, (half + 1) * HCH)
                        pool.wait_ge(S("kread1"), 4 * c + k + 1)
                        pool.tensor_tensor(kt3[:, 1, b, cols], kf[:, k % 2, :], kt3[:, 0, b, cols],
                                           ALU.subtract).then_inc(S("k21"), 1)
                        pool.wait_ge(S("k21"), 4 * c + k + 1)
                        pool.tensor_tensor(kf[:, k % 2, :], kf[:, k % 2, :], kt3[:, 0, b, cols],
                                           ALU.subtract).then_inc(S("kr1"), 1)
                        pool.wait_ge(S("kr1"), 4 * c + k + 1)
                        pool.tensor_tensor(kt3[:, 2, b, cols], kf[:, k % 2, :], kt3[:, 1, b, cols],
                                           ALU.subtract).then_inc(S("k31"), 1)
                with pool.Fori(0, NCH) as c:
                    parts(c)

            @block.tensor
            def _(pe):
                def side(op, c, s, n):
                    k = int(op[1:])
                    if op[0] == "T":
                        if k == 0:
                            pe.wait_ge(S(f"ctx1_{s}"), 16 * n + 16)
                            if some(c - 1):
                                pe.wait_ge(S("n3T1"), c - 1)
                        if some(4 * c + k):
                            pe.wait_ge(S("ctxT1"), 4 * c + k)
                        h, t0, nt = TG[k]
                        for t in range(nt):
                            ins = pe.transpose(bank[XP1][:, t * P:(t + 1) * P], ctx1[:, s, t0 + t, h * P:(h + 1) * P],
                                               ident[:])
                        ins.then_inc(S("xp1"), 1)
                    elif op[0] == "K":
                        half, b = k // 2, k % 2
                        pe.wait_ge(S("ctxT1"), 4 * c + 2 * half + 2)
                        if k == 0 and not (isinstance(c, int) and c < 2):
                            pe.wait_ge(S("vread1"), 4 * (c - 1) + 2)
                        elif some(4 * c + k):
                            pe.wait_ge(S("kread1"), 4 * c + k)
                        for i in range(DC):
                            ins = pe.matmul(bank[KV1][:, 0:HCH], WT1[:, 1, i, b * P:(b + 1) * P],
                                            ctxT1[:, s, i, half * HCH:(half + 1) * HCH],
                                            start=(i == 0), stop=(i == DC - 1))
                        ins.then_inc(S("kmm1"), 1)
                    elif op[0] == "S":
                        h, half = k // 2, k % 2
                        if k == 0:
                            pe.wait_ge(S(f"krows_{s}"), 16 * NJ * (n + 1))
                        if k == 2:
                            pe.wait_ge(S("ctxT1"), min(4 * (c + 2), 4 * NCH) if isinstance(c, int) else 4 * (c + 2))
                        elif some(2 * H1 * c + max(k - 2, 0)):
                            pe.wait_ge(S("smread1"), 2 * H1 * c + max(k - 2, 0))
                        pe.matmul(bank[SM1[k % 3]][:, 0:HCH], qrows[0:KROWS, s, h, :],
                                  krows[0:KROWS, s, h, half * HCH:(half + 1) * HCH],
                                  start=True, stop=True).then_inc(S("sm1"), 1)
                    elif op[0] == "V":
                        t0, nt = VG[k]
                        if k == 2 or isinstance(c, int) and c == 0:
                            pe.wait_ge(S("kread1"), min(4 * (c + 2), 4 * NCH) if isinstance(c, int) else 4 * (c + 2))
                        if some(4 * c + k):
                            pe.wait_ge(S("vread1"), 4 * c + k)
                        for t in range(nt):
                            for i in range(DC):
                                ins = pe.matmul(bank[KV1][:, t * D:(t + 1) * D],
                                                ctxT1[:, s, i, (t0 + t) * P:(t0 + t + 1) * P], WT1[:, 2, i, :],
                                                start=(i == 0), stop=(i == DC - 1))
                        ins.then_inc(S("vmm1"), 1)
                    else:
                        pe.wait_ge(S("n31"), c + 1)
                        pe.wait_ge(S("ctxT1"), min(4 * (c + 2), 4 * NCH) if isinstance(c, int) else 4 * (c + 2))
                        pe.transpose(bankb[XP1][0:3 * HP, 0:P], n31[:].rearrange("p k h -> p (k h)"),
                                     identb[:]).then_inc(S("mt1"), 1)

                def scores(c, s, n, u):
                    t, j = u // 4, u % 4
                    if u == 0:
                        pe.wait_ge(S(f"mrow1_{s}"), 48 * n + 48)
                    if some(UNITS * c + u - 1):
                        pe.wait_ge(S("exp1"), UNITS * c + u - 1)
                    for i in range(GH):
                        h = GH * j + i
                        ins = pe.matmul(bank[ST1[u % 2]][:, i * P:(i + 1) * P], krows[:, s, h, t * P:(t + 1) * P],
                                        qrows[:, s, h, :], start=True, stop=True)
                    ins.then_inc(S("st1"), 1)

                def values(c, s, u):
                    t, j = u // 4, u % 4
                    pe.wait_ge(S("exp1"), UNITS * c + u + 1)
                    if u == 0:
                        if some(c):
                            pe.wait_ge(S("ots1"), c)
                    if u % 8 == 0:
                        pe.wait_ge(S("vread1"), 4 * c + u // 8 + 1)
                    for i in range(GH):
                        h = GH * j + i
                        ins = pe.matmul(bank[OT1][32 * i:32 * i + 32, j * P:(j + 1) * P],
                                        v1[:, s, t, h * (D1 + 1):h * (D1 + 1) + 32],
                                        p1[:, u % 4, i * P:(i + 1) * P],
                                        start=(u == 0), stop=(t == CT - 1), skip_group_check=True)
                    ins.then_inc(S("pv1"), 1)

                def turn(c):
                    pe.wait_ge(S("ots1"), c + 1)
                    if some(2 * c):
                        pe.wait_ge(S("acc1"), 2 * c)
                    for j in range(4):
                        ins = pe.transpose(bank[OB1][:, j * P:(j + 1) * P], ots1[:, j * P:(j + 1) * P], ident[:])
                    ins.then_inc(S("ob1"), 1)

                pe.wait_ge(S("qrows_in"), 16 * 2 * NJ)
                pe.wait_ge(S("krows_ones"), 16)
                for c in range(2):
                    for op in ALL1:
                        if early(op):
                            side(op, c, c, 0)
                for op in ALL1:
                    if not early(op):
                        side(op, 0, 0, 0)

                def step(c, s, n, two, one):
                    scores(c, s, n, 0)
                    if not (isinstance(c, int) and c == 0):
                        turn(c - 1)
                    for u in range(UNITS):
                        if u + 1 < UNITS:
                            scores(c, s, n, u + 1)
                        sides(side, PLAN1[u][0], c, s, n, two, one)
                        values(c, s, u)
                        sides(side, PLAN1[u][1], c, s, n, two, one)
                steps1(pe, step)
                turn(NCH - 1)

            @block.vector
            def _(dve):
                def side(op, c, s, n):
                    k = int(op[1:])
                    if op[0] == "S":
                        h, half = k // 2, k % 2
                        dve.wait_ge(S("sm1"), 2 * H1 * c + k + 1)
                        dve.tensor_reduce(mx1[:, h, half:half + 1], bank[SM1[k % 3]][:, 0:HCH], AX.X,
                                          ALU.max).then_inc(S("smread1"), 1)
                    elif op[0] == "M":
                        maximum(dve, "1", c, s, mx1, top1, run1, dm1, neg1, n31[:, :, 0:H1], 2 * H1)

                def rescale(c, s):
                    dve.wait_ge(S("f1"), c + 1)
                    dve.tensor_tensor(acc1[:], acc1[:], bc(f1[:, s, :], 2, [P, H1, D1 + 1]), ALU.mult).then_inc(S("acc1"), 1)
                    dve.wait_ge(S("acc1"), 2 * c + 1)
                    dve.wait_ge(S("ob1"), c + 1)
                    dve.tensor_tensor(acc1[:], acc1[:],
                                      bank[OB1][:].rearrange("p (h d) -> p h d", h=H1)[:, :, 0:D1 + 1],
                                      ALU.add).then_inc(S("acc1"), 1)
                    dve.wait_ge(S("acc1"), 2 * c + 2)

                for c in range(2):
                    for op in ALL1:
                        if early(op):
                            side(op, c, c, 0)
                for op in ALL1:
                    if not early(op):
                        side(op, 0, 0, 0)

                def step(c, s, n, two, one):
                    if not (isinstance(c, int) and c == 0):
                        rescale(c - 1, 1 - s)
                    sides(side, ALL1, c, s, n, two, one)
                steps1(dve, step)
                rescale(NCH - 1, 1)

            @block.scalar
            def _(act):
                def side(op, c, s, n):
                    k = int(op[1:])
                    if op[0] == "T":
                        h, t0, nt = TG[k]
                        act.wait_ge(S("xp1"), 4 * c + k + 1)
                        if some(4 * (c - 1)):
                            act.wait_ge(S("vmm1"), 4 * (c - 1))
                        act.copy(ctxT1[:, s, h, t0 * P:(t0 + nt) * P], bank[XP1][:, 0:nt * P]).then_inc(S("ctxT1"), 1)
                    elif op[0] == "K":
                        half, b = k // 2, k % 2
                        cols = slice(half * HCH, (half + 1) * HCH)
                        act.wait_ge(S("kmm1"), 4 * c + k + 1)
                        if some(4 * c + k - 1):
                            act.wait_ge(S("k31"), 4 * c + k - 1)
                        if some(16 * (n + s)):
                            act.wait_ge(S(f"kscr_{1 - s}"), 16 * (n + s))
                        act.activation(kf[:, k % 2, :], bank[KV1][:, 0:HCH], ACT.Identity, bias=b1[:, 1, b:b + 1])
                        act.activation(kt3[:, 0, b, cols], bank[KV1][:, 0:HCH], ACT.Identity,
                                       bias=b1[:, 1, b:b + 1]).then_inc(S("kread1"), 1)
                    elif op[0] == "V":
                        t0, nt = VG[k]
                        act.wait_ge(S("vmm1"), 4 * c + k + 1)
                        if some(UNITS * (c - 1)):
                            act.wait_ge(S("pv1"), UNITS * (c - 1))
                        act.copy(v1[:, s, t0:t0 + nt, 0:H1 * (D1 + 1)].rearrange("p t (h d) -> p t h d", h=H1)[:, :, :, 0:D1],
                                 bank[KV1][:, 0:nt * D].rearrange("p (t h d) -> p t h d", t=nt, h=H1)
                                 ).then_inc(S("vread1"), 1)
                    elif op[0] == "M":
                        act.wait_ge(S("mt1"), c + 1)
                        act.copy(n3T1[:, s, :], bankb[XP1][0:3 * HP, 0:P]).then_inc(S("n3T1"), 1)
                        act.wait_ge(S("dm1"), c + 1)
                        act.activation(f1[:, s, :], dm1[:, s, :], ACT.Exp).then_inc(S("f1"), 1)

                def softmax(c, s, u):
                    act.wait_ge(S("st1"), UNITS * c + u + 1)
                    if some(UNITS * c + u - 3):
                        act.wait_ge(S("pv1"), UNITS * c + u - 3)
                    act.activation(p1[:, u % 4, :], bank[ST1[u % 2]][:], ACT.Exp).then_inc(S("exp1"), 1)

                def read_out(c):
                    act.wait_ge(S("pv1"), UNITS * (c + 1))
                    if some(c):
                        act.wait_ge(S("ob1"), c)
                    act.copy(ots1[:], bank[OT1][:]).then_inc(S("ots1"), 1)

                for c in range(2):
                    for op in ALL1:
                        if early(op):
                            side(op, c, c, 0)
                for op in ALL1:
                    if not early(op):
                        side(op, 0, 0, 0)

                def step(c, s, n, two, one):
                    if not (isinstance(c, int) and c == 0):
                        read_out(c - 1)
                    softmax(c, s, 0)
                    for u in range(UNITS):
                        if u + 1 < UNITS:
                            softmax(c, s, u + 1)
                        sides(side, PLAN1[u][0] + PLAN1[u][1], c, s, n, two, one)
                steps1(act, step)
                read_out(NCH - 1)
        l1.close()

        la = ExitStack()
        lT = sb(la, "lT", [P, DC, 10, P])
        dec = sb(la, "dec", [P, DC])
        bg = sb(la, "bg", [P, DC])
        blk16 = sb(la, "blk16", [P, P])
        qkv = sb(la, "qkv", [P, 6, P])
        ng = sb(la, "ng", [P, 4, P])
        kvp = sb(la, "kvp", [P, DC, P])
        scan = sb(la, "scan", [P, 4, P])
        qs = sb(la, "qs", [P, DC, P])
        rden = sb(la, "rden", [P, DC, P])
        ol = sb(la, "ol", [P, DC, P])
        gl = sb(la, "gl", [P, DC, P])

        with nc.Block() as block:
            @block.sync
            def _(sp):
                dp = a["L1_attn_decay_param"].rearrange("(c h) -> c h", c=DC)
                for c in range(DC):
                    sp.dma_start(dec[:, c:c + 1], dp[c].unsqueeze(1).to_broadcast([HL // DC, DL]).unsqueeze(2)
                                 ).then_inc(S("dec_in"), 16)
                sp.dma_start(bg[:], a["L1_attn_bgate"].rearrange("(c p) -> p c", c=DC),
                             allow_slow_non_contiguous=True).then_inc(S("bg_in"), 16)

            @block.gpsimd
            def _(pool):
                pool.memset(blk16[:], 1.0).then_inc(S("blk16"), 1)
                pool.wait_ge(S("blk16"), nth("blk16"))
                v = blk16[:].rearrange("p (b u) -> p b u", u=DL)
                pool.affine_select(out=v, in_=v, compare_op=ALU.is_ge, fill=0.0, base=0,
                                              pattern=[[-DL, P // DL], [0, DL]], channel_multiplier=1).then_inc(S("blk16"), 1)
                pool.wait_ge(S("blk16"), nth("blk16"))
                pool.affine_select(out=v, in_=v, compare_op=ALU.is_ge, fill=0.0, base=DL - 1,
                                              pattern=[[DL, P // DL], [0, DL]], channel_multiplier=-1).then_inc(S("blk16"), 1)
                pool.wait_ge(S("blk16"), nth("blk16"))
                ln_pool(pool, "ln3")

            @block.vector
            def _(dve):
                dve.reciprocal(rd1[:], acc1[:, :, D1]).then_inc(S("lstep"), 1)
                dve.wait_ge(S("lstep"), nth("lstep"))
                o3 = o1[:].rearrange("p (h d) -> p h d", h=H1)
                dve.tensor_tensor(o3, acc1[:, :, 0:D1], bc(rd1[:], 2, [P, H1, D1]), ALU.mult).then_inc(S("lstep"), 1)
                dve.wait_ge(S("lstep"), nth("lstep"))
                dve.wait_ge(S("bv1_in"), 16)
                dve.tensor_tensor(o1[:], o1[:], bv1[:], ALU.add).then_inc(S("lstep"), 1)
                dve.wait_ge(S("lstep"), nth("lstep"))
                dve.tensor_tensor(xres[:], xres[:], o1[:], ALU.add).then_inc(S("lstep"), 1)
                dve.wait_ge(S("lstep"), nth("lstep"))
                ln_dve(dve, "ln3")
                dve.wait_ge(S("edec"), 1)
                dve.tensor_scalar(dec[:], dec[:], 1.0, None, ALU.add).then_inc(S("lstep"), 1)
                dve.wait_ge(S("lstep"), nth("lstep"))
                dve.reciprocal(dec[:], dec[:]).then_inc(S("lstep"), 1)
                dve.wait_ge(S("lstep"), nth("lstep"))
                dve.tensor_scalar(dec[:], dec[:], 1e-8, None, ALU.max).then_inc(S("lstep"), 1)
                dve.wait_ge(S("lstep"), nth("lstep"))
                dve.wait_ge(S("bg_in"), 16)
                dve.tensor_scalar(bg[:], bg[:], -1.0, None, ALU.mult).then_inc(S("nbg"), 1)
                dve.wait_ge(S("nbg"), nth("nbg"))
                dve.wait_ge(S("qkv"), 2)
                q4 = qkv[:, 0:4]
                dve.tensor_scalar(ng[:], q4, 0.0, None, ALU.min).then_inc(S("ng"), 1)
                dve.wait_ge(S("ng"), nth("ng"))
                dve.tensor_scalar(q4, q4, 0.0, None, ALU.max).then_inc(S("lstep"), 1)
                dve.wait_ge(S("lstep"), nth("lstep"))
                dve.wait_ge(S("eng"), 1)
                dve.tensor_tensor(q4, q4, ng[:], ALU.add).then_inc(S("lstep"), 1)
                dve.wait_ge(S("lstep"), nth("lstep"))
                dve.tensor_tensor(kvp[:], qkv[:, 2:4], qkv[:, 4:6], ALU.mult).then_inc(S("lstep"), 1)
                dve.wait_ge(S("lstep"), nth("lstep"))
                for c in range(DC):
                    d = dec[:, c:c + 1].to_broadcast([P, P])
                    dve.tensor_tensor_scan(scan[:, 2 + c], d, qkv[:, 2 + c], 0.0, ALU.mult, ALU.add).then_inc(S("lstep"), 1)
                    dve.wait_ge(S("lstep"), nth("lstep"))
                    dve.tensor_tensor(qs[:, c], qkv[:, c], scan[:, 2 + c], ALU.mult).then_inc(S("qs"), 1)
                    dve.wait_ge(S("qs"), nth("qs"))
                for c in range(DC):
                    d = dec[:, c:c + 1].to_broadcast([P, P])
                    dve.tensor_tensor_scan(scan[:, c], d, kvp[:, c], 0.0, ALU.mult, ALU.add).then_inc(S("lstep"), 1)
                    dve.wait_ge(S("lstep"), nth("lstep"))
                dve.tensor_tensor(ol[:], qkv[:, 0:2], scan[:, 0:2], ALU.mult).then_inc(S("lstep"), 1)
                dve.wait_ge(S("lstep"), nth("lstep"))
                dve.wait_ge(S("den_psum"), 1)
                dve.tensor_scalar(rden[:], bank[4][:, 0:D].rearrange("p (c t) -> p c t", c=DC), 1e-6, None, ALU.max).then_inc(S("lstep"), 1)
                dve.wait_ge(S("lstep"), nth("lstep"))
                dve.reciprocal(rden[:], rden[:]).then_inc(S("lstep"), 1)
                dve.wait_ge(S("lstep"), nth("lstep"))
                dve.tensor_tensor(ol[:], ol[:], rden[:], ALU.mult).then_inc(S("ol"), 1)
                dve.wait_ge(S("ol"), nth("ol"))
                dve.tensor_tensor(kvp[:], ol[:], qkv[:, 4:6], ALU.subtract).then_inc(S("lstep"), 1)
                dve.wait_ge(S("lstep"), nth("lstep"))
                dve.wait_ge(S("egate"), DC)
                dve.tensor_scalar(gl[:], gl[:], 1.0, None, ALU.add).then_inc(S("lstep"), 1)
                dve.wait_ge(S("lstep"), nth("lstep"))
                dve.reciprocal(gl[:], gl[:]).then_inc(S("lstep"), 1)
                dve.wait_ge(S("lstep"), nth("lstep"))
                dve.tensor_tensor(kvp[:], kvp[:], gl[:], ALU.mult).then_inc(S("lstep"), 1)
                dve.wait_ge(S("lstep"), nth("lstep"))
                dve.tensor_tensor(kvp[:], kvp[:], qkv[:, 4:6], ALU.add).then_inc(S("mixed"), 1)
                dve.wait_ge(S("mixed"), nth("mixed"))
                dve.wait_ge(S("x5_psum"), 1)
                dve.tensor_tensor(xres[:], xres[:], bank[6][:, 0:D], ALU.add).then_inc(S("x5"), 1)
                dve.wait_ge(S("x5"), nth("x5"))

            @block.scalar
            def _(act):
                act.wait_ge(S("dec_in"), 16 * DC)
                act.activation(dec[:], dec[:], ACT.Exp, scale=-1.0).then_inc(S("edec"), 1)
                for i in range(5):
                    act.wait_ge(S("lT_psum"), i + 1)
                    act.copy(lT[:, :, 2 * i:2 * i + 2, :], bank[1 + i % 2][:].rearrange("p (k c o) -> p k c o", k=DC, c=2)
                             ).then_inc(S("lT"), 1)
                ln_act(act, "ln3", 0)
                act.wait_ge(S("qkv_psum"), 1)
                act.copy(qkv[:, 0:4], b4(3)).then_inc(S("qkv"), 1)
                act.wait_ge(S("qkv_psum"), 2)
                act.copy(qkv[:, 4:6], bank[4][:, 0:D].rearrange("p (c t) -> p c t", c=2)).then_inc(S("qkv"), 1)
                act.wait_ge(S("ng"), 1)
                act.activation(ng[:], ng[:], ACT.Exp).then_inc(S("eng"), 1)
                act.wait_ge(S("gate_psum"), 1)
                act.wait_ge(S("nbg"), 1)
                for c in range(DC):
                    act.activation(gl[:, c], bank[5][:, c * P:(c + 1) * P], ACT.Exp, scale=-1.0,
                                   bias=bg[:, c:c + 1]).then_inc(S("egate"), 1)

            @block.tensor
            def _(pe):
                pe.wait_ge(S("lraw_in"), 48)
                for i in range(5):
                    if i >= 2:
                        if some(i - 1):
                            pe.wait_ge(S("lT"), i - 1)
                    for k in range(DC):
                        for c in range(2):
                            ins = pe.transpose(bank[1 + i % 2][:, (k * 2 + c) * P:(k * 2 + c + 1) * P],
                                               lraw[:, 2 * i + c, k * P:(k + 1) * P], ident[:])
                    ins.then_inc(S("lT_psum"), 1)
                ln_pe(pe, "ln3", 0)
                pe.wait_ge(S("ln3_hT"), 1)
                pe.wait_ge(S("lT"), 5)
                for b in range(6):
                    o = bank[3][:, b * P:(b + 1) * P] if b < 4 else bank[4][:, (b - 4) * P:(b - 3) * P]
                    for k in range(DC):
                        ins = pe.matmul(o, lT[:, k, b, :], hT[:, k, :], start=(k == 0), stop=(k == DC - 1))
                    if b in (3, 5):
                        ins.then_inc(S("qkv_psum"), 1)
                pe.wait_ge(S("blk16"), 3)
                pe.wait_ge(S("qkv"), 2)
                pe.wait_ge(S("qs"), DC)
                pe.matmul(bank[4][:, 0:D], blk16[:], qs[:].rearrange("p c t -> p (c t)"), start=True,
                          stop=True).then_inc(S("den_psum"), 1)
                pe.wait_ge(S("ol"), 1)
                for b in range(DC):
                    for k in range(DC):
                        ins = pe.matmul(bank[5][:, b * P:(b + 1) * P], lT[:, k, 8 + b, :], ol[:, k, :],
                                        start=(k == 0), stop=(k == DC - 1))
                ins.then_inc(S("gate_psum"), 1)
                pe.wait_ge(S("mixed"), 1)
                for k in range(DC):
                    ins = pe.matmul(bank[6][:, 0:D], kvp[:, k, :], lT[:, k, 6:8, :].rearrange("p c o -> p (c o)"),
                                    start=(k == 0), stop=(k == DC - 1))
                ins.then_inc(S("x5_psum"), 1)
        la.close()
        xb.close()
        lw.close()

        experts("moe1", ew1, a["L1_ffn_Wg"], False, a["L1_ffn_bg"], a["L1_ffn_be"], 2, True)
        fw.close()


def kernel(**inputs):
    import numpy as _np
    import concourse.bacc as _bacc
    from concourse import mybir as _mybir
    from concourse.bass_utils import run_bass_kernel_spmd as _run

    nc = _bacc.Bacc("TRN2", target_bir_lowering=False, num_devices=1)
    arrays, args = {}, {}
    for name, value in inputs.items():
        v = _np.ascontiguousarray(value)
        if v.dtype == _np.bool_:
            v = v.view(_np.uint8)
        arrays[name] = v
        args[name] = nc.dram_tensor(name, v.shape, _mybir.dt.from_np(v.dtype), kind="ExternalInput").ap()
    result = nc.dram_tensor("out_0_dram", (1, P, D), F32, kind="ExternalOutput").ap()
    build(nc, args, result)
    r = _run(nc, [arrays], core_ids=[0])
    return r.results[0]["out_0_dram"]
```

```python
from contextlib import ExitStack

import concourse.bass as bass
from concourse import mybir

F32 = mybir.dt.float32
BF16 = mybir.dt.bfloat16
U8 = mybir.dt.uint8
ALU = mybir.AluOpType
ACT = mybir.ActivationFunctionType
AX = mybir.AxisListType

P = 128
D = 256
DC = D // P
M = 12544
CT = 7
CH = CT * P
HCH = CH // 2
NCH = M // CH
LN_EPS = 1e-5
MASKED = float(2.0 ** 100)
LOWEST = -float(2.0 ** 101)

H0, D0 = 4, 64
S0 = D0 ** -0.5
H1, D1 = 16, 16
S1 = D1 ** -0.5
K_TERM = (0, 1, 0, 1, 2, 0)
Q_TERM = (0, 0, 1, 1, 0, 2)
NJ = len(K_TERM)
KROWS = NJ * D1
KONES = KROWS + 3

NH, DK, DV = 12, 64, 128
KB = NH * DK // P
VB = NH * DV // P
CB = 2 * KB + VB
TAPS = 4
GH = 4
NG = NH // GH
LEVELS = (1, 2, 4, 8, 16, 32, 64)

E = 8
HL, DL = 16, 16


def build(nc, a, out):
    sems = {}
    counts = {}
    ctx = ExitStack()

    def S(name):
        if name not in sems:
            sems[name] = nc.alloc_semaphore(name)
        return sems[name]

    def renew(keep):
        old = [sems.pop(name) for name in list(sems) if name not in keep]
        counts.clear()
        nc.clear_and_free_semaphores(old)
        with nc.Block() as block:
            @block.gpsimd
            def _(pool):
                pool.nop()

    def some(value):
        return not (isinstance(value, int) and value <= 0)

    def nth(name):
        counts[name] = counts.get(name, 0) + 1
        return counts[name]

    def bc(ap, axis, shape):
        return ap.unsqueeze(axis).to_broadcast(shape)

    def wcols(w, c=DC):
        return w.rearrange("(c p) n -> p c n", c=c)

    def sb(st, name, shape, dt=F32):
        return st.enter_context(nc.sbuf_tensor(name, shape, dt))

    def running_maximum(dve, x, c, s, mx, top, run, reads, steps):
        dve.wait_ge(S("smread" + x), reads * (c + 1))
        dve.tensor_reduce(top[:], mx[:], AX.X, ALU.max).then_inc(S("maxstep" + x), 1)
        dve.wait_ge(S("maxstep" + x), steps * c + 1)
        dve.tensor_tensor(run[:, s], run[:, 1 - s], top[:], ALU.max).then_inc(S("maxstep" + x), 1)
        dve.wait_ge(S("maxstep" + x), steps * c + 2)

    with ctx:
        bank = [ctx.enter_context(nc.psum_tensor(f"bank{i}", [P, 512], F32)) for i in range(8)]
        bankb = [b[:].bitcast(BF16) for b in bank]

        keep = ctx.enter_context(ExitStack())
        xres = sb(keep, "xres", [P, D])
        ident = sb(keep, "ident", [P, P])
        identb = sb(keep, "identb", [P, P], BF16)
        onesb = sb(keep, "onesb", [P, P], BF16)
        tri = sb(keep, "tri", [P, P])
        below = sb(keep, "below", [P, P])
        mhalf = sb(keep, "mhalf", [P, NH])
        eps6 = sb(keep, "eps6", [P, 1])
        stats = sb(keep, "stats", [P, 6])
        mv = sb(keep, "mv", [P, 2])
        rstd = sb(keep, "rstd", [P, 1])
        xn = sb(keep, "xn", [P, D])
        hT = sb(keep, "hT", [P, DC, P])

        def ln_dve(dve, tag):
            dve.bn_stats(stats[:], xres[:]).then_inc(S(tag + "_stats"), 1)
            dve.wait_ge(S(tag + "_stats"), nth(tag + "_stats"))
            dve.bn_aggr(mv[:], stats[:]).then_inc(S(tag + "_var"), 1)
            dve.wait_ge(S(tag + "_var"), nth(tag + "_var"))
            dve.wait_ge(S(tag + "_rstd"), 2)
            dve.tensor_scalar(xn[:], xres[:], mv[:, 0:1], rstd[:, 0:1], ALU.subtract, ALU.mult).then_inc(S(tag + "_xn"), 1)
            dve.wait_ge(S(tag + "_xn"), nth(tag + "_xn"))

        def ln_pool(pool, tag):
            pool.wait_ge(S(tag + "_var"), 1)
            pool.tensor_scalar(rstd[:], mv[:, 1:2], LN_EPS, None, ALU.add).then_inc(S(tag + "_rstd"), 1)
            pool.wait_ge(S(tag + "_rstd"), nth(tag + "_rstd"))
            pool.tensor_tensor(rstd[:], rstd[:], mhalf[:, 0:1], ALU.pow).then_inc(S(tag + "_rstd"), 1)
            pool.wait_ge(S(tag + "_rstd"), nth(tag + "_rstd"))

        def ln_pe(pe, tag, b):
            pe.wait_ge(S(tag + "_xn"), 1)
            for k in range(DC):
                ins = pe.transpose(bank[b][:, k * P:(k + 1) * P], xn[:, k * P:(k + 1) * P], ident[:])
            ins.then_inc(S(tag + "_xnT"), 1)

        def ln_act(act, tag, b):
            act.wait_ge(S(tag + "_xnT"), 1)
            act.copy(hT[:].rearrange("p k t -> p (k t)"), bank[b][:, 0:D]).then_inc(S(tag + "_hT"), 1)

        raw1 = sb(keep, "raw1", [P, 3, DC, D])
        WT1 = sb(keep, "WT1", [P, 3, DC, D])
        ew = sb(keep, "ew", [P, E * DC, D])

        gw = ExitStack()
        Wc = sb(gw, "Wc", [P, DC, CB * P])
        Wg = sb(gw, "Wg", [P, DC, NH * DV])
        Wo = sb(gw, "Wo", [P, NH, D])
        Wgb = sb(gw, "Wgb", [P, DC, 2 * NH])
        convw = sb(gw, "convw", [P, CB, TAPS])
        gbias = sb(gw, "gbias", [P, 2 * NH])
        nA = sb(gw, "nA", [P, NH])
        gnw = sb(gw, "gnw", [P, DV])

        def load_delta_weights(eng):
            def get(dst, src):
                eng.dma_start(dst, src).then_inc(S("gw_in"), 16)
            get(Wc[:, :, 0:KB * P], wcols(a["L0_attn_Wq"]))
            get(Wc[:, :, KB * P:2 * KB * P], wcols(a["L0_attn_Wk"]))
            get(Wc[:, :, 2 * KB * P:], wcols(a["L0_attn_Wv"]))
            get(Wg[:], wcols(a["L0_attn_Wg"]))
            get(Wo[:], wcols(a["L0_attn_Wo"], NH))
            get(Wgb[:, :, 0:NH], wcols(a["L0_attn_Wgk"]))
            get(Wgb[:, :, NH:], wcols(a["L0_attn_Wb"]))
            get(convw[:, 0:KB], wcols(a["L0_attn_conv_q"], KB))
            get(convw[:, KB:2 * KB], wcols(a["L0_attn_conv_k"], KB))
            get(convw[:, 2 * KB:], wcols(a["L0_attn_conv_v"], VB))
            get(gbias[:, 0:NH], a["L0_attn_dt_bias"].partition_broadcast(P))
            get(gbias[:, NH:], a["L0_attn_b_b"].partition_broadcast(P))
            get(nA[:], a["L0_attn_A_log"].partition_broadcast(P))
            get(gnw[:], a["L0_attn_g_norm_weight"].partition_broadcast(P))
            eng.dma_start(ew[:], a["L0_ffn_expert_w"].rearrange("e (c p) d -> p (e c) d", p=P)).then_inc(S("ew0_in"), 16)
            for k, name in enumerate(("L1_xattn_Wq", "L1_xattn_Wk", "L1_xattn_Wv")):
                eng.dma_start(raw1[:, k], wcols(a[name])).then_inc(S("raw1_in"), 16)
        GW_LOADS = 14

        xa = ExitStack()
        Wo0 = sb(xa, "Wo0", [P, DC, D])
        run0 = sb(xa, "run0", [P, 2, H0])
        acc0 = sb(xa, "acc0", [P, H0, D0 + 1])
        o0 = sb(xa, "o0", [P, D])
        oT0 = sb(xa, "oT0", [P, DC, P])
        rd0 = sb(xa, "rd0", [P, H0])
        fl0 = sb(xa, "fl0", [P, H0])
        l0 = ExitStack()
        Wq0 = sb(l0, "Wq0", [P, DC, D])
        Wkv0 = sb(l0, "Wkv0", [P, DC, 2 * D])
        q0 = sb(l0, "q0", [P, DC, 2, P])
        ctx0 = sb(l0, "ctx0", [P, 2, CT, D])
        ctxT0 = sb(l0, "ctxT0", [P, DC, CH])
        kT0 = sb(l0, "kT0", [P, DC, CH])
        v0 = sb(l0, "v0", [P, 2, CT, H0, D0])
        mask0 = sb(l0, "mask0", [P, 2, CH], U8)
        pen0 = sb(l0, "pen0", [P, CH], BF16)
        gate0 = sb(l0, "gate0", [P, 2])
        sc0 = sb(l0, "sc0", [P, 2, H0, CH])
        mx0 = sb(l0, "mx0", [P, H0, 2])
        top0 = sb(l0, "top0", [P, H0])
        neg0 = sb(l0, "neg0", [P, H0])
        dm0 = sb(l0, "dm0", [P, 2, H0])
        f0 = sb(l0, "f0", [P, 2, H0])
        den0 = sb(l0, "den0", [P, 2, H0, 2])
        pT0 = sb(l0, "pT0", [P, 2, H0 * P])
        ots0 = sb(l0, "ots0", [P, H0 // 2 * P])

        ctx_rows = a["ctx_1024"].rearrange("b m d -> (b m) d")
        mask_rows = a["mask_BxSxS2_bf1"].rearrange("b q m -> (b q) m")

        def chunk_of(c):
            return ctx_rows[bass.ds(c * CH, CH), :].rearrange("(t p) d -> p t d", p=P)

        with nc.Block() as block:
            @block.sync
            def _(sp):
                sp.dma_start(xres[:], a["x"].rearrange("b q d -> (b q) d")).then_inc(S("x_in"), 16)
                sp.dma_start(Wq0[:], wcols(a["L0_xattn_Wq"])).then_inc(S("wq0_in"), 16)
                for c in range(2):
                    sp.dma_start(ctx0[:, c], chunk_of(c)).then_inc(S(f"ctx0_{c}"), 16)
                    if c == 0:
                        sp.dma_start(Wkv0[:], wcols(a["L0_xattn_Wkv"])).then_inc(S("wkv0_in"), 16)
                    sp.dma_start(mask0[:, c], mask_rows[:, c * CH:(c + 1) * CH]).then_inc(S(f"mask0_{c}"), 16)
                sp.dma_start(Wo0[:], wcols(a["L0_xattn_Wo"])).then_inc(S("wo0_in"), 16)

            @block.gpsimd
            def _(pool):
                pool.memset(eps6[:], 1e-6).then_inc(S("eps6"), 1)
                pool.memset(mhalf[:], -0.5).then_inc(S("mhalf"), 1)
                pool.wait_ge(S("mhalf"), 1)
                pool.memset(ident[:], 0.0).then_inc(S("ident"), 1)
                pool.wait_ge(S("ident"), nth("ident"))
                pool.affine_select(out=ident[:], in_=ident[:], compare_op=ALU.not_equal, fill=1.0, base=0,
                                              pattern=[[-1, P]], channel_multiplier=1).then_inc(S("ident"), 1)
                pool.wait_ge(S("ident"), nth("ident"))
                ln_pool(pool, "ln0")
                pool.memset(acc0[:], 0.0).then_inc(S("acc0"), 1)
                pool.memset(run0[:], LOWEST).then_inc(S("run0_lowest"), 1)

            @block.vector
            def _(dve):
                dve.memset(q0[:], 0.0).then_inc(S("q0_zero"), 1)
                dve.wait_ge(S("x_in"), 16)
                ln_dve(dve, "ln0")
                dve.wait_ge(S("q0_zero"), 1)
                dve.wait_ge(S("q0_psum"), 1)
                for b in range(DC):
                    for e in range(2):
                        r = slice(e * D0, (e + 1) * D0)
                        dve.tensor_scalar(q0[r, b, e, :], bank[1][r, b * P:(b + 1) * P], S0, None,
                                          ALU.mult).then_inc(S("q0"), 1)

            @block.tensor
            def _(pe):
                pe.wait_ge(S("ident"), 2)
                ln_pe(pe, "ln0", 0)
                pe.wait_ge(S("ln0_hT"), 1)
                pe.wait_ge(S("wq0_in"), 16)
                for b in range(DC):
                    for k in range(DC):
                        ins = pe.matmul(bank[1][:, b * P:(b + 1) * P], Wq0[:, k, b * P:(b + 1) * P], hT[:, k, :],
                                        start=(k == 0), stop=(k == DC - 1))
                ins.then_inc(S("q0_psum"), 1)

            @block.scalar
            def _(act):
                ln_act(act, "ln0", 0)

        SX, KV, PT, OT, OB = (0, 3), (1, 2), (4, 5), 6, 7
        TG = ((0, 0, 4), (1, 0, 4), (0, 4, 3), (1, 4, 3))
        VG = ((0, 2), (2, 2), (4, 2), (6, 1))
        PLAN0 = ((("T0",), ("T1",)), (("T2",), ("T3", "K0")), (("K1",), ("S0", "K2")), (("S1", "K3"), ("S2", "S3")),
                 (("S4", "V0"), ("S5",)), (("S6", "S7", "M0"), ("E0", "E1", "E2", "E3", "V1")),
                 (("V2", "F0"), ("V3",)))
        ALL0 = tuple(op for before, after in PLAN0 for op in before + after)

        def steps(eng, step, last):
            step(0, 0, 0)
            with eng.Fori(0, (NCH - 2) // 2) as i:
                step(i * 2 + 1, 1, i)
                step(i * 2 + 2, 0, i + 1)
            last(NCH - 1, 1, (NCH - 2) // 2)

        with nc.Block() as block:
            @block.gpsimd
            def _(pool):
                pool.tensor_copy(identb[:], ident[:]).then_inc(S("identb"), 1)
                pool.wait_ge(S("identb"), nth("identb"))
                pool.memset(onesb[:], 1.0).then_inc(S("onesb"), 1)
                pool.wait_ge(S("onesb"), nth("onesb"))
                pool.memset(tri[:], 1.0).then_inc(S("tri"), 1)
                pool.wait_ge(S("tri"), nth("tri"))
                pool.affine_select(out=tri[:], in_=tri[:], compare_op=ALU.is_ge, fill=0.0, base=0,
                                              pattern=[[1, P]], channel_multiplier=-1).then_inc(S("tri"), 1)
                pool.wait_ge(S("tri"), nth("tri"))
                pool.memset(below[:], 1.0).then_inc(S("below"), 1)
                pool.wait_ge(S("below"), nth("below"))
                pool.affine_select(out=below[:], in_=below[:], compare_op=ALU.is_gt, fill=0.0, base=0,
                                              pattern=[[-1, P]], channel_multiplier=1).then_inc(S("below"), 1)
                pool.wait_ge(S("below"), nth("below"))

            @block.sync
            def _(sp):
                def load(c, s):
                    if some(4 * (c - 1)):
                        sp.wait_ge(S("xp0"), 4 * (c - 1))
                    sp.dma_start(ctx0[:, s], chunk_of(c)).then_inc(S(f"ctx0_{s}"), 16)
                    if some(c - 1):
                        sp.wait_ge(S("pen0"), c - 1)
                    sp.dma_start(mask0[:, s], mask_rows[:, bass.ds(c * CH, CH)]).then_inc(S(f"mask0_{s}"), 16)

                def step(c, s, n):
                    load(c + 2, s)
                step(0, 0, 0)
                with sp.Fori(0, (NCH - 4) // 2) as i:
                    step(i * 2 + 1, 1, i)
                    step(i * 2 + 2, 0, i + 1)
                step(NCH - 3, 1, None)

            @block.tensor
            def _(pe):
                def side(op, c, s, n):
                    k = int(op[1:])
                    if op[0] == "T":
                        if k == 0:
                            pe.wait_ge(S(f"ctx0_{s}"), 16 * n + 16)
                            if some(8 * c):
                                pe.wait_ge(S("smread0"), 8 * c)
                        if k >= 2:
                            pe.wait_ge(S("ctxT0"), 4 * c + k - 1)
                        h, t0, nt = TG[k]
                        for t in range(nt):
                            ins = pe.transpose(bank[SX[k % 2]][:, t * P:(t + 1) * P], ctx0[:, s, t0 + t, h * P:(h + 1) * P],
                                               ident[:])
                        ins.then_inc(S("xp0"), 1)
                    elif op[0] == "K":
                        half, b = k // 2, k % 2
                        if isinstance(c, int) and c == 0:
                            pe.wait_ge(S("wkv0_in"), 16)
                        pe.wait_ge(S("ctxT0"), 4 * c + 2 * half + 2)
                        if some(8 * c + k - 1):
                            pe.wait_ge(S("kvread0"), 8 * c + k - 1)
                        for i in range(DC):
                            ins = pe.matmul(bank[KV[k % 2]][:, 0:HCH], Wkv0[:, i, b * P:(b + 1) * P],
                                            ctxT0[:, i, half * HCH:(half + 1) * HCH], start=(i == 0), stop=(i == DC - 1))
                        ins.then_inc(S("kv0"), 1)
                    elif op[0] == "S":
                        if isinstance(c, int) and c == 0:
                            pe.wait_ge(S("q0"), 4)
                        half, h = k // H0, k % H0
                        pe.wait_ge(S("kvread0"), 8 * c + 2 * half + h // 2 + 1)
                        if k == 0:
                            pe.wait_ge(S("ctxT0"), 4 * c + 4)
                        if k >= 2:
                            pe.wait_ge(S("smread0"), 8 * c + k - 1)
                        pe.matmul(bank[SX[k % 2]][:, 0:HCH], q0[:, h // 2, h % 2, :],
                                  kT0[:, h // 2, half * HCH:(half + 1) * HCH],
                                  start=True, stop=True).then_inc(S("sm0"), 1)
                    elif op[0] == "V":
                        t0, nt = VG[k]
                        if some(8 * c + 4 + k - 1):
                            pe.wait_ge(S("kvread0"), 8 * c + 4 + k - 1)
                        for t in range(nt):
                            for i in range(DC):
                                ins = pe.matmul(bank[KV[k % 2]][:, t * D:(t + 1) * D],
                                                ctxT0[:, i, (t0 + t) * P:(t0 + t + 1) * P], Wkv0[:, i, D:2 * D],
                                                start=(i == 0), stop=(i == DC - 1))
                        ins.then_inc(S("kv0"), 1)

                def turn_exps(c, s, t):
                    pe.wait_ge(S("exp0"), 8 * c + (4 if (t + 1) * P <= HCH else 8))
                    if some(CT * c + t - 1):
                        pe.wait_ge(S("pT0"), CT * c + t - 1)
                    for h in range(H0):
                        ins = pe.transpose(bank[PT[(s + t) % 2]][:, h * P:(h + 1) * P],
                                           sc0[:, s, h, t * P:(t + 1) * P], ident[:])
                    ins.then_inc(S("pt0"), 1)

                def values(c, s, t):
                    pe.wait_ge(S("pT0"), CT * c + t + 1)
                    if t == 0:
                        if some(c):
                            pe.wait_ge(S("ots0"), c)
                    if t % 2 == 0:
                        pe.wait_ge(S("kvread0"), 8 * c + 4 + t // 2 + 1)
                    for h in range(H0):
                        ins = pe.matmul(bank[OT][h % 2 * D0:(h % 2 + 1) * D0, h // 2 * P:(h // 2 + 1) * P],
                                        v0[:, s, t, h, :], pT0[:, (s + t) % 2, h * P:(h + 1) * P],
                                        start=(t == 0 and h < 2), stop=(t == CT - 1), skip_group_check=True)
                    ins.then_inc(S("pv0"), 1)

                def turn(c):
                    pe.wait_ge(S("ots0"), c + 1)
                    pe.wait_ge(S("acc0"), 4 * c + 1)
                    for j in range(H0 // 2):
                        ins = pe.transpose(bank[OB][:, j * P:(j + 1) * P], ots0[:, j * P:(j + 1) * P], ident[:])
                    ins.then_inc(S("ob0"), 1)

                for op in ALL0:
                    side(op, 0, 0, 0)

                def step(c, s, n, ahead=True):
                    turn_exps(c, s, 0)
                    if not (isinstance(c, int) and c == 0):
                        turn(c - 1)
                    for t in range(CT):
                        if t + 1 < CT:
                            turn_exps(c, s, t + 1)
                        for op in PLAN0[t][0] if ahead else ():
                            side(op, c + 1, 1 - s, n + s)
                        values(c, s, t)
                        for op in PLAN0[t][1] if ahead else ():
                            side(op, c + 1, 1 - s, n + s)
                steps(pe, step, lambda c, s, n: step(c, s, n, False))
                turn(NCH - 1)

            @block.vector
            def _(dve):
                def side(op, c, s, n):
                    k = int(op[1:])
                    if op[0] == "T":
                        h, t0, nt = TG[k]
                        dve.wait_ge(S("xp0"), 4 * c + k + 1)
                        if some(8 * c):
                            dve.wait_ge(S("kv0"), 8 * c)
                        dve.tensor_copy(ctxT0[:, h, t0 * P:(t0 + nt) * P],
                                        bank[SX[k % 2]][:, 0:nt * P]).then_inc(S("ctxT0"), 1)
                    elif op[0] == "S":
                        half, h = k // H0, k % H0
                        dve.wait_ge(S("sm0"), 8 * c + k + 1)
                        if k == 0:
                            dve.wait_ge(S("pen0"), c + 1)
                            if some(CT * (c - 1)):
                                dve.wait_ge(S("pt0"), CT * (c - 1))
                        dve.memset(gate0[:, k % 2:k % 2 + 1], 0.0)
                        dve.tensor_tensor_reduce(out=sc0[:, s, h, half * HCH:(half + 1) * HCH],
                                                 in0=bank[SX[k % 2]][:, 0:HCH],
                                                 in1=pen0[:, half * HCH:(half + 1) * HCH], scale=1.0,
                                                 scalar=LOWEST, op0=ALU.add, op1=ALU.max,
                                                 accum_out=mx0[:, h, half:half + 1]).then_inc(S("smread0"), 1)
                    elif op[0] == "M":
                        running_maximum(dve, "0", c, s, mx0, top0, run0, 8, 2)
                        if some(8 * c):
                            dve.wait_ge(S("exp0"), 8 * c)
                        dve.tensor_scalar(neg0[:], run0[:, s], -1.0, None, ALU.mult).then_inc(S("neg0"), 1)
                        if some(c - 1):
                            dve.wait_ge(S("f0"), c - 1)
                        dve.tensor_tensor(dm0[:, s], run0[:, 1 - s], run0[:, s], ALU.subtract).then_inc(S("dm0"), 1)

                def read_out(c):
                    dve.wait_ge(S("pv0"), CT * (c + 1))
                    dve.wait_ge(S("acc0"), 4 * c + 1)
                    dve.tensor_copy(ots0[:], bank[OT][:, 0:H0 // 2 * P]).then_inc(S("ots0"), 1)

                def rescale(c, s):
                    dve.wait_ge(S("acc0"), 4 * c + 1)
                    dve.wait_ge(S("f0"), c + 1)
                    dve.tensor_tensor(acc0[:], acc0[:], bc(f0[:, s, :], 2, [P, H0, D0 + 1]), ALU.mult).then_inc(S("acc0"), 1)
                    for half in range(2):
                        dve.wait_ge(S("acc0"), 4 * c + 2 + half)
                        dve.tensor_tensor(acc0[:, :, D0], acc0[:, :, D0], den0[:, s, :, half],
                                          ALU.add).then_inc(S("acc0"), 1)
                    dve.wait_ge(S("ob0"), c + 1)
                    dve.tensor_tensor(acc0[:, :, 0:D0], acc0[:, :, 0:D0],
                                      bank[OB][:, 0:D].rearrange("p (h d) -> p h d", h=H0),
                                      ALU.add).then_inc(S("acc0"), 1)

                def penalty(c, s, n):
                    dve.wait_ge(S(f"mask0_{s}"), 16 * n + 16)
                    if some(8 * c):
                        dve.wait_ge(S("smread0"), 8 * c)
                    dve.tensor_scalar(pen0[:], mask0[:, s], MASKED, -MASKED, ALU.mult,
                                      ALU.add).then_inc(S("pen0"), 1)

                penalty(0, 0, 0)
                for op in ALL0:
                    side(op, 0, 0, 0)

                def step(c, s, n):
                    if not (isinstance(c, int) and c == 0):
                        read_out(c - 1)
                    for op in ALL0:
                        side(op, c + 1, 1 - s, n + s)
                        if op == "T1":
                            penalty(c + 1, 1 - s, n + s)
                        if op == "T2" and not (isinstance(c, int) and c == 0):
                            rescale(c - 1, 1 - s)

                def last(c, s, n):
                    read_out(c - 1)
                    rescale(c - 1, 1 - s)
                    read_out(c)
                    rescale(c, s)
                steps(dve, step, last)

            @block.scalar
            def _(act):
                def side(op, c, s, n):
                    k = int(op[1:])
                    if op[0] == "K":
                        half, b = k // 2, k % 2
                        act.wait_ge(S("kv0"), 8 * c + k + 1)
                        if some(8 * c):
                            act.wait_ge(S("sm0"), 8 * c)
                        act.copy(kT0[:, b, half * HCH:(half + 1) * HCH],
                                 bank[KV[k % 2]][:, 0:HCH]).then_inc(S("kvread0"), 1)
                    elif op[0] == "V":
                        t0, nt = VG[k]
                        act.wait_ge(S("kv0"), 8 * c + 4 + k + 1)
                        if some(CT * (c - 1)):
                            act.wait_ge(S("pv0"), CT * (c - 1))
                        act.copy(v0[:, s, t0:t0 + nt],
                                 bank[KV[k % 2]][:, 0:nt * D].rearrange("p (t h d) -> p t h d", t=nt, h=H0)
                                 ).then_inc(S("kvread0"), 1)
                    elif op[0] == "E":
                        exps(c, s, 0, k)
                    elif op[0] == "F":
                        act.wait_ge(S("dm0"), c + 1)
                        act.activation(f0[:, s, :], dm0[:, s, :], ACT.Exp).then_inc(S("f0"), 1)

                def exps(c, s, half, h):
                    cols = slice(half * HCH, (half + 1) * HCH)
                    act.wait_ge(S("neg0"), c + 1)
                    act.activation(sc0[:, s, h, cols], sc0[:, s, h, cols], ACT.Exp, bias=neg0[:, h:h + 1],
                                   accum_out=den0[:, s, h, half:half + 1]).then_inc(S("exp0"), 1)

                def take_exps(c, s, t):
                    act.wait_ge(S("pt0"), CT * c + t + 1)
                    if some(CT * c + t - 1):
                        act.wait_ge(S("pv0"), CT * c + t - 1)
                    u = (s + t) % 2
                    act.copy(pT0[:, u, :], bank[PT[u]][:]).then_inc(S("pT0"), 1)

                load_delta_weights(act)
                for op in ALL0:
                    side(op, 0, 0, 0)

                def step(c, s, n, ahead=True):
                    take_exps(c, s, 0)
                    for t in range(CT):
                        if t + 1 < CT:
                            take_exps(c, s, t + 1)
                        if t == 0:
                            for h in range(H0):
                                exps(c, s, 1, h)
                        for op in PLAN0[t][0] + PLAN0[t][1] if ahead else ():
                            side(op, c + 1, 1 - s, n + s)
                steps(act, step, lambda c, s, n: step(c, s, n, False))
        l0.close()


        gd = ExitStack()
        level = sb(gd, "level", [P, len(LEVELS), P])
        pair = sb(gd, "pair", [P, P])
        blk64 = sb(gd, "blk64", [P, P])
        half = sb(gd, "half", [P, 2])
        xpad = sb(gd, "xpad", [P, CB, P + TAPS - 1])
        cv = sb(gd, "cv", [P, CB, P])
        gz = sb(gd, "gz", [P, 2 * NH])
        ge = sb(gd, "ge", [P, 2 * NH])
        gp = sb(gd, "gp", [P, NH])
        beta = sb(gd, "beta", [P, NH])
        gk = sb(gd, "gk", [P, NH])
        sg = sb(gd, "sg", [P, NH, DV])
        R = sb(gd, "R", [P, 2, NH, P])
        DT = sb(gd, "DT", [P, NH, P])
        Dm = sb(gd, "Dm", [P, NH, P])
        sq = sb(gd, "sq", [P, NH, P])
        rs = sb(gd, "rs", [P, NH, P])
        kz = sb(gd, "kz", [P, NH, P])
        Am = sb(gd, "Am", [P, 2, NH, P])
        bv = sb(gd, "bv", [P, NH, DV])
        w = sb(gd, "w", [P, NH, DV])
        at = sb(gd, "at", [P, NH, P])
        oh = sb(gd, "oh", [P, NH, DV])
        ss = sb(gd, "ss", [P, NH])
        oT = sb(gd, "oT", [P, NH, P])
        A, AT = (xpad[:].rearrange("p a b -> p (a b)")[:, k * NH * P:(k + 1) * NH * P].rearrange(
            "p (h t) -> p h t", h=NH) for k in range(2))
        X, U = R[:, 0], R[:, 1]
        Z, dl = sq, rs

        def hb(g):
            return slice(g * GH, (g + 1) * GH)

        def b4(i):
            return bank[i][:].rearrange("p (h t) -> p h t", h=GH)

        with nc.Block() as block:
            @block.gpsimd
            def _(pool):
                pool.memset(xpad[:, :, 0:TAPS - 1], 0.0).then_inc(S("xpad_zero"), 1)
                ln_pool(pool, "ln1")
                pool.memset(level[:], 0.0).then_inc(S("masks"), 1)
                pool.wait_ge(S("masks"), nth("masks"))
                for n, z in enumerate(LEVELS):
                    v = level[:, n].rearrange("p (b u) -> p b u", u=2 * z)[:, :, z:2 * z]
                    nb = P // (2 * z)
                    pool.memset(v, 1.0).then_inc(S("masks"), 1)
                    pool.wait_ge(S("masks"), nth("masks"))
                    pool.affine_select(out=v, in_=v, compare_op=ALU.is_ge, fill=0.0, base=0,
                                                  pattern=[[-2 * z, nb], [0, z]], channel_multiplier=1).then_inc(S("masks"), 1)
                    pool.wait_ge(S("masks"), nth("masks"))
                    pool.affine_select(out=v, in_=v, compare_op=ALU.is_ge, fill=0.0, base=z - 1,
                                                  pattern=[[2 * z, nb], [0, z]], channel_multiplier=-1).then_inc(S("masks"), 1)
                    pool.wait_ge(S("masks"), nth("masks"))
                pool.memset(pair[:], 0.0).then_inc(S("masks"), 1)
                pool.wait_ge(S("masks"), nth("masks"))
                v = pair[:].rearrange("p (b u) -> p b u", u=2)[:, :, 0:1]
                pool.affine_select(out=v, in_=v, compare_op=ALU.not_equal, fill=1.0, base=-1,
                                              pattern=[[-2, P // 2], [0, 1]], channel_multiplier=1).then_inc(S("masks"), 1)
                pool.wait_ge(S("masks"), nth("masks"))
                pool.memset(blk64[:], 0.0).then_inc(S("masks"), 1)
                pool.wait_ge(S("masks"), nth("masks"))
                pool.memset(half[:], 0.0).then_inc(S("masks"), 1)
                pool.wait_ge(S("masks"), nth("masks"))
                for e in range(2):
                    r = slice(e * DK, (e + 1) * DK)
                    pool.memset(blk64[r, r], 1.0).then_inc(S("masks"), 1)
                    pool.wait_ge(S("masks"), nth("masks"))
                    pool.memset(half[r, e:e + 1], 1.0).then_inc(S("masks"), 1)
                    pool.wait_ge(S("masks"), nth("masks"))
                pool.wait_ge(S("gk"), 1)
                pool.tensor_tensor(R[:, 0], bc(tri[:], 1, [P, NH, P]), bc(gk[:], 2, [P, NH, P]), ALU.mult).then_inc(S("R"), 1)
                pool.wait_ge(S("R"), nth("R"))
                pool.tensor_tensor(R[:, 1], bc(below[:], 1, [P, NH, P]), bc(gk[:], 2, [P, NH, P]), ALU.mult).then_inc(S("R"), 1)
                pool.wait_ge(S("R"), nth("R"))
                pool.wait_ge(S("dexp"), 6)
                pool.tensor_tensor(Dm[:], Dm[:], bc(below[:], 1, [P, NH, P]), ALU.mult).then_inc(S("Dm"), 1)
                pool.wait_ge(S("Dm"), nth("Dm"))
                pool.tensor_tensor(Dm[:], Dm[:], bc(beta[:], 2, [P, NH, P]), ALU.mult).then_inc(S("Dm"), 1)
                pool.wait_ge(S("Dm"), nth("Dm"))
                pool.tensor_tensor(DT[:], DT[:], bc(tri[:], 1, [P, NH, P]), ALU.mult).then_inc(S("DT"), 1)
                pool.wait_ge(S("DT"), nth("DT"))
                pool.wait_ge(S("sg"), NG)
                pool.tensor_tensor(sg[:], sg[:], bc(gnw[:], 1, [P, NH, DV]), ALU.mult).then_inc(S("sgw"), 1)
                for n in range(1, len(LEVELS)):
                    pool.wait_ge(S("AT"), NG)
                    if some(NG * (n - 2)):
                        pool.wait_ge(S("Zmm"), NG * (n - 2))
                    pool.tensor_tensor(Am[:, n % 2], AT, bc(level[:, n], 1, [P, NH, P]), ALU.mult).then_inc(S("Am"), 1)
                for g in range(NG):
                    pool.wait_ge(S("ss"), g + 1)
                    pool.tensor_scalar(ss[:, hb(g)], ss[:, hb(g)], 1.0 / DV, LN_EPS, ALU.mult,
                                       ALU.add).then_inc(S("rms"), 1)
                    pool.wait_ge(S("rms"), nth("rms"))
                    pool.tensor_tensor(ss[:, hb(g)], ss[:, hb(g)], mhalf[:, hb(g)], ALU.pow).then_inc(S("rms"), 1)
                    pool.wait_ge(S("rms"), nth("rms"))

            @block.vector
            def _(dve):
                dve.tensor_scalar(fl0[:], run0[:, 1], -MASKED / 2, None, ALU.is_gt).then_inc(S("o0step"), 1)
                dve.wait_ge(S("o0step"), nth("o0step"))
                dve.tensor_tensor(rd0[:], acc0[:, :, D0], fl0[:], ALU.mult).then_inc(S("o0step"), 1)
                dve.wait_ge(S("o0step"), nth("o0step"))
                dve.reciprocal(rd0[:], rd0[:]).then_inc(S("o0step"), 1)
                dve.wait_ge(S("o0step"), nth("o0step"))
                o3 = o0[:].rearrange("p (h d) -> p h d", h=H0)
                dve.tensor_tensor(o3, acc0[:, :, 0:D0], bc(fl0[:], 2, [P, H0, D0]), ALU.mult).then_inc(S("o0step"), 1)
                dve.wait_ge(S("o0step"), nth("o0step"))
                dve.tensor_tensor(o3, o3, bc(rd0[:], 2, [P, H0, D0]), ALU.mult).then_inc(S("o0"), 1)
                dve.wait_ge(S("o0"), nth("o0"))
                dve.wait_ge(S("x1_psum"), 1)
                dve.tensor_tensor(xres[:], xres[:], bank[6][:, 0:D], ALU.add).then_inc(S("x1"), 1)
                dve.wait_ge(S("x1"), nth("x1"))
                ln_dve(dve, "ln1")
                dve.wait_ge(S("gates_psum"), 1)
                dve.tensor_tensor(gz[:], bank[7][:, 0:2 * NH], gbias[:], ALU.add).then_inc(S("gstep"), 1)
                dve.wait_ge(S("gstep"), nth("gstep"))
                dve.tensor_scalar(gp[:], gz[:, 0:NH], -1.0, None, ALU.mult).then_inc(S("gstep"), 1)
                dve.wait_ge(S("gstep"), nth("gstep"))
                dve.tensor_tensor(ge[:, 0:NH], gz[:, 0:NH], gp[:], ALU.min).then_inc(S("gstep"), 1)
                dve.wait_ge(S("gstep"), nth("gstep"))
                dve.tensor_scalar(ge[:, NH:], gz[:, NH:], -1.0, None, ALU.mult).then_inc(S("ge_in"), 1)
                dve.wait_ge(S("ge_in"), nth("ge_in"))
                dve.tensor_scalar(gp[:], gz[:, 0:NH], 0.0, None, ALU.max).then_inc(S("gstep"), 1)
                dve.wait_ge(S("gstep"), nth("gstep"))
                dve.wait_ge(S("ge"), 1)
                dve.tensor_scalar(ge[:], ge[:], 1.0, None, ALU.add).then_inc(S("ge1"), 1)
                dve.wait_ge(S("ge1"), nth("ge1"))
                dve.reciprocal(beta[:], ge[:, NH:]).then_inc(S("beta"), 1)
                dve.wait_ge(S("beta"), nth("beta"))
                dve.wait_ge(S("softplus"), 1)
                dve.tensor_tensor(gp[:], gp[:], ge[:, 0:NH], ALU.add).then_inc(S("gstep"), 1)
                dve.wait_ge(S("gstep"), nth("gstep"))
                dve.scalar_tensor_tensor(out=gk[:], in0=gp[:], scalar=-1.0, in1=nA[:], op0=ALU.mult,
                                                   op1=ALU.mult).then_inc(S("gk"), 1)
                dve.wait_ge(S("gk"), nth("gk"))
                for g in range(CB // GH):
                    if g == NG + 1:
                        dve.wait_ge(S("silu"), NG)
                        dve.tensor_tensor(sq[:], cv[:, 0:NH], cv[:, 0:NH], ALU.mult).then_inc(S("sq"), 1)
                        dve.wait_ge(S("sq"), nth("sq"))
                    dve.wait_ge(S("tap"), g + 1)
                    for j in range(TAPS - 1):
                        for b in range(g * GH, (g + 1) * GH):
                            ins = dve.scalar_tensor_tensor(out=cv[:, b], in0=xpad[:, b, j:j + P],
                                                           scalar=convw[:, b, j:j + 1], in1=cv[:, b],
                                                           op0=ALU.mult, op1=ALU.add)
                        ins.then_inc(S("conv" if j == TAPS - 2 else "convstep"), 1)
                        dve.wait_ge(S("conv" if j == TAPS - 2 else "convstep"), nth("conv" if j == TAPS - 2 else "convstep"))
                dve.wait_ge(S("rs"), NG)
                dve.tensor_tensor(cv[:, KB:2 * KB], cv[:, KB:2 * KB], rs[:, KB:], ALU.mult).then_inc(S("kn"), 1)
                dve.wait_ge(S("kn"), nth("kn"))
                kv_ = kz[:].rearrange("p (b e) t -> p b e t", e=2)
                for e in range(2):
                    dve.tensor_scalar(kv_[:, :, e], cv[:, KB:2 * KB], half[:, e:e + 1], None, ALU.mult).then_inc(S("kz"), 1)
                    dve.wait_ge(S("kz"), nth("kz"))
                dve.scalar_tensor_tensor(out=cv[:, 0:KB], in0=cv[:, 0:KB], scalar=DK ** -0.5,
                                                   in1=rs[:, 0:KB], op0=ALU.mult, op1=ALU.mult).then_inc(S("qn"), 1)
                dve.wait_ge(S("qn"), nth("qn"))
                dve.wait_ge(S("Dm"), 2)
                for g in range(NG):
                    dve.wait_ge(S("KK"), g + 1)
                    dve.tensor_tensor(A[:, hb(g)], b4(g), Dm[:, hb(g)], ALU.mult).then_inc(S("A"), 1)
                    dve.wait_ge(S("A"), nth("A"))
                for g in range(NG):
                    dve.wait_ge(S("A"), g + 1)
                    dve.tensor_tensor(X[:, hb(g)], A[:, hb(g)], bc(pair[:], 1, [P, GH, P]), ALU.mult).then_inc(S("XU"), 1)
                    dve.wait_ge(S("XU"), nth("XU"))
                    dve.tensor_tensor(X[:, hb(g)], bc(ident[:], 1, [P, GH, P]), X[:, hb(g)], ALU.subtract).then_inc(S("XU"), 1)
                    dve.wait_ge(S("XU"), nth("XU"))
                dve.wait_ge(S("DT"), 1)
                for g in range(NG):
                    dve.wait_ge(S("KQ"), g + 1)
                    dve.tensor_tensor(at[:, hb(g)], b4(5 + g), DT[:, hb(g)], ALU.mult).then_inc(S("at"), 1)
                    dve.wait_ge(S("at"), nth("at"))
                for g in range(NG):
                    dve.wait_ge(S("AT"), g + 1)
                    dve.tensor_tensor(U[:, hb(g)], AT[:, hb(g)], bc(level[:, 0], 1, [P, GH, P]), ALU.mult).then_inc(S("XU"), 1)
                    dve.wait_ge(S("XU"), nth("XU"))
                    dve.tensor_tensor(U[:, hb(g)], bc(ident[:], 1, [P, GH, P]), U[:, hb(g)], ALU.subtract).then_inc(S("XU"), 1)
                    dve.wait_ge(S("XU"), nth("XU"))
                for g in range(NG):
                    dve.wait_ge(S("vT"), g + 1)
                    dve.tensor_tensor(bv[:, hb(g)], b4(5 + g), bc(beta[:, hb(g)], 2, [P, GH, P]), ALU.mult).then_inc(S("bv"), 1)
                    dve.wait_ge(S("bv"), nth("bv"))
                for n in range(1, len(LEVELS) - 1):
                    for g in range(NG):
                        dve.wait_ge(S("XZ"), NG * (n - 1) + g + 1)
                        dve.tensor_tensor(X[:, hb(g)], X[:, hb(g)], b4(3 + g), ALU.subtract).then_inc(S("X"), 1)
                        dve.wait_ge(S("ZU"), NG * (n - 1) + g + 1)
                        dve.tensor_tensor(U[:, hb(g)], U[:, hb(g)], b4(g), ALU.subtract).then_inc(S("U"), 1)
                for g in range(NG):
                    dve.wait_ge(S("dmm"), g + 1)
                    dve.wait_ge(S("w"), g + 1)
                    dve.tensor_tensor(dl[:, hb(g)], w[:, hb(g)], b4(g), ALU.subtract).then_inc(S("dl"), 1)
                    dve.wait_ge(S("dl"), nth("dl"))
                dve.wait_ge(S("sgw"), 1)
                for g in range(NG):
                    dve.wait_ge(S("omm"), g + 1)
                    dve.tensor_tensor(oh[:, hb(g)], b4(3 + g), sg[:, hb(g)], ALU.mult).then_inc(S("og"), 1)
                for g in range(NG):
                    dve.wait_ge(S("og"), g + 1)
                    dve.wait_ge(S("rms"), 2 * (g + 1))
                    dve.tensor_tensor(oh[:, hb(g)], oh[:, hb(g)], bc(ss[:, hb(g)], 2, [P, GH, DV]), ALU.mult).then_inc(S("on"), 1)
                dve.wait_ge(S("x2_psum"), 1)
                dve.tensor_tensor(xres[:], xres[:], bank[6][:, 0:D], ALU.add).then_inc(S("x2"), 1)
                dve.wait_ge(S("x2"), nth("x2"))

            @block.scalar
            def _(act):
                act.wait_ge(S("o0T_psum"), 1)
                act.copy(oT0[:].rearrange("p k t -> p (k t)"), bank[7][:, 0:D]).then_inc(S("o0T"), 1)
                for w_ in range(3):
                    act.wait_ge(S("WT1_psum"), w_ + 1)
                    act.copy(WT1[:, w_].rearrange("p k o -> p (k o)"), bank[3 + w_][:]).then_inc(S("WT1"), 1)
                ln_act(act, "ln1", 7)
                act.wait_ge(S("gw_in"), 16 * GW_LOADS)
                act.activation(nA[:], nA[:], ACT.Exp).then_inc(S("nA"), 1)
                act.wait_ge(S("ge_in"), 1)
                act.activation(ge[:], ge[:], ACT.Exp).then_inc(S("ge"), 1)
                act.wait_ge(S("ge1"), 1)
                act.activation(ge[:, 0:NH], ge[:, 0:NH], ACT.Ln).then_inc(S("softplus"), 1)
                act.wait_ge(S("xpad_zero"), 1)
                for g in range(CB // GH):
                    act.wait_ge(S("cproj"), g + 1)
                    act.copy(xpad[:, g * GH:(g + 1) * GH, TAPS - 1:], b4(g))
                    for j in range(GH):
                        b = g * GH + j
                        ins = act.activation(cv[:, b], bank[g][:, j * P:(j + 1) * P], ACT.Copy,
                                             scale=convw[:, b, TAPS - 1:TAPS])
                    ins.then_inc(S("tap"), 1)
                for k, b in enumerate((6, 0, 1)):
                    act.wait_ge(S("gproj"), k + 1)
                    act.activation(sg[:, hb(k)], b4(b), ACT.Silu).then_inc(S("sg"), 1)
                for g in range(NG):
                    act.wait_ge(S("conv"), g + 1)
                    act.activation(cv[:, g * GH:(g + 1) * GH], cv[:, g * GH:(g + 1) * GH], ACT.Silu).then_inc(S("silu"), 1)
                for k, b in enumerate((5, 6, 0, 2, 3, 4)):
                    act.wait_ge(S("dsum"), k + 1)
                    dst = (Dm, DT)[k // NG]
                    act.activation(dst[:, hb(k % NG)], b4(b), ACT.Exp).then_inc(S("dexp"), 1)
                for g in range(NG):
                    act.wait_ge(S("n2"), g + 1)
                    act.activation(rs[:, hb(g)], b4(1 + g), ACT.Ln, bias=eps6[:, 0:1]).then_inc(S("lnn"), 1)
                for g in range(NG):
                    act.wait_ge(S("lnn"), g + 1)
                    act.activation(rs[:, hb(g)], rs[:, hb(g)], ACT.Exp, scale=-0.5).then_inc(S("rs"), 1)
                for g in range(NG, CB // GH):
                    act.wait_ge(S("conv"), g + 1)
                    act.activation(cv[:, g * GH:(g + 1) * GH], cv[:, g * GH:(g + 1) * GH], ACT.Silu).then_inc(S("silu"), 1)
                for g in range(NG):
                    act.wait_ge(S("AT_psum"), g + 1)
                    act.copy(AT[:, hb(g)], b4((3, 4, 3)[g])).then_inc(S("AT"), 1)
                for n in range(1, len(LEVELS) - 1):
                    for g in range(NG):
                        act.wait_ge(S("Zmm"), NG * (n - 1) + g + 1)
                        act.copy(Z[:, hb(g)], b4(g)).then_inc(S("Z"), 1)
                for g in range(NG):
                    act.wait_ge(S("wmm"), g + 1)
                    act.copy(w[:, hb(g)], b4(3 + g)).then_inc(S("w"), 1)
                for g in range(NG):
                    act.wait_ge(S("zmm"), g + 1)
                    act.copy(Z[:, hb(g)], b4(g)).then_inc(S("z"), 1)
                for g in range(NG):
                    act.wait_ge(S("og"), g + 1)
                    for j in range(GH):
                        h = g * GH + j
                        ins = act.activation(Z[:, h], bank[3 + g][:, j * P:(j + 1) * P], ACT.Square,
                                             accum_out=ss[:, h:h + 1])
                    ins.then_inc(S("ss"), 1)
                for g in range(NG):
                    act.wait_ge(S("oT_psum"), g + 1)
                    act.copy(oT[:, hb(g)], b4(g)).then_inc(S("oT"), 1)

            @block.tensor
            def _(pe):
                def heads(g, b, lhs, rhs, name, transpose=False):
                    for j in range(GH):
                        h = g * GH + j
                        o = bank[b][:, j * P:(j + 1) * P]
                        ins = pe.transpose(o, lhs(h), ident[:]) if transpose else \
                            pe.matmul(o, lhs(h), rhs(h), start=True, stop=True)
                    ins.then_inc(S(name), 1)

                pe.wait_ge(S("o0"), 1)
                for k in range(DC):
                    ins = pe.transpose(bank[7][:, k * P:(k + 1) * P], o0[:, k * P:(k + 1) * P], ident[:])
                ins.then_inc(S("o0T_psum"), 1)
                pe.wait_ge(S("o0T"), 1)
                pe.wait_ge(S("wo0_in"), 16)
                for k in range(DC):
                    ins = pe.matmul(bank[6][:, 0:D], oT0[:, k, :], Wo0[:, k, :], start=(k == 0), stop=(k == DC - 1))
                ins.then_inc(S("x1_psum"), 1)
                pe.wait_ge(S("raw1_in"), 48)
                for w_ in range(3):
                    for k in range(DC):
                        for c in range(DC):
                            ins = pe.transpose(bank[3 + w_][:, (k * DC + c) * P:(k * DC + c + 1) * P],
                                               raw1[:, w_, c, k * P:(k + 1) * P], ident[:])
                    ins.then_inc(S("WT1_psum"), 1)
                ln_pe(pe, "ln1", 7)
                pe.wait_ge(S("ln1_hT"), 1)
                pe.wait_ge(S("gw_in"), 16 * GW_LOADS)
                for k in range(DC):
                    ins = pe.matmul(bank[7][:, 0:2 * NH], hT[:, k, :], Wgb[:, k, :], start=(k == 0), stop=(k == DC - 1))
                ins.then_inc(S("gates_psum"), 1)
                for g in range(CB // GH):
                    if g >= 3:
                        pe.wait_ge(S("WT1"), g - 2)
                    for j in range(GH):
                        b = g * GH + j
                        for k in range(DC):
                            ins = pe.matmul(bank[g][:, j * P:(j + 1) * P], Wc[:, k, b * P:(b + 1) * P], hT[:, k, :],
                                            start=(k == 0), stop=(k == DC - 1))
                    ins.then_inc(S("cproj"), 1)
                for g, b in enumerate((6, 0, 1)):
                    if b != 6:
                        pe.wait_ge(S("tap"), b + 1)
                    for k in range(DC):
                        ins = pe.matmul(bank[b][:], hT[:, k, :], Wg[:, k, g * 512:(g + 1) * 512],
                                        start=(k == 0), stop=(k == DC - 1))
                    ins.then_inc(S("gproj"), 1)
                pe.wait_ge(S("R"), 2)
                pe.wait_ge(S("tap"), CB // GH)
                pe.wait_ge(S("sg"), 2)
                for g, b in enumerate((5, 6, 0)):
                    pe.matmul(bank[b][:], tri[:], R[:, 1, hb(g)].rearrange("p h t -> p (h t)"), start=True,
                              stop=True).then_inc(S("dsum"), 1)
                for g, b in enumerate((2, 3, 4)):
                    pe.matmul(bank[b][:], below[:], R[:, 0, hb(g)].rearrange("p h t -> p (h t)"), start=True,
                              stop=True).then_inc(S("dsum"), 1)
                pe.wait_ge(S("sq"), 1)
                pe.wait_ge(S("dexp"), 6)
                pe.wait_ge(S("sg"), 3)
                for g in range(NG):
                    pe.matmul(bank[1 + g][:], blk64[:], sq[:, hb(g)].rearrange("p h t -> p (h t)"), start=True,
                              stop=True).then_inc(S("n2"), 1)
                pe.wait_ge(S("kz"), 2)
                kn = lambda h: cv[:, KB + h // 2]
                for g in range(NG):
                    if some(g):
                        pe.wait_ge(S("rs"), g)
                    heads(g, g, lambda h: kz[:, h], kn, "KK")
                for g in range(NG):
                    pe.wait_ge(S("A"), g + 1)
                    if some(g - 1):
                        pe.wait_ge(S("AT"), g - 1)
                    heads(g, (3, 4, 3)[g], lambda h: A[:, h], None, "AT_psum", True)
                pe.wait_ge(S("qn"), 1)
                for g in range(NG):
                    heads(g, 5 + g, lambda h: kz[:, h], lambda h: cv[:, h // 2], "KQ")
                pe.wait_ge(S("silu"), CB // GH)
                for g in range(NG):
                    pe.wait_ge(S("at"), g + 1)
                    heads(g, 5 + g, lambda h: cv[:, 2 * KB + h], None, "vT", True)
                pe.wait_ge(S("AT"), NG)
                for n in range(1, len(LEVELS) - 1):
                    pe.wait_ge(S("Am"), n)
                    for g in range(NG):
                        pe.wait_ge(S("XU"), 2 * NG + 2 * (g + 1))
                        if some(NG * (n - 2) + g + 1):
                            pe.wait_ge(S("X"), NG * (n - 2) + g + 1)
                        if some(NG * (n - 2) + g + 1):
                            pe.wait_ge(S("U"), NG * (n - 2) + g + 1)
                        heads(g, g, lambda h: Am[:, n % 2, h], lambda h: X[:, h], "Zmm")
                    for g in range(NG):
                        pe.wait_ge(S("Z"), NG * (n - 1) + g + 1)
                        pe.wait_ge(S("bv"), 1)
                        heads(g, 3 + g, lambda h: U[:, h], lambda h: Z[:, h], "XZ")
                        heads(g, g, lambda h: Z[:, h], lambda h: U[:, h], "ZU")
                nl = len(LEVELS) - 2
                for g in range(NG):
                    pe.wait_ge(S("U"), NG * (nl - 1) + g + 1)
                    pe.wait_ge(S("X"), NG * (nl - 1) + g + 1)
                    pe.wait_ge(S("bv"), g + 1)
                    heads(g, 3 + g, lambda h: U[:, h], lambda h: bv[:, h], "wmm")
                pe.wait_ge(S("Am"), nl + 1)
                for g in range(NG):
                    pe.wait_ge(S("w"), g + 1)
                    heads(g, g, lambda h: Am[:, (nl + 1) % 2, h], lambda h: w[:, h], "zmm")
                for g in range(NG):
                    pe.wait_ge(S("z"), g + 1)
                    heads(g, g, lambda h: U[:, h], lambda h: Z[:, h], "dmm")
                for g in range(NG):
                    pe.wait_ge(S("dl"), g + 1)
                    heads(g, 3 + g, lambda h: at[:, h], lambda h: dl[:, h], "omm")
                for g in range(NG):
                    pe.wait_ge(S("on"), g + 1)
                    heads(g, g, lambda h: oh[:, h], None, "oT_psum", True)
                for g in range(NG):
                    pe.wait_ge(S("oT"), g + 1)
                    for h in range(g * GH, (g + 1) * GH):
                        ins = pe.matmul(bank[6][:, 0:D], oT[:, h], Wo[:, h], start=(h == 0), stop=(h == NH - 1))
                ins.then_inc(S("x2_psum"), 1)
        gd.close()
        xa.close()
        gw.close()

        def experts(tag, router, router_rows, router_bias, expert_bias, top, last, loads=None, clears=None):
            mo = ExitStack()
            eT = sb(mo, "eT" + tag, [P, DC, E, D])
            rwT = sb(mo, "rwT" + tag, [P, DC, E])
            rw = sb(mo, "rw" + tag, [E, D])
            rb = sb(mo, "rb" + tag, [P, E])
            eb = sb(mo, "eb" + tag, [E, D])
            order = sb(mo, "order" + tag, [P, E])
            lg = sb(mo, "lg" + tag, [P, E])
            lx = sb(mo, "lx" + tag, [P, E])
            best = sb(mo, "best" + tag, [P, 1])
            pick = sb(mo, "pick" + tag, [P, E])
            eq = sb(mo, "eq" + tag, [P, E])
            chosen = sb(mo, "chosen" + tag, [P, E])
            ex = sb(mo, "ex" + tag, [P, E])
            total = sb(mo, "total" + tag, [P, 1])
            wt = sb(mo, "wt" + tag, [P, E])
            wtT = sb(mo, "wtT" + tag, [E, P])
            n = lambda name: tag + name

            def product(pe, g):
                pe.wait_ge(S(n("eT")), 2 * g + 2)
                b = (5, 6, 7, 0)[g]
                for k in range(DC):
                    ins = pe.matmul(bank[b][:], hT[:, k, :], eT[:, k, 2 * g:2 * g + 2].rearrange("p e o -> p (e o)"),
                                    start=(k == 0), stop=(k == DC - 1))
                ins.then_inc(S(n("y")), 1)

            with nc.Block() as block:
                @block.sync
                def _(sp):
                    if router_rows:
                        sp.dma_start(rw[:], router).then_inc(S(n("rw_in")), 16)
                    else:
                        sp.dma_start(rwT[:], wcols(router)).then_inc(S(n("rw_in")), 16)
                    sp.dma_start(rb[:], router_bias.partition_broadcast(P)).then_inc(S(n("rb_in")), 16)
                    sp.dma_start(eb[:], expert_bias).then_inc(S(n("eb_in")), 16)
                    if loads:
                        loads(sp)
                    if last:
                        sp.wait_ge(S(n("x")), 1)
                        sp.dma_start(out.rearrange("b q d -> (b q) d"), xres[:]).then_inc(S("out"), 16)
                        sp.wait_ge(S("out"), 16)

                @block.gpsimd
                def _(pool):
                    for e in range(E):
                        pool.memset(order[:, e:e + 1], float(E - e)).then_inc(S(n("order")), 1)
                    ln_pool(pool, n("ln"))
                    if clears:
                        clears(pool)

                @block.tensor
                def _(pe):
                    def expert(i):
                        if i >= 2:
                            pe.wait_ge(S(n("eT")), i - 1)
                        for k in range(DC):
                            for c in range(DC):
                                ins = pe.transpose(bank[3 + i % 2][:, (k * DC + c) * P:(k * DC + c + 1) * P],
                                                   ew[:, i * DC + c, k * P:(k + 1) * P], ident[:])
                        ins.then_inc(S(n("eT_psum")), 1)

                    pe.wait_ge(S(tag + "ew_in" if last else "ew0_in"), 16)
                    expert(0)
                    expert(1)
                    ln_pe(pe, n("ln"), 0)
                    pe.wait_ge(S(n("rw_in")), 16)
                    if router_rows:
                        for k in range(DC):
                            ins = pe.transpose(bank[1][:, k * E:(k + 1) * E], rw[:, k * P:(k + 1) * P], ident[0:E, 0:E])
                        ins.then_inc(S(n("rwT_psum")), 1)
                        pe.wait_ge(S(n("rwT")), 1)
                    pe.wait_ge(S(n("ln_hT")), 1)
                    for k in range(DC):
                        ins = pe.matmul(bank[2][:, 0:E], hT[:, k, :], rwT[:, k, :], start=(k == 0), stop=(k == DC - 1))
                    ins.then_inc(S(n("logits_psum")), 1)
                    for i in range(2, E):
                        expert(i)
                        if i % 2:
                            product(pe, i // 2 - 1)
                    product(pe, E // 2 - 1)
                    pe.wait_ge(S(n("wt")), 1)
                    pe.transpose(bank[1][0:E, 0:P], wt[:], ident[:]).then_inc(S(n("wtT_psum")), 1)
                    pe.wait_ge(S(n("wtT")), 1)
                    pe.wait_ge(S(n("eb_in")), 16)
                    pe.matmul(bank[2][:, 0:D], wtT[:], eb[:], start=True, stop=True).then_inc(S(n("bias_psum")), 1)

                @block.scalar
                def _(act):
                    def expert(i):
                        act.wait_ge(S(n("eT_psum")), i + 1)
                        act.copy(eT[:, :, i, :], bank[3 + i % 2][:].rearrange("p (k o) -> p k o", k=DC)
                                 ).then_inc(S(n("eT")), 1)

                    expert(0)
                    expert(1)
                    if router_rows:
                        act.wait_ge(S(n("rwT_psum")), 1)
                        act.copy(rwT[:].rearrange("p k e -> p (k e)"), bank[1][:, 0:DC * E]).then_inc(S(n("rwT")), 1)
                    ln_act(act, n("ln"), 0)
                    for i in range(2, E):
                        expert(i)
                        if i == 2:
                            act.wait_ge(S(n("shifted")), 1)
                            act.activation(ex[:], lx[:], ACT.Exp).then_inc(S(n("ex")), 1)
                    act.wait_ge(S(n("wtT_psum")), 1)
                    act.copy(wtT[:], bank[1][0:E, 0:P]).then_inc(S(n("wtT")), 1)

                @block.vector
                def _(dve):
                    ln_dve(dve, n("ln"))
                    dve.wait_ge(S(n("rb_in")), 16)
                    dve.wait_ge(S(n("logits_psum")), 1)
                    dve.tensor_tensor(lg[:], bank[2][:, 0:E], rb[:], ALU.add).then_inc(S(n("step")), 1)
                    dve.wait_ge(S(n("step")), nth(n("step")))
                    dve.tensor_reduce(best[:], lg[:], AX.X, ALU.max).then_inc(S(n("step")), 1)
                    dve.wait_ge(S(n("step")), nth(n("step")))
                    dve.tensor_scalar(lx[:], lg[:], best[:, 0:1], None, ALU.subtract).then_inc(S(n("shifted")), 1)
                    dve.wait_ge(S(n("shifted")), nth(n("shifted")))
                    dve.wait_ge(S(n("order")), E)
                    for r in range(top):
                        if r:
                            dve.scalar_tensor_tensor(out=lg[:], in0=pick[:], scalar=LOWEST, in1=lg[:], op0=ALU.mult,
                                                         op1=ALU.add).then_inc(S(n("step")), 1)
                            dve.wait_ge(S(n("step")), nth(n("step")))
                            dve.tensor_reduce(best[:], lg[:], AX.X, ALU.max).then_inc(S(n("step")), 1)
                            dve.wait_ge(S(n("step")), nth(n("step")))
                        dve.tensor_scalar(eq[:], lg[:], best[:, 0:1], None, ALU.is_ge).then_inc(S(n("step")), 1)
                        dve.wait_ge(S(n("step")), nth(n("step")))
                        dve.tensor_tensor(eq[:], eq[:], order[:], ALU.mult).then_inc(S(n("step")), 1)
                        dve.wait_ge(S(n("step")), nth(n("step")))
                        dve.tensor_reduce(best[:], eq[:], AX.X, ALU.max).then_inc(S(n("step")), 1)
                        dve.wait_ge(S(n("step")), nth(n("step")))
                        dve.tensor_scalar(pick[:], eq[:], best[:, 0:1], None, ALU.is_ge).then_inc(S(n("step")), 1)
                        dve.wait_ge(S(n("step")), nth(n("step")))
                        if r:
                            dve.tensor_tensor(chosen[:], chosen[:], pick[:], ALU.add).then_inc(S(n("step")), 1)
                            dve.wait_ge(S(n("step")), nth(n("step")))
                        else:
                            dve.tensor_copy(chosen[:], pick[:]).then_inc(S(n("step")), 1)
                            dve.wait_ge(S(n("step")), nth(n("step")))
                    dve.wait_ge(S(n("ex")), 1)
                    dve.tensor_tensor(wt[:], ex[:], chosen[:], ALU.mult).then_inc(S(n("step")), 1)
                    dve.wait_ge(S(n("step")), nth(n("step")))
                    dve.tensor_reduce(total[:], ex[:] if top == 1 else wt[:], AX.X, ALU.add).then_inc(S(n("step")), 1)
                    dve.wait_ge(S(n("step")), nth(n("step")))
                    dve.reciprocal(total[:], total[:]).then_inc(S(n("step")), 1)
                    dve.wait_ge(S(n("step")), nth(n("step")))
                    dve.tensor_scalar(wt[:], wt[:], total[:, 0:1], None, ALU.mult).then_inc(S(n("wt")), 1)
                    dve.wait_ge(S(n("wt")), nth(n("wt")))
                    for e in range(E):
                        dve.wait_ge(S(n("y")), e // 2 + 1)
                        dve.scalar_tensor_tensor(out=xres[:], in0=bank[(5, 6, 7, 0)[e // 2]][:, (e % 2) * D:(e % 2 + 1) * D],
                                                     scalar=wt[:, e:e + 1], in1=xres[:], op0=ALU.mult, op1=ALU.add).then_inc(S(n("step")), 1)
                        dve.wait_ge(S(n("step")), nth(n("step")))
                    dve.wait_ge(S(n("bias_psum")), 1)
                    dve.tensor_tensor(xres[:], xres[:], bank[2][:, 0:D], ALU.add).then_inc(S(n("x")), 1)
                    dve.wait_ge(S(n("x")), nth(n("x")))
            mo.close()

        lw = ExitStack()
        lraw = sb(lw, "lraw", [P, 10, D])
        xb = ExitStack()
        acc1 = sb(xb, "acc1", [P, H1, D1 + 1])
        bv1 = sb(xb, "bv1", [P, D])
        rd1 = sb(xb, "rd1", [P, H1])
        o1 = sb(xb, "o1", [P, D])
        l1 = ExitStack()
        VW = H1 * (D1 + 1) + D1 - 1
        qrows = sb(l1, "qrows", [KONES, 2, H1, P], BF16)
        krows = sb(l1, "krows", [KONES, 2, H1, CH], BF16)
        v1 = sb(l1, "v1", [P, 2, CT, VW])
        b1 = sb(l1, "b1", [P, 2, DC])
        ctx1 = sb(l1, "ctx1", [P, 2, CT, D])
        ctxT1 = sb(l1, "ctxT1", [P, 2, DC, CH])
        kf = sb(l1, "kf", [P, 2, HCH])
        kt3 = sb(l1, "kt3", [P, 3, DC, CH], BF16)
        mx1 = sb(l1, "mx1", [P, H1, 2])
        top1 = sb(l1, "top1", [P, H1])
        run1 = sb(l1, "run1", [P, 2, H1])
        dm1 = sb(l1, "dm1", [P, 2, H1])
        f1 = sb(l1, "f1", [P, 2, H1])
        HP = 32
        neg1 = sb(l1, "neg1", [P, H1])
        n31 = sb(l1, "n31", [P, 3, HP], BF16)
        n3T1 = sb(l1, "n3T1", [3 * HP, 2, P], BF16)
        p1 = sb(l1, "p1", [P, 4, GH * P])
        ots1 = sb(l1, "ots1", [P, GH * P])
        kscr = nc.dram_tensor("kscr", (2, 3, D, CH), BF16).ap()
        qscr = nc.dram_tensor("qscr", (3, D, P), BF16).ap()

        q3 = sb(l1, "q3", [P, 3, DC, P], BF16)

        qf = sb(l1, "qf", [P, DC, P])

        def l1_loads(sp):
            for c in range(2):
                sp.dma_start(ctx1[:, c], chunk_of(c)).then_inc(S(f"ctx1_{c}"), 16)
            for k, name in enumerate(("L1_xattn_bq", "L1_xattn_bk")):
                sp.dma_start(b1[:, k, :], a[name].rearrange("(c p) -> p c", c=DC),
                             allow_slow_non_contiguous=True).then_inc(S("b1_in"), 16)
            sp.dma_start(bv1[:], a["L1_xattn_bv"].partition_broadcast(P)).then_inc(S("bv1_in"), 16)
            sp.dma_start(krows[KROWS:KONES].rearrange("p s h (r c) -> p (s h r) c", c=P),
                         onesb[KROWS:KONES].unsqueeze(1).to_broadcast([3, 2 * H1 * CT, P])
                         ).then_inc(S("krows_ones"), 16)

        def l1_clears(pool):
            v = v1[:].rearrange("p s t w -> p (s t) w")
            pool.memset(v[:, :, 0:H1 * (D1 + 1)].rearrange("p t (h d) -> p t h d", h=H1)[:, :, :, D1],
                        1.0).then_inc(S("v1_ones"), 1)
            pool.memset(v[:, :, H1 * (D1 + 1):], 0.0).then_inc(S("v1_ones"), 1)
            pool.memset(n31[:], 0.0).then_inc(S("n31_zero"), 1)
            pool.memset(acc1[:], 0.0).then_inc(S("acc1"), 1)
            pool.memset(run1[:], LOWEST).then_inc(S("run1_lowest"), 1)

        renew(("ew0_in",))
        experts("moe0", a["L0_ffn_router_w"], True, a["L0_ffn_router_b"], a["L0_ffn_expert_b"], 1, False,
                l1_loads, l1_clears)

        XP1, KV1, SM1, ST1, OT1, OB1 = (0, 2), 1, (2, 3, 0), (4, 5), 6, 7
        UNITS = CT * H1 // GH
        PLAN1 = (
            (("T0",), ("T1",)), (("T2",), ("V0",)), (("T3",), ()), (("V1",), ()), (("S0",), ("S1",)),
            (("S2", "K0", "S3"), ("S4",)), (("S5",), ("S6",)), (("S7",), ("S8",)), (("K1", "S9"), ("S10",)),
            (("S11",), ("S12",)), (("S13",), ("S14",)), (("K2", "S15"), ("S16",)), (("S17",), ("S18",)),
            (("S19",), ("S20",)), (("K3", "S21"), ("S22",)), (("S23",), ("S24",)), (("S25",), ("S26",)),
            ((), ("S27",)), ((), ("S28",)), ((), ("S29",)), ((), ("S30",)), (("S31", "V2"), ()), ((), ()),
            (("M0",), ()), (("V3",), ()), ((), ()), ((), ()), ((), ()))

        def early(op):
            return op[0] in "TK"

        ALL1 = tuple(op for before, after in PLAN1 for op in before + after)

        PRO1 = []
        for ops in ("T00 T10 K00 L00 T20 K10 Q00 T30 K20 T01 K30 T11 V00 T21 V10 T31 V20 V30 K01",
                    *(" ".join(f"S{8 * j + i}0" for i in range(8)) + (f" K{j + 1}1" if j < 3 else "") for j in range(4)),
                    "M00"):
            for op in ops.split():
                last_kv = [done for done in PRO1 if done[0][0] in "KV"][-1:]
                PRO1.append((op[:-1], int(op[-1]), last_kv[0][:2] if last_kv else None))

        def steps1(eng, step):
            step(0, 0, 0, True, True)
            with eng.Fori(0, (NCH - 4) // 2) as i:
                step(i * 2 + 1, 1, i, True, True)
                step(i * 2 + 2, 0, i + 1, True, True)
            step(NCH - 3, 1, (NCH - 4) // 2, True, True)
            step(NCH - 2, 0, (NCH - 2) // 2, False, True)
            step(NCH - 1, 1, (NCH - 2) // 2, False, False)

        def sides(side, ops, c, s, n, two, one):
            for op in ops:
                if early(op):
                    if two:
                        side(op, c + 2, s, n + 1)
                elif one:
                    side(op, c + 1, 1 - s, n + s)

        def take_values(eng, copy, c, s, k):
            t0, nt = VG[k]
            eng.wait_ge(S("vmm1"), 4 * c + k + 1)
            if some(UNITS * (c - 1)):
                eng.wait_ge(S("pv1"), UNITS * (c - 1))
            copy(v1[:, s, t0:t0 + nt, 0:H1 * (D1 + 1)].rearrange("p t (h d) -> p t h d", h=H1)[:, :, :, 0:D1],
                 bank[KV1][:, 0:nt * D].rearrange("p (t h d) -> p t h d", t=nt, h=H1)).then_inc(S("vread1"), 1)

        def parts(eng, c, k):
            half, b = k // 2, k % 2
            cols = slice(half * HCH, (half + 1) * HCH)
            eng.wait_ge(S("kread1"), 4 * c + k + 1)
            eng.tensor_tensor(kt3[:, 1, b, cols], kf[:, k % 2, :], kt3[:, 0, b, cols], ALU.subtract).then_inc(S("k21"), 1)
            eng.wait_ge(S("k21"), 4 * c + k + 1)
            eng.tensor_tensor(kf[:, k % 2, :], kf[:, k % 2, :], kt3[:, 0, b, cols], ALU.subtract).then_inc(S("kr1"), 1)
            eng.wait_ge(S("kr1"), 4 * c + k + 1)
            eng.tensor_tensor(kt3[:, 2, b, cols], kf[:, k % 2, :], kt3[:, 1, b, cols], ALU.subtract).then_inc(S("k31"), 1)

        with nc.Block() as block:
            @block.sync
            def _(sp):
                def load(c, s):
                    if some(4 * (c - 1)):
                        sp.wait_ge(S("xp1"), 4 * (c - 1))
                    sp.dma_start(ctx1[:, s], chunk_of(c)).then_inc(S(f"ctx1_{s}"), 16)

                def store(c, s, n):
                    sp.wait_ge(S("k31"), 4 * (c + 1))
                    sp.dma_start(kscr[s].rearrange("k (b p) m -> p (k b) m", b=DC),
                                 kt3[:].rearrange("p k b m -> p (k b) m")).then_inc(S(f"kscr_{s}"), 16)

                def gather(c, s, n):
                    used = UNITS * (c - 1)
                    stored = 16 * (n + 1)
                    if not isinstance(used, int):
                        used, stored = sp.snap(used), sp.snap(stored)
                    sp.wait_ge(S(f"kscr_{s}"), stored)
                    if some(used):
                        sp.wait_ge(S("st1"), used)
                    for j in range(NJ):
                        sp.dma_start(krows[j * D1:(j + 1) * D1, s],
                                     kscr[s, K_TERM[j]].rearrange("(h d) m -> d h m", d=D1)
                                     ).then_inc(S(f"krows_{s}"), 16)

                def rows(c, s):
                    sp.wait_ge(S("n3T1"), c + 1)
                    for k in range(3):
                        sp.dma_start(qrows[KROWS + k:KROWS + k + 1, s],
                                     n3T1[k * HP:k * HP + H1, s, :]).then_inc(S(f"mrow1_{s}"), 16)

                sp.wait_ge(S("q3"), 3)
                sp.dma_start(qscr.rearrange("k (b p) q -> p (k b) q", b=DC),
                             q3[:].rearrange("p k b q -> p (k b) q")).then_inc(S("qscr"), 16)
                sp.wait_ge(S("qscr"), 16)
                for j in range(NJ):
                    sp.dma_start(qrows[j * D1:(j + 1) * D1, 0],
                                 qscr[Q_TERM[j]].rearrange("(h d) q -> d h q", d=D1)).then_inc(S("qrows_in"), 16)
                for half, name in enumerate(("first", "0")):
                    cols = slice(half * HCH, (half + 1) * HCH)
                    sp.wait_ge(S("k31"), 2 * (half + 1))
                    sp.dma_start(kscr[0, :, :, cols].rearrange("k (b p) m -> p (k b) m", b=DC),
                                 kt3[:, :, :, cols].rearrange("p k b m -> p (k b) m")).then_inc(S("kscr_" + name), 16)
                    sp.wait_ge(S("kscr_" + name), 16)
                    for j in range(NJ):
                        sp.dma_start(krows[j * D1:(j + 1) * D1, 0, :, cols],
                                     kscr[0, K_TERM[j], :, cols].rearrange("(h d) m -> d h m", d=D1)
                                     ).then_inc(S("krows_" + name), 16)
                sp.wait_ge(S("qrows_in"), 16 * NJ)
                sp.dma_start(qrows[0:KROWS, 1], qrows[0:KROWS, 0]).then_inc(S("qrows_copy"), 16)
                load(2, 0)
                store(1, 1, 0)
                rows(0, 0)
                gather(1, 1, 0)
                sp.dma_start(ew[:], a["L1_ffn_We"].rearrange("e (c p) d -> p (e c) d", p=P)).then_inc(S("moe1ew_in"), 16)
                for k, name in enumerate(("L1_attn_Wqkv", "L1_attn_Wout", "L1_attn_Wgate")):
                    o = (0, 6, 8, 10)
                    sp.dma_start(lraw[:, o[k]:o[k + 1]], wcols(a[name], o[k + 1] - o[k])).then_inc(S("lraw_in"), 16)

                def step(c, s, n, two, one):
                    if one and not (isinstance(c, int) and c == 0):
                        gather(c + 1, 1 - s, n + s)
                    if two and not (isinstance(c, int) and c == NCH - 3):
                        load(c + 3, 1 - s)
                    if two:
                        store(c + 2, s, n + 1)
                    if one:
                        rows(c + 1, 1 - s)
                steps1(sp, step)

            @block.gpsimd
            def _(pool):
                ln_pool(pool, "ln2")
                with pool.Fori(1, NCH) as c:
                    for k in range(4):
                        parts(pool, c, k)

            @block.tensor
            def _(pe):
                def bank_free(last_kv):
                    if last_kv:
                        op, c = last_kv
                        pe.wait_ge(S("kread1" if op[0] == "K" else "vread1"), 4 * c + int(op[1:]) + 1)

                def side(op, c, s, n, last_kv=None):
                    k = int(op[1:])
                    if op == "K0" and last_kv is None:
                        last_kv = ("V1", c - 1)
                    elif op == "V2" and last_kv is None:
                        last_kv = ("K3", min(c + 1, NCH - 1) if isinstance(c, int) else c + 1)
                    elif op[0] in "KV" and last_kv is None:
                        last_kv = (f"{op[0]}{(k - 1) % 4}", c if k else c - 1)
                    if op[0] == "T":
                        if k == 0:
                            pe.wait_ge(S(f"ctx1_{s}"), 16 * n + 16)
                            if some(c - 1):
                                pe.wait_ge(S("n3T1"), c - 1)
                        if some(4 * c + k - 1):
                            pe.wait_ge(S("ctxT1"), 4 * c + k - 1)
                        h, t0, nt = TG[k]
                        for t in range(nt):
                            ins = pe.transpose(bank[XP1[k % 2]][:, t * P:(t + 1) * P], ctx1[:, s, t0 + t, h * P:(h + 1) * P],
                                               ident[:])
                        ins.then_inc(S("xp1"), 1)
                    elif op[0] == "K":
                        half, b = k // 2, k % 2
                        pe.wait_ge(S("ctxT1"), 4 * c + 2 * half + 2)
                        bank_free(last_kv)
                        for i in range(DC):
                            ins = pe.matmul(bank[KV1][:, 0:HCH], WT1[:, 1, i, b * P:(b + 1) * P],
                                            ctxT1[:, s, i, half * HCH:(half + 1) * HCH],
                                            start=(i == 0), stop=(i == DC - 1))
                        ins.then_inc(S("kmm1"), 1)
                    elif op[0] == "S":
                        half, h = k // H1, k % H1
                        first = isinstance(c, int) and c == 0
                        if first and k == 0:
                            pe.wait_ge(S("krows_first"), 16 * NJ)
                            pe.wait_ge(S("qrows_in"), 16 * NJ)
                            pe.wait_ge(S("krows_ones"), 16)
                        if k == (H1 if first else 0):
                            pe.wait_ge(S(f"krows_{s}"), 16 * NJ * (n + 1))
                            if isinstance(c, int) and c == 1:
                                pe.wait_ge(S("qrows_copy"), 16)
                        if k == 0:
                            pe.wait_ge(S("ctxT1"), min(4 * (c + 2), 4 * NCH) if isinstance(c, int) else 4 * (c + 2))
                        if some(2 * H1 * c + max(k - 2, 0)):
                            pe.wait_ge(S("smread1"), 2 * H1 * c + max(k - 2, 0))
                        pe.matmul(bank[SM1[k % 3]][:, 0:HCH], qrows[0:KROWS, s, h, :],
                                  krows[0:KROWS, s, h, half * HCH:(half + 1) * HCH],
                                  start=True, stop=True).then_inc(S("sm1"), 1)
                    elif op[0] == "V":
                        t0, nt = VG[k]
                        bank_free(last_kv)
                        for t in range(nt):
                            for i in range(DC):
                                ins = pe.matmul(bank[KV1][:, t * D:(t + 1) * D],
                                                ctxT1[:, s, i, (t0 + t) * P:(t0 + t + 1) * P], WT1[:, 2, i, :],
                                                start=(i == 0), stop=(i == DC - 1))
                        ins.then_inc(S("vmm1"), 1)
                    elif op[0] == "L":
                        ln_pe(pe, "ln2", 4)
                    elif op[0] == "Q":
                        pe.wait_ge(S("ln2_hT"), 1)
                        for b in range(DC):
                            for i in range(DC):
                                ins = pe.matmul(bank[5][:, b * P:(b + 1) * P], WT1[:, 0, i, b * P:(b + 1) * P],
                                                hT[:, i, :], start=(i == 0), stop=(i == DC - 1))
                        ins.then_inc(S("q1_psum"), 1)
                    else:
                        pe.wait_ge(S("n31"), c + 1)
                        pe.wait_ge(S("ctxT1"), min(4 * (c + 2), 4 * NCH) if isinstance(c, int) else 4 * (c + 2))
                        pe.transpose(bankb[XP1[0]][0:3 * HP, 0:P], n31[:].rearrange("p k h -> p (k h)"),
                                     identb[:]).then_inc(S("mt1"), 1)

                def scores(c, s, n, u):
                    t, j = u // 4, u % 4
                    if u == 0:
                        pe.wait_ge(S(f"mrow1_{s}"), 48 * n + 48)
                    if some(UNITS * c + u - 1):
                        pe.wait_ge(S("exp1"), UNITS * c + u - 1)
                    for i in range(GH):
                        h = GH * j + i
                        ins = pe.matmul(bank[ST1[u % 2]][:, i * P:(i + 1) * P], krows[:, s, h, t * P:(t + 1) * P],
                                        qrows[:, s, h, :], start=True, stop=True)
                    ins.then_inc(S("st1"), 1)

                def values(c, s, u):
                    t, j = u // 4, u % 4
                    pe.wait_ge(S("exp1"), UNITS * c + u + 1)
                    if u == 0:
                        if some(c):
                            pe.wait_ge(S("ots1"), c)
                    if u % 8 == 0:
                        pe.wait_ge(S("vread1"), 4 * c + u // 8 + 1)
                    for i in range(GH):
                        h = GH * j + i
                        ins = pe.matmul(bank[OT1][32 * i:32 * i + 32, j * P:(j + 1) * P],
                                        v1[:, s, t, h * (D1 + 1):h * (D1 + 1) + 32],
                                        p1[:, u % 4, i * P:(i + 1) * P],
                                        start=(u == 0), stop=(t == CT - 1), skip_group_check=True)
                    ins.then_inc(S("pv1"), 1)

                def turn(c):
                    pe.wait_ge(S("ots1"), c + 1)
                    pe.wait_ge(S("acc1"), 2 * c + 1)
                    for j in range(4):
                        ins = pe.transpose(bank[OB1][:, j * P:(j + 1) * P], ots1[:, j * P:(j + 1) * P], ident[:])
                    ins.then_inc(S("ob1"), 1)

                for op, c, last_kv in PRO1:
                    side(op, c, c, 0, last_kv or ())

                def step(c, s, n, two, one):
                    scores(c, s, n, 0)
                    if not (isinstance(c, int) and c == 0):
                        turn(c - 1)
                    for u in range(UNITS):
                        if u + 1 < UNITS:
                            scores(c, s, n, u + 1)
                        sides(side, PLAN1[u][0], c, s, n, two, one)
                        values(c, s, u)
                        sides(side, PLAN1[u][1], c, s, n, two, one)
                steps1(pe, step)
                turn(NCH - 1)

            @block.vector
            def _(dve):
                def side(op, c, s, n):
                    k = int(op[1:])
                    if op[0] == "Q":
                        dve.wait_ge(S("b1_in"), 32)
                        dve.wait_ge(S("q1_psum"), 1)
                        for b in range(DC):
                            dve.tensor_scalar(qf[:, b], bank[5][:, b * P:(b + 1) * P], b1[:, 0, b:b + 1], S1,
                                                        ALU.add, ALU.mult).then_inc(S("qf"), 1)
                            dve.wait_ge(S("qf"), nth("qf"))
                        dve.tensor_copy(q3[:, 0], qf[:]).then_inc(S("q3"), 1)
                        dve.wait_ge(S("q3"), nth("q3"))
                        dve.tensor_tensor(qf[:], qf[:], q3[:, 0], ALU.subtract).then_inc(S("qf"), 1)
                        dve.wait_ge(S("qf"), nth("qf"))
                        dve.tensor_copy(q3[:, 1], qf[:]).then_inc(S("q3"), 1)
                        dve.wait_ge(S("q3"), nth("q3"))
                        dve.tensor_tensor(q3[:, 2], qf[:], q3[:, 1], ALU.subtract).then_inc(S("q3"), 1)
                        dve.wait_ge(S("q3"), nth("q3"))
                    elif op == "V3":
                        take_values(dve, dve.tensor_copy, c, s, k)
                    elif op[0] == "K" and isinstance(c, int) and c == 0:
                        parts(dve, c, k)
                    elif op[0] == "S":
                        half, h = k // H1, k % H1
                        dve.wait_ge(S("sm1"), 2 * H1 * c + k + 1)
                        dve.tensor_reduce(mx1[:, h, half:half + 1], bank[SM1[k % 3]][:, 0:HCH], AX.X,
                                          ALU.max).then_inc(S("smread1"), 1)
                    elif op[0] == "M":
                        running_maximum(dve, "1", c, s, mx1, top1, run1, 2 * H1, 6)
                        dve.tensor_scalar(neg1[:], run1[:, s], -1.0, None, ALU.mult).then_inc(S("maxstep1"), 1)
                        if some(c):
                            dve.wait_ge(S("mt1"), c)
                        dve.tensor_scalar(n31[:, 0, 0:H1], run1[:, s], -1.0, None, ALU.mult).then_inc(S("maxstep1"), 1)
                        if some(c - 1):
                            dve.wait_ge(S("f1"), c - 1)
                        dve.tensor_tensor(dm1[:, s], run1[:, 1 - s], run1[:, s], ALU.subtract).then_inc(S("dm1"), 1)
                        dve.wait_ge(S("maxstep1"), 6 * c + 4)
                        dve.tensor_tensor(neg1[:], neg1[:], n31[:, 0, 0:H1], ALU.subtract).then_inc(S("maxstep1"), 1)
                        dve.wait_ge(S("maxstep1"), 6 * c + 5)
                        dve.tensor_copy(n31[:, 1, 0:H1], neg1[:]).then_inc(S("maxstep1"), 1)
                        dve.wait_ge(S("maxstep1"), 6 * c + 6)
                        dve.tensor_tensor(n31[:, 2, 0:H1], neg1[:], n31[:, 1, 0:H1], ALU.subtract).then_inc(S("n31"), 1)

                def read_out(c):
                    dve.wait_ge(S("pv1"), UNITS * (c + 1))
                    dve.wait_ge(S("acc1"), 2 * c + 1)
                    dve.tensor_copy(ots1[:], bank[OT1][:]).then_inc(S("ots1"), 1)

                def rescale(c, s):
                    dve.wait_ge(S("acc1"), 2 * c + 1)
                    dve.wait_ge(S("f1"), c + 1)
                    dve.tensor_tensor(acc1[:], acc1[:], bc(f1[:, s, :], 2, [P, H1, D1 + 1]), ALU.mult).then_inc(S("acc1"), 1)
                    dve.wait_ge(S("acc1"), 2 * c + 2)
                    dve.wait_ge(S("ob1"), c + 1)
                    dve.tensor_tensor(acc1[:], acc1[:],
                                      bank[OB1][:].rearrange("p (h d) -> p h d", h=H1)[:, :, 0:D1 + 1],
                                      ALU.add).then_inc(S("acc1"), 1)

                ln_dve(dve, "ln2")
                for op, c, _ in PRO1:
                    side(op, c, c, 0)

                def step(c, s, n, two, one):
                    if not (isinstance(c, int) and c == 0):
                        read_out(c - 1)
                        rescale(c - 1, 1 - s)
                    sides(side, ALL1, c, s, n, two, one)
                steps1(dve, step)
                read_out(NCH - 1)
                rescale(NCH - 1, 1)

            @block.scalar
            def _(act):
                def side(op, c, s, n):
                    k = int(op[1:])
                    if op[0] == "T":
                        h, t0, nt = TG[k]
                        act.wait_ge(S("xp1"), 4 * c + k + 1)
                        if some(4 * (c - 1)):
                            act.wait_ge(S("vmm1"), 4 * (c - 1))
                        act.copy(ctxT1[:, s, h, t0 * P:(t0 + nt) * P], bank[XP1[k % 2]][:, 0:nt * P]).then_inc(S("ctxT1"), 1)
                    elif op[0] == "K":
                        half, b = k // 2, k % 2
                        cols = slice(half * HCH, (half + 1) * HCH)
                        act.wait_ge(S("kmm1"), 4 * c + k + 1)
                        if some(4 * c + k - 1):
                            act.wait_ge(S("k31"), 4 * c + k - 1)
                        if some(16 * (n + s)):
                            act.wait_ge(S(f"kscr_{1 - s}"), 16 * (n + s))
                            if isinstance(c, int) and c == 1:
                                act.wait_ge(S("kscr_first"), 16)
                        act.activation(kf[:, k % 2, :], bank[KV1][:, 0:HCH], ACT.Identity, bias=b1[:, 1, b:b + 1])
                        act.activation(kt3[:, 0, b, cols], bank[KV1][:, 0:HCH], ACT.Identity,
                                       bias=b1[:, 1, b:b + 1]).then_inc(S("kread1"), 1)
                    elif op[0] == "V" and k != 3:
                        take_values(act, act.copy, c, s, k)
                    elif op[0] == "L":
                        ln_act(act, "ln2", 4)
                    elif op[0] == "M":
                        act.wait_ge(S("mt1"), c + 1)
                        act.copy(n3T1[:, s, :], bankb[XP1[0]][0:3 * HP, 0:P]).then_inc(S("n3T1"), 1)
                        act.wait_ge(S("dm1"), c + 1)
                        act.activation(f1[:, s, :], dm1[:, s, :], ACT.Exp).then_inc(S("f1"), 1)

                def softmax(c, s, u):
                    act.wait_ge(S("st1"), UNITS * c + u + 1)
                    if some(UNITS * c + u - 3):
                        act.wait_ge(S("pv1"), UNITS * c + u - 3)
                    act.activation(p1[:, u % 4, :], bank[ST1[u % 2]][:], ACT.Exp).then_inc(S("exp1"), 1)

                act.wait_ge(S("b1_in"), 32)
                for op, c, _ in PRO1:
                    side(op, c, c, 0)

                def step(c, s, n, two, one):
                    softmax(c, s, 0)
                    for u in range(UNITS):
                        if u + 1 < UNITS:
                            softmax(c, s, u + 1)
                        sides(side, PLAN1[u][0] + PLAN1[u][1], c, s, n, two, one)
                steps1(act, step)
        l1.close()

        la = ExitStack()
        lT = sb(la, "lT", [P, DC, 10, P])
        dec = sb(la, "dec", [P, DC])
        bg = sb(la, "bg", [P, DC])
        blk16 = sb(la, "blk16", [P, P])
        qkv = sb(la, "qkv", [P, 6, P])
        ng = sb(la, "ng", [P, 4, P])
        kvp = sb(la, "kvp", [P, DC, P])
        scan = sb(la, "scan", [P, 4, P])
        qs = sb(la, "qs", [P, DC, P])
        rden = sb(la, "rden", [P, DC, P])
        ol = sb(la, "ol", [P, DC, P])
        gl = sb(la, "gl", [P, DC, P])

        with nc.Block() as block:
            @block.sync
            def _(sp):
                dp = a["L1_attn_decay_param"].rearrange("(c h) -> c h", c=DC)
                for c in range(DC):
                    sp.dma_start(dec[:, c:c + 1], dp[c].unsqueeze(1).to_broadcast([HL // DC, DL]).unsqueeze(2)
                                 ).then_inc(S("dec_in"), 16)
                sp.dma_start(bg[:], a["L1_attn_bgate"].rearrange("(c p) -> p c", c=DC),
                             allow_slow_non_contiguous=True).then_inc(S("bg_in"), 16)

            @block.gpsimd
            def _(pool):
                pool.memset(blk16[:], 1.0).then_inc(S("blk16"), 1)
                pool.wait_ge(S("blk16"), nth("blk16"))
                v = blk16[:].rearrange("p (b u) -> p b u", u=DL)
                pool.affine_select(out=v, in_=v, compare_op=ALU.is_ge, fill=0.0, base=0,
                                              pattern=[[-DL, P // DL], [0, DL]], channel_multiplier=1).then_inc(S("blk16"), 1)
                pool.wait_ge(S("blk16"), nth("blk16"))
                pool.affine_select(out=v, in_=v, compare_op=ALU.is_ge, fill=0.0, base=DL - 1,
                                              pattern=[[DL, P // DL], [0, DL]], channel_multiplier=-1).then_inc(S("blk16"), 1)
                pool.wait_ge(S("blk16"), nth("blk16"))
                ln_pool(pool, "ln3")

            @block.vector
            def _(dve):
                dve.reciprocal(rd1[:], acc1[:, :, D1]).then_inc(S("lstep"), 1)
                dve.wait_ge(S("lstep"), nth("lstep"))
                o3 = o1[:].rearrange("p (h d) -> p h d", h=H1)
                dve.tensor_tensor(o3, acc1[:, :, 0:D1], bc(rd1[:], 2, [P, H1, D1]), ALU.mult).then_inc(S("lstep"), 1)
                dve.wait_ge(S("lstep"), nth("lstep"))
                dve.wait_ge(S("bv1_in"), 16)
                dve.tensor_tensor(o1[:], o1[:], bv1[:], ALU.add).then_inc(S("lstep"), 1)
                dve.wait_ge(S("lstep"), nth("lstep"))
                dve.tensor_tensor(xres[:], xres[:], o1[:], ALU.add).then_inc(S("lstep"), 1)
                dve.wait_ge(S("lstep"), nth("lstep"))
                ln_dve(dve, "ln3")
                dve.wait_ge(S("edec"), 1)
                dve.tensor_scalar(dec[:], dec[:], 1.0, None, ALU.add).then_inc(S("lstep"), 1)
                dve.wait_ge(S("lstep"), nth("lstep"))
                dve.reciprocal(dec[:], dec[:]).then_inc(S("lstep"), 1)
                dve.wait_ge(S("lstep"), nth("lstep"))
                dve.tensor_scalar(dec[:], dec[:], 1e-8, None, ALU.max).then_inc(S("lstep"), 1)
                dve.wait_ge(S("lstep"), nth("lstep"))
                dve.wait_ge(S("bg_in"), 16)
                dve.tensor_scalar(bg[:], bg[:], -1.0, None, ALU.mult).then_inc(S("nbg"), 1)
                dve.wait_ge(S("nbg"), nth("nbg"))
                dve.wait_ge(S("qkv"), 2)
                q4 = qkv[:, 0:4]
                dve.tensor_scalar(ng[:], q4, 0.0, None, ALU.min).then_inc(S("ng"), 1)
                dve.wait_ge(S("ng"), nth("ng"))
                dve.tensor_scalar(q4, q4, 0.0, None, ALU.max).then_inc(S("lstep"), 1)
                dve.wait_ge(S("lstep"), nth("lstep"))
                dve.wait_ge(S("eng"), 1)
                dve.tensor_tensor(q4, q4, ng[:], ALU.add).then_inc(S("lstep"), 1)
                dve.wait_ge(S("lstep"), nth("lstep"))
                dve.tensor_tensor(kvp[:], qkv[:, 2:4], qkv[:, 4:6], ALU.mult).then_inc(S("lstep"), 1)
                dve.wait_ge(S("lstep"), nth("lstep"))
                for c in range(DC):
                    d = dec[:, c:c + 1].to_broadcast([P, P])
                    dve.tensor_tensor_scan(scan[:, 2 + c], d, qkv[:, 2 + c], 0.0, ALU.mult, ALU.add).then_inc(S("lstep"), 1)
                    dve.wait_ge(S("lstep"), nth("lstep"))
                    dve.tensor_tensor(qs[:, c], qkv[:, c], scan[:, 2 + c], ALU.mult).then_inc(S("qs"), 1)
                    dve.wait_ge(S("qs"), nth("qs"))
                for c in range(DC):
                    d = dec[:, c:c + 1].to_broadcast([P, P])
                    dve.tensor_tensor_scan(scan[:, c], d, kvp[:, c], 0.0, ALU.mult, ALU.add).then_inc(S("lstep"), 1)
                    dve.wait_ge(S("lstep"), nth("lstep"))
                dve.tensor_tensor(ol[:], qkv[:, 0:2], scan[:, 0:2], ALU.mult).then_inc(S("lstep"), 1)
                dve.wait_ge(S("lstep"), nth("lstep"))
                dve.wait_ge(S("den_psum"), 1)
                dve.tensor_scalar(rden[:], bank[4][:, 0:D].rearrange("p (c t) -> p c t", c=DC), 1e-6, None, ALU.max).then_inc(S("lstep"), 1)
                dve.wait_ge(S("lstep"), nth("lstep"))
                dve.reciprocal(rden[:], rden[:]).then_inc(S("lstep"), 1)
                dve.wait_ge(S("lstep"), nth("lstep"))
                dve.tensor_tensor(ol[:], ol[:], rden[:], ALU.mult).then_inc(S("ol"), 1)
                dve.wait_ge(S("ol"), nth("ol"))
                dve.tensor_tensor(kvp[:], ol[:], qkv[:, 4:6], ALU.subtract).then_inc(S("lstep"), 1)
                dve.wait_ge(S("lstep"), nth("lstep"))
                dve.wait_ge(S("egate"), DC)
                dve.tensor_scalar(gl[:], gl[:], 1.0, None, ALU.add).then_inc(S("lstep"), 1)
                dve.wait_ge(S("lstep"), nth("lstep"))
                dve.reciprocal(gl[:], gl[:]).then_inc(S("lstep"), 1)
                dve.wait_ge(S("lstep"), nth("lstep"))
                dve.tensor_tensor(kvp[:], kvp[:], gl[:], ALU.mult).then_inc(S("lstep"), 1)
                dve.wait_ge(S("lstep"), nth("lstep"))
                dve.tensor_tensor(kvp[:], kvp[:], qkv[:, 4:6], ALU.add).then_inc(S("mixed"), 1)
                dve.wait_ge(S("mixed"), nth("mixed"))
                dve.wait_ge(S("x5_psum"), 1)
                dve.tensor_tensor(xres[:], xres[:], bank[6][:, 0:D], ALU.add).then_inc(S("x5"), 1)
                dve.wait_ge(S("x5"), nth("x5"))

            @block.scalar
            def _(act):
                act.wait_ge(S("dec_in"), 16 * DC)
                act.activation(dec[:], dec[:], ACT.Exp, scale=-1.0).then_inc(S("edec"), 1)
                for i in range(5):
                    act.wait_ge(S("lT_psum"), i + 1)
                    act.copy(lT[:, :, 2 * i:2 * i + 2, :], bank[1 + i % 2][:].rearrange("p (k c o) -> p k c o", k=DC, c=2)
                             ).then_inc(S("lT"), 1)
                ln_act(act, "ln3", 0)
                act.wait_ge(S("qkv_psum"), 1)
                act.copy(qkv[:, 0:4], b4(3)).then_inc(S("qkv"), 1)
                act.wait_ge(S("qkv_psum"), 2)
                act.copy(qkv[:, 4:6], bank[4][:, 0:D].rearrange("p (c t) -> p c t", c=2)).then_inc(S("qkv"), 1)
                act.wait_ge(S("ng"), 1)
                act.activation(ng[:], ng[:], ACT.Exp).then_inc(S("eng"), 1)
                act.wait_ge(S("gate_psum"), 1)
                act.wait_ge(S("nbg"), 1)
                for c in range(DC):
                    act.activation(gl[:, c], bank[5][:, c * P:(c + 1) * P], ACT.Exp, scale=-1.0,
                                   bias=bg[:, c:c + 1]).then_inc(S("egate"), 1)

            @block.tensor
            def _(pe):
                pe.wait_ge(S("lraw_in"), 48)
                for i in range(5):
                    if i >= 2:
                        if some(i - 1):
                            pe.wait_ge(S("lT"), i - 1)
                    for k in range(DC):
                        for c in range(2):
                            ins = pe.transpose(bank[1 + i % 2][:, (k * 2 + c) * P:(k * 2 + c + 1) * P],
                                               lraw[:, 2 * i + c, k * P:(k + 1) * P], ident[:])
                    ins.then_inc(S("lT_psum"), 1)
                ln_pe(pe, "ln3", 0)
                pe.wait_ge(S("ln3_hT"), 1)
                pe.wait_ge(S("lT"), 5)
                for b in range(6):
                    o = bank[3][:, b * P:(b + 1) * P] if b < 4 else bank[4][:, (b - 4) * P:(b - 3) * P]
                    for k in range(DC):
                        ins = pe.matmul(o, lT[:, k, b, :], hT[:, k, :], start=(k == 0), stop=(k == DC - 1))
                    if b in (3, 5):
                        ins.then_inc(S("qkv_psum"), 1)
                pe.wait_ge(S("blk16"), 3)
                pe.wait_ge(S("qkv"), 2)
                pe.wait_ge(S("qs"), DC)
                pe.matmul(bank[4][:, 0:D], blk16[:], qs[:].rearrange("p c t -> p (c t)"), start=True,
                          stop=True).then_inc(S("den_psum"), 1)
                pe.wait_ge(S("ol"), 1)
                for b in range(DC):
                    for k in range(DC):
                        ins = pe.matmul(bank[5][:, b * P:(b + 1) * P], lT[:, k, 8 + b, :], ol[:, k, :],
                                        start=(k == 0), stop=(k == DC - 1))
                ins.then_inc(S("gate_psum"), 1)
                pe.wait_ge(S("mixed"), 1)
                for k in range(DC):
                    ins = pe.matmul(bank[6][:, 0:D], kvp[:, k, :], lT[:, k, 6:8, :].rearrange("p c o -> p (c o)"),
                                    start=(k == 0), stop=(k == DC - 1))
                ins.then_inc(S("x5_psum"), 1)
        la.close()
        xb.close()
        lw.close()

        experts("moe1", a["L1_ffn_Wg"], False, a["L1_ffn_bg"], a["L1_ffn_be"], 2, True)


def kernel(**inputs):
    import numpy as _np
    import concourse.bacc as _bacc
    from concourse import mybir as _mybir
    from concourse.bass_utils import run_bass_kernel_spmd as _run

    nc = _bacc.Bacc("TRN2", target_bir_lowering=False, num_devices=1)
    arrays, args = {}, {}
    for name, value in inputs.items():
        v = _np.ascontiguousarray(value)
        if v.dtype == _np.bool_:
            v = v.view(_np.uint8)
        arrays[name] = v
        args[name] = nc.dram_tensor(name, v.shape, _mybir.dt.from_np(v.dtype), kind="ExternalInput").ap()
    result = nc.dram_tensor("out_0_dram", (1, P, D), F32, kind="ExternalOutput").ap()
    build(nc, args, result)
    r = _run(nc, [arrays], core_ids=[0])
    return r.results[0]["out_0_dram"]
```
